# Optimizing a Trainium2 kernel written in Bass

```python
import numpy as np
import jax
import jax.numpy as jnp

def _softmax(x, axis=-1):
    return jax.nn.softmax(x, axis=axis)

def _gelu(x):
    return jax.nn.gelu(x, approximate=True)

def _silu(x):
    return jax.nn.silu(x)

def _sigmoid(x):
    return jax.nn.sigmoid(x)

def _layernorm(x, axis=-1, eps=1e-05):
    m = jnp.mean(x, axis=axis, keepdims=True)
    v = jnp.var(x, axis=axis, keepdims=True)
    return (x - m) / jnp.sqrt(v + eps)

def _scatter_add(tgt, idx, src, axis=0):
    return tgt.at[idx].add(src)

def _segment_sum(src, seg, n):
    return jax.ops.segment_sum(src, seg, n)
kernel_name = 'mk_early_fusion_d1_tok_img512_r4_25bf9b'

def setup_inputs(seed: int=0):
    np.random.seed(seed)
    _w = jnp.asarray

    def _rec_inputs():
        import jax
        import jax.numpy as jnp
        _rk = jax.random.key(seed)
        x = 7.57192e-06 + 1.00007 * jax.random.normal(jax.random.fold_in(_rk, 1), (64, 3, 224, 224), jnp.float32)
        txt = -1.28643e-11 + 0.999988 * jax.random.normal(jax.random.fold_in(_rk, 2), (64, 32, 128), jnp.float32)
        return (x, txt)
    x, txt = _rec_inputs()

    def _L0_tok_setup():
        import jax, jax.numpy as jnp
        import numpy as np
        DEPTH = 4
        HEADS = 8
        DIM = 128
        HID = 256
        P = 16
        IMG = 224
        GRID = IMG // P
        NPATCH = GRID * GRID
        NTOK = NPATCH + 1
        BATCH = 64
        EPS = 1e-05

        def layernorm(x, w, b):
            mu = jnp.mean(x, axis=-1, keepdims=True)
            var = jnp.mean(jnp.square(x - mu), axis=-1, keepdims=True)
            return (x - mu) * jax.lax.rsqrt(var + EPS) * w + b
        key = jax.random.key(seed)
        ks = jax.random.split(key, 12)
        s = 0.02
        inp = {'x': jax.random.normal(ks[0], (BATCH, 3, IMG, IMG), jnp.float32), 'conv_w': jax.random.normal(ks[1], (3 * P * P, DIM), jnp.float32) * s, 'conv_b': jnp.zeros((DIM,), jnp.float32), 'cls_token': jax.random.normal(ks[2], (1, 1, DIM), jnp.float32) * s, 'pos_embed': jax.random.normal(ks[3], (1, NTOK, DIM), jnp.float32) * s, 'ln1_w': jnp.ones((DEPTH, DIM), jnp.float32), 'ln1_b': jnp.zeros((DEPTH, DIM), jnp.float32), 'qkv_w': jax.random.normal(ks[4], (DEPTH, DIM, 3 * DIM), jnp.float32) * s, 'qkv_b': jnp.zeros((DEPTH, 3 * DIM), jnp.float32), 'proj_w': jax.random.normal(ks[5], (DEPTH, DIM, DIM), jnp.float32) * s, 'proj_b': jnp.zeros((DEPTH, DIM), jnp.float32), 'ln2_w': jnp.ones((DEPTH, DIM), jnp.float32), 'ln2_b': jnp.zeros((DEPTH, DIM), jnp.float32), 'fc1_w': jax.random.normal(ks[6], (DEPTH, DIM, HID), jnp.float32) * s, 'fc1_b': jnp.zeros((DEPTH, HID), jnp.float32), 'fc2_w': jax.random.normal(ks[7], (DEPTH, HID, DIM), jnp.float32) * s, 'fc2_b': jnp.zeros((DEPTH, DIM), jnp.float32), 'norm_w': jnp.ones((DIM,), jnp.float32), 'norm_b': jnp.zeros((DIM,), jnp.float32)}
        return inp
    _L0_tok_all = _L0_tok_setup()
    _L0_tok_in = {k: v for k, v in _L0_tok_all.items() if k in ('conv_w', 'conv_b', 'cls_token', 'pos_embed', 'ln1_w', 'ln1_b', 'qkv_w', 'qkv_b', 'proj_w', 'proj_b', 'ln2_w', 'ln2_b', 'fc1_w', 'fc1_b', 'fc2_w', 'fc2_b', 'norm_w', 'norm_b')}
    del _L0_tok_all

    def _L0_attn_setup():
        import jax, jax.numpy as jnp
        import numpy as np
        DIM = 128
        D_INNER = 128
        D_STATE = 16
        DT_RANK = 32
        D_CONV = 4
        EPS = 1e-05

        def _causal_dwconv(u, w, b):
            x = u.transpose(0, 2, 1)
            y = jax.lax.conv_general_dilated(x, w, (1,), [(D_CONV - 1, 0)], feature_group_count=D_INNER)
            return (y + b[None, :, None]).transpose(0, 2, 1)

        def _ssm(u, W_x, W_dt, b_dt, A_log, D):
            b, s, d = u.shape
            A = -jnp.exp(A_log)
            dbc = u @ W_x
            dt, B, C = jnp.split(dbc, [DT_RANK, DT_RANK + D_STATE], axis=-1)
            delta = jax.nn.softplus(dt @ W_dt + b_dt)
            dA = jnp.exp(delta[..., None] * A)
            dBx = delta[..., None] * B[:, :, None, :] * u[..., None]

            def step(h, inp):
                a, bx = inp
                h = a * h + bx
                return (h, h)
            _, hs = jax.lax.scan(step, jnp.zeros((b, d, D_STATE), u.dtype), (dA.transpose(1, 0, 2, 3), dBx.transpose(1, 0, 2, 3)))
            y = jnp.einsum('sbdn,bsn->bsd', hs, C)
            return y + u * D
        key = jax.random.key(seed)
        ks = jax.random.split(key, 8)
        s = lambda k, shape, sc=0.02: jax.random.normal(k, shape, jnp.float32) * sc
        return {'x': jax.random.normal(ks[0], (2, 1024, DIM), jnp.float32), 'ln_g': jnp.ones((DIM,), jnp.float32), 'ln_b': jnp.zeros((DIM,), jnp.float32), 'W_proj': s(ks[1], (DIM, 2 * D_INNER)), 'conv_w': s(ks[2], (D_INNER, 1, D_CONV), 0.1), 'conv_b': jnp.zeros((D_INNER,), jnp.float32), 'W_x': s(ks[3], (D_INNER, DT_RANK + 2 * D_STATE)), 'W_dt': s(ks[4], (DT_RANK, D_INNER), 0.05), 'b_dt': jnp.full((D_INNER,), -4.6, jnp.float32), 'A_log': jnp.tile(jnp.log(jnp.arange(1, D_STATE + 1, dtype=jnp.float32)), (D_INNER, 1)), 'D': jnp.ones((D_INNER,), jnp.float32)}
    _L0_attn_all = _L0_attn_setup()
    _L0_attn_in = {k: v for k, v in _L0_attn_all.items() if k in ('ln_g', 'ln_b', 'W_proj', 'conv_w', 'conv_b', 'W_x', 'W_dt', 'b_dt', 'A_log', 'D')}
    del _L0_attn_all

    def _L0_ffn_setup():
        import jax, jax.numpy as jnp
        import numpy as np
        T = 128
        B = 64
        C = 256

        def _triu_apply(x, W, b):
            Wm = jnp.tril(W)
            return jnp.einsum('bct,st->bcs', x, Wm) + b
        key = jax.random.key(seed)
        ks = jax.random.split(key, 5)
        x = jax.random.normal(ks[0], (B, C, T), dtype=jnp.float32)
        scale = 1.0 / jnp.sqrt(jnp.arange(1, T + 1, dtype=jnp.float32))[:, None]
        W1 = jax.random.uniform(ks[1], (T, T), jnp.float32, -1.0, 1.0) * scale
        b1 = jax.random.uniform(ks[2], (T,), jnp.float32, -1.0, 1.0) * scale[:, 0]
        W2 = jax.random.uniform(ks[3], (T, T), jnp.float32, -1.0, 1.0) * scale
        b2 = jax.random.uniform(ks[4], (T,), jnp.float32, -1.0, 1.0) * scale[:, 0]
        return {'x': x, 'W1': W1, 'b1': b1, 'W2': W2, 'b2': b2}
    _L0_ffn_all = _L0_ffn_setup()
    _L0_ffn_in = {k: v for k, v in _L0_ffn_all.items() if k in ('W1', 'b1', 'W2', 'b2')}
    del _L0_ffn_all
    return {'x': x, 'txt': txt, 'L0_tok_conv_w': _L0_tok_in['conv_w'], 'L0_tok_conv_b': _L0_tok_in['conv_b'], 'L0_tok_cls_token': _L0_tok_in['cls_token'], 'L0_tok_pos_embed': _L0_tok_in['pos_embed'], 'L0_tok_ln1_w': _L0_tok_in['ln1_w'], 'L0_tok_ln1_b': _L0_tok_in['ln1_b'], 'L0_tok_qkv_w': _L0_tok_in['qkv_w'], 'L0_tok_qkv_b': _L0_tok_in['qkv_b'], 'L0_tok_proj_w': _L0_tok_in['proj_w'], 'L0_tok_proj_b': _L0_tok_in['proj_b'], 'L0_tok_ln2_w': _L0_tok_in['ln2_w'], 'L0_tok_ln2_b': _L0_tok_in['ln2_b'], 'L0_tok_fc1_w': _L0_tok_in['fc1_w'], 'L0_tok_fc1_b': _L0_tok_in['fc1_b'], 'L0_tok_fc2_w': _L0_tok_in['fc2_w'], 'L0_tok_fc2_b': _L0_tok_in['fc2_b'], 'L0_tok_norm_w': _L0_tok_in['norm_w'], 'L0_tok_norm_b': _L0_tok_in['norm_b'], 'L0_attn_ln_g': _L0_attn_in['ln_g'], 'L0_attn_ln_b': _L0_attn_in['ln_b'], 'L0_attn_W_proj': _L0_attn_in['W_proj'], 'L0_attn_conv_w': _L0_attn_in['conv_w'], 'L0_attn_conv_b': _L0_attn_in['conv_b'], 'L0_attn_W_x': _L0_attn_in['W_x'], 'L0_attn_W_dt': _L0_attn_in['W_dt'], 'L0_attn_b_dt': _L0_attn_in['b_dt'], 'L0_attn_A_log': _L0_attn_in['A_log'], 'L0_attn_D': _L0_attn_in['D'], 'L0_ffn_W1': _L0_ffn_in['W1'], 'L0_ffn_b1': _L0_ffn_in['b1'], 'L0_ffn_W2': _L0_ffn_in['W2'], 'L0_ffn_b2': _L0_ffn_in['b2']}

def reference(x, txt, L0_tok_conv_w, L0_tok_conv_b, L0_tok_cls_token, L0_tok_pos_embed, L0_tok_ln1_w, L0_tok_ln1_b, L0_tok_qkv_w, L0_tok_qkv_b, L0_tok_proj_w, L0_tok_proj_b, L0_tok_ln2_w, L0_tok_ln2_b, L0_tok_fc1_w, L0_tok_fc1_b, L0_tok_fc2_w, L0_tok_fc2_b, L0_tok_norm_w, L0_tok_norm_b, L0_attn_ln_g, L0_attn_ln_b, L0_attn_W_proj, L0_attn_conv_w, L0_attn_conv_b, L0_attn_W_x, L0_attn_W_dt, L0_attn_b_dt, L0_attn_A_log, L0_attn_D, L0_ffn_W1, L0_ffn_b1, L0_ffn_W2, L0_ffn_b2):
    import jax
    import jax.numpy as jnp

    def _L0_tok_ref(x, conv_w, conv_b, cls_token, pos_embed, ln1_w, ln1_b, qkv_w, qkv_b, proj_w, proj_b, ln2_w, ln2_b, fc1_w, fc1_b, fc2_w, fc2_b, norm_w, norm_b):
        import jax, jax.numpy as jnp
        import numpy as np
        DEPTH = 4
        HEADS = 8
        DIM = 128
        HID = 256
        P = 16
        IMG = 224
        GRID = IMG // P
        NPATCH = GRID * GRID
        NTOK = NPATCH + 1
        BATCH = 64
        EPS = 1e-05

        def layernorm(x, w, b):
            mu = jnp.mean(x, axis=-1, keepdims=True)
            var = jnp.mean(jnp.square(x - mu), axis=-1, keepdims=True)
            return (x - mu) * jax.lax.rsqrt(var + EPS) * w + b
        B = x.shape[0]
        hd = DIM // HEADS
        scale = hd ** (-0.5)
        patches = x.reshape(B, 3, GRID, P, GRID, P)
        patches = patches.transpose(0, 2, 4, 1, 3, 5).reshape(B, NPATCH, 3 * P * P)
        tok = patches @ conv_w + conv_b
        cls = jnp.broadcast_to(cls_token, (B, 1, DIM))
        h = jnp.concatenate([cls, tok], axis=1) + pos_embed
        for i in range(DEPTH):
            y = layernorm(h, ln1_w[i], ln1_b[i])
            qkv = (y @ qkv_w[i] + qkv_b[i]).reshape(B, NTOK, 3, HEADS, hd)
            qkv = qkv.transpose(2, 0, 3, 1, 4)
            q, k, v = (qkv[0], qkv[1], qkv[2])
            attn = jax.nn.softmax(jnp.einsum('bhnd,bhmd->bhnm', q, k) * scale, axis=-1)
            o = jnp.einsum('bhnm,bhmd->bhnd', attn, v)
            o = o.transpose(0, 2, 1, 3).reshape(B, NTOK, DIM)
            h = h + (o @ proj_w[i] + proj_b[i])
            y = layernorm(h, ln2_w[i], ln2_b[i])
            y = jax.nn.gelu(y @ fc1_w[i] + fc1_b[i], approximate=False)
            h = h + (y @ fc2_w[i] + fc2_b[i])
        return layernorm(h, norm_w, norm_b)

    def _L0_attn_ref(x, ln_g, ln_b, W_proj, conv_w, conv_b, W_x, W_dt, b_dt, A_log, D):
        import jax, jax.numpy as jnp
        import numpy as np
        DIM = 128
        D_INNER = 128
        D_STATE = 16
        DT_RANK = 32
        D_CONV = 4
        EPS = 1e-05

        def _causal_dwconv(u, w, b):
            x = u.transpose(0, 2, 1)
            y = jax.lax.conv_general_dilated(x, w, (1,), [(D_CONV - 1, 0)], feature_group_count=D_INNER)
            return (y + b[None, :, None]).transpose(0, 2, 1)

        def _ssm(u, W_x, W_dt, b_dt, A_log, D):
            b, s, d = u.shape
            A = -jnp.exp(A_log)
            dbc = u @ W_x
            dt, B, C = jnp.split(dbc, [DT_RANK, DT_RANK + D_STATE], axis=-1)
            delta = jax.nn.softplus(dt @ W_dt + b_dt)
            dA = jnp.exp(delta[..., None] * A)
            dBx = delta[..., None] * B[:, :, None, :] * u[..., None]

            def step(h, inp):
                a, bx = inp
                h = a * h + bx
                return (h, h)
            _, hs = jax.lax.scan(step, jnp.zeros((b, d, D_STATE), u.dtype), (dA.transpose(1, 0, 2, 3), dBx.transpose(1, 0, 2, 3)))
            y = jnp.einsum('sbdn,bsn->bsd', hs, C)
            return y + u * D
        skip = x
        mu = x.mean(-1, keepdims=True)
        var = x.var(-1, keepdims=True)
        xn = (x - mu) * jax.lax.rsqrt(var + EPS) * ln_g + ln_b
        zx = xn @ W_proj
        xin, z = jnp.split(zx, 2, axis=-1)

        def direction(u):
            return _ssm(jax.nn.softplus(_causal_dwconv(u, conv_w, conv_b)), W_x, W_dt, b_dt, A_log, D)
        x1 = direction(xin)
        x2 = jnp.flip(direction(jnp.flip(xin, 1)), 1)
        zg = jax.nn.silu(z)
        return x1 * zg + x2 * zg + skip

    def _L0_ffn_ref(x, W1, b1, W2, b2):
        import jax, jax.numpy as jnp
        import numpy as np
        T = 128
        B = 64
        C = 256

        def _triu_apply(x, W, b):
            Wm = jnp.tril(W)
            return jnp.einsum('bct,st->bcs', x, Wm) + b
        h = _triu_apply(x, W1, b1)
        h = jax.nn.gelu(h, approximate=False)
        return _triu_apply(h, W2, b2)
    h = _L0_tok_ref(x, L0_tok_conv_w, L0_tok_conv_b, L0_tok_cls_token, L0_tok_pos_embed, L0_tok_ln1_w, L0_tok_ln1_b, L0_tok_qkv_w, L0_tok_qkv_b, L0_tok_proj_w, L0_tok_proj_b, L0_tok_ln2_w, L0_tok_ln2_b, L0_tok_fc1_w, L0_tok_fc1_b, L0_tok_fc2_w, L0_tok_fc2_b, L0_tok_norm_w, L0_tok_norm_b)
    h = jnp.concatenate([h, txt], axis=1)
    h = h + _L0_attn_ref(_layernorm(h, axis=-1), L0_attn_ln_g, L0_attn_ln_b, L0_attn_W_proj, L0_attn_conv_w, L0_attn_conv_b, L0_attn_W_x, L0_attn_W_dt, L0_attn_b_dt, L0_attn_A_log, L0_attn_D)
    h = h + _L0_ffn_ref(_layernorm(h, axis=-1), L0_ffn_W1, L0_ffn_b1, L0_ffn_W2, L0_ffn_b2)
    return h

_drawn_inputs = setup_inputs


def setup_inputs(seed=0):
    import zlib

    import numpy as np

    out = dict(_drawn_inputs(seed))
    spreads = {'L0_tok_conv_b': (0.0, 0.1),
     'L0_tok_ln1_w': (1.0, 0.6),
     'L0_tok_ln1_b': (0.0, 0.529),
     'L0_tok_qkv_b': (0.0, 0.1),
     'L0_tok_proj_b': (0.0, 0.1),
     'L0_tok_ln2_w': (1.0, 0.6),
     'L0_tok_ln2_b': (0.0, 0.734),
     'L0_tok_fc1_b': (0.0, 0.1),
     'L0_tok_fc2_b': (0.0, 0.1),
     'L0_tok_norm_w': (1.0, 0.2),
     'L0_tok_norm_b': (0.0, 0.1),
     'L0_attn_ln_g': (1.0, 0.6),
     'L0_attn_ln_b': (0.0, 0.8),
     'L0_attn_conv_b': (0.0, 0.8),
     'L0_attn_b_dt': (-4.599999904632568, 0.6),
     'L0_attn_D': (1.0, 0.6)}
    factors = {'L0_tok_cls_token': 8.0,
     'L0_attn_conv_w': 8.0,
     'L0_attn_W_x': 8.0,
     'L0_attn_W_dt': 8.0,
     'L0_attn_A_log': 8.0}
    for name, (base, spread) in spreads.items():
        noise = np.random.default_rng([zlib.crc32(name.encode()), seed]).standard_normal(out[name].shape)
        drawn = base * np.exp(spread * noise) if base else spread * noise
        out[name] = jnp.asarray(drawn.astype(out[name].dtype))
    for name, factor in factors.items():
        out[name] = (out[name] * factor).astype(out[name].dtype)
    return out
```

```python
from contextlib import ExitStack

import concourse.bass as bass
from concourse import mybir

F32 = mybir.dt.float32
BF16 = mybir.dt.bfloat16
ACT = mybir.ActivationFunctionType
ALU = mybir.AluOpType
AX = mybir.AxisListType

P = 128
ARENA = 33500
CREDIT = 3


def shift(u, d):
    q, par, lq = u
    n = par + d
    return (q + n // 2, n % 2, lq + n // 2)


def V(u, k=1, j=0):
    q, par = u[:2]
    return q * (2 * k) + ((par + CREDIT) * k + j + 1)


def VD(u, n):
    return u[0] * (16 * n) + 16 * n


def early_fusion(nc, x, txt, conv_w, conv_b, cls_token, pos_embed, ln1_w, ln1_b, qkv_w, qkv_b,
                 proj_w, proj_b, ln2_w, ln2_b, fc1_w, fc1_b, fc2_w, fc2_b, norm_w, norm_b,
                 m_ln_g, m_ln_b, m_W_proj, m_conv_w, m_conv_b, m_W_x, m_W_dt, m_b_dt, m_A_log, m_D,
                 f_W1, f_b1, f_W2, f_b2, out, scratch, debug=None):
    B, CH, IMG, _ = x.shape
    D = conv_w.shape[1]
    DEPTH = ln1_w.shape[0]
    NT = pos_embed.shape[1]
    PS = 16
    G = IMG // PS
    NP = G * G
    HEADS, HD = 8, D // 8
    HG = 4
    T2 = 2 * NT
    UNITS = B // 2
    PAIRS = UNITS // 2
    TXT = txt.shape[1]
    S = NT + TXT
    S2 = 2 * S
    NS = m_A_log.shape[1]
    RANK = m_W_dt.shape[0]
    TAPS = m_conv_w.shape[2]
    EPS = 1e-5
    KT = (P, NT - P)
    SCALE = HD ** -0.5

    with ExitStack() as ctx:
        def sb(name, shape, dt=F32):
            return ctx.enter_context(nc.sbuf_tensor(name, shape, dt))

        sems = {}

        def sem(name):
            if name not in sems:
                sems[name] = ctx.enter_context(nc.semaphore(name))
            return sems[name]

        def passed(eng):
            eng.sem_inc(sem("s_passed"), 1)

        ps = ctx.enter_context(nc.psum_tensor("ps", [P, 8, 512], F32))

        ident = sb("ident", [P, P])
        identb = sb("identb", [P, P], BF16)
        center = sb("center", [P, P])
        mean = sb("mean", [P, P])
        e0 = sb("e0", [P, 1])
        eps_col = sb("eps_col", [P, 1])
        one_col = sb("one_col", [P, 1])
        h = sb("h", [P, B * NT])
        arena = sb("arena", [P, ARENA])
        h3 = h[:, :].rearrange("p (b n) -> p b n", n=NT)

        at = [0]

        def carve(*dims, dt=F32):
            n = 1
            for d_ in dims:
                n *= d_
            words = n if dt == F32 else (n + 1) // 2
            a = arena[:, at[0]:at[0] + words]
            at[0] += words
            assert at[0] <= ARENA, at[0]
            if dt != F32:
                a = a.bitcast(dt)
            if len(dims) == 2:
                a = a.rearrange("p (a b) -> p a b", b=dims[1])
            elif len(dims) == 3:
                a = a.rearrange("p (a b c) -> p a b c", b=dims[1], c=dims[2])
            elif len(dims) == 4:
                a = a.rearrange("p (a b c d) -> p a b c d", b=dims[1], c=dims[2], d=dims[3])
            return a

        def hu(u):
            _, par, lq = u
            return h[:, bass.ds(lq * (2 * T2) + par * T2, T2)]

        XW = G * IMG
        patches = carve(2, 2, XW)
        wconv = carve(8, D)
        pos_rows = carve(2, D)
        posb = carve(NT)
        cls_col = carve(1)
        convb_col = carve(1)
        s_const = sem("s_const")
        s_init = sem("s_init")
        s_wl = sem("s_wl")
        s_xl = [sem("s_xl0"), sem("s_xl1")]
        s_posT = sem("s_posT")
        s_pose = sem("s_pose")
        s_emb = sem("s_emb")
        s_hemb = sem("s_hemb")
        NXL = 2 * 2 * CH

        with nc.Block() as block:
            @block.gpsimd
            def _(pool):
                pool.memset(ident[:, :], 0.0).then_inc(s_const, 1)
                pool.memset(identb[:, :], 0.0).then_inc(s_const, 1)
                pool.memset(center[:, :], -1.0 / D).then_inc(s_const, 1)
                pool.memset(mean[:, :], 1.0 / D).then_inc(s_const, 1)
                pool.memset(e0[:, :], 0.0).then_inc(s_const, 1)
                pool.memset(eps_col[:, :], EPS).then_inc(s_const, 1)
                pool.memset(one_col[:, :], 1.0).then_inc(s_const, 1)
                pool.wait_ge(s_const, 7)
                for m, v in ((ident, 1.0), (identb, 1.0), (center, 1.0 - 1.0 / D)):
                    pool.affine_select(out=m[:, :], in_=m[:, :], compare_op=ALU.not_equal, fill=v, base=0,
                                       pattern=[[-1, P]], channel_multiplier=1).then_inc(s_init, 1)
                pool.affine_select(out=e0[:, :], in_=e0[:, :], compare_op=ALU.not_equal, fill=1.0, base=0,
                                   pattern=[[0, 1]], channel_multiplier=1).then_inc(s_init, 1)

            @block.sync
            def _(sp):
                for half in range(2):
                    for c in range(CH):
                        r = (half * CH + c) * PS
                        src = conv_w.rearrange("(c i f j) n -> f c i j n", c=CH, i=PS, f=2)[half, c]
                        sp.dma_start(wconv[r:r + PS], src).then_inc(s_wl, 16)
                sp.dma_start(pos_rows[:, 0, :], pos_embed[0, 0:P, :]).then_inc(s_wl, 16)
                sp.dma_start(pos_rows[0:NT - P, 1, :], pos_embed[0, P:NT, :]).then_inc(s_wl, 16)
                sp.dma_start(cls_col, cls_token[0].rearrange("a d -> d a")).then_inc(s_wl, 16)
                sp.dma_start(convb_col, conv_b.rearrange("(d a) -> d a", a=1)).then_inc(s_wl, 16)

                def load(u):
                    q, par = u
                    for half in range(2):
                        for c in range(CH):
                            for b in range(2):
                                r = (half * CH + c) * PS
                                src = x[bass.ds(q * 4 + (par * 2 + b), 1), c].rearrange(
                                    "b (g i) w -> i (b g) w", i=PS)[:, :, 8 * half:]
                                dst = patches[r:r + PS, par, b].rearrange(
                                    "p (g w) -> p g w", w=IMG)[:, :, 0:IMG - 8 * half]
                                sp.dma_start(dst, src).then_inc(s_xl[par], 16)
                load((0, 0))
                load((0, 1))
                with sp.Fori(1, PAIRS) as q:
                    for par in range(2):
                        sp.wait_ge(s_emb, q * 2 + (par - 1))
                        passed(sp)
                        load((q, par))

            @block.tensor
            def _(pe):
                pe.wait_ge(s_init, 4)
                pe.wait_ge(s_wl, 16 * 10)
                pe.transpose(ps[:, 0, 0:P], pos_rows[:, 0, :], ident[:, :])
                pe.transpose(ps[:, 0, P:NT], pos_rows[0:NT - P, 1, :], ident[0:NT - P, 0:NT - P]).then_inc(s_posT, 1)
                with pe.Fori(0, PAIRS) as q:
                    for par in range(2):
                        pe.wait_ge(s_xl[par], VD((q, par), NXL))
                        pe.wait_ge(s_hemb, q * 2 + par)
                        for j in range(8):
                            last = pe.matmul(ps[:, 2 + par, 0:2 * NP], wconv[0:96, j, :],
                                             patches[0:96, par, :, bass.ds(j, NP, step=PS)],
                                             start=(j == 0), stop=(j == 7))
                        last.then_inc(s_emb, 1)

            @block.vector
            def _(dve):
                dve.wait_ge(s_posT, 1)
                dve.tensor_scalar(posb[:, 1:NT], ps[:, 0, 1:NT], convb_col, None, ALU.add).then_inc(s_pose, 1)
                dve.tensor_scalar(h3[:, :, 0:1], cls_col.rearrange("p (a b) -> p a b", b=1).broadcast_to((P, B, 1)),
                                  ps[:, 0, 0:1], None, ALU.add).then_inc(s_hemb, 1)
                dve.wait_ge(s_pose, 1)
                with dve.Fori(0, PAIRS) as q:
                    for par in range(2):
                        dve.wait_ge(s_emb, q * 2 + (par + 1))
                        dst = h[:, bass.ds(q * (2 * T2) + par * T2, T2)].rearrange("p (b n) -> p b n", n=NT)
                        dve.tensor_tensor(dst[:, :, 1:NT],
                                          ps[:, 2 + par, 0:2 * NP].rearrange("p (b n) -> p b n", n=NP),
                                          posb[:, 1:NT].rearrange("p (a n) -> p a n", a=1).broadcast_to((P, 2, NP)),
                                          ALU.add).then_inc(s_hemb, 1)
        if debug == "embed":
            s_dbg = sem("s_dbg")
            with nc.Block() as block:
                @block.sync
                def _(sp):
                    sp.dma_start(out, h[:, :]).then_inc(s_dbg, 16)
                    sp.wait_ge(s_dbg, 16)
            return

        at[0] = 0
        stack = carve(2, 2, HEADS * T2, dt=BF16)
        vaug = carve(2, 2 * 2 * HEADS * 2 * HD)
        probs = carve(2, 2, HG, NT)
        onorm = carve(2, 2, T2)
        sums = carve(2, NT)
        rsum = carve(2, NT)
        negmax = carve(2, 2, HG)
        negres = carve(2, 2, HG)
        mparts = carve(2, 2, 32, dt=BF16)
        mrows = carve(2, NT + 1, dt=BF16)
        sq, rs, y = carve(T2), carve(T2), carve(T2)
        qk32 = carve(2, T2)
        res32 = carve(2, T2)
        parts = carve(3, 2, T2, dt=BF16)
        act = carve(2, T2)
        wqkv_raw = carve(3 * D)
        wqk_perm = carve(2, D)
        bqkv_row = carve(3 * D)
        bqk_perm = carve(2, D)
        wq_f, wk_f, wv_f = carve(D), carve(D), carve(D)
        wproj_pad = carve(2, D)
        wproj_raw = carve(D)
        wfc1_raw = carve(2 * D)
        wfc1_f = carve(2 * D)
        wfc2 = carve(2, D)
        vecs = carve(8)
        bias = carve(8)
        msel = carve(HG, P, dt=BF16)
        L1W, L1B, L2W, L2B, PB, F2B, F1B = 0, 1, 2, 3, 4, 5, 6
        QB, KB, VB, HB, OB = 0, 1, 2, 3, 5
        Q_TERMS = (0, 0, 0, 1, 1, 2)
        K_TERMS = (0, 1, 2, 0, 1, 0)
        NLD = 2 * len(Q_TERMS)
        KROWS = HD * len(Q_TERMS)
        NWL = 4 + 1 + 1 + 1 + 1 + 1 + 1 + 6 + 2

        vau = [vaug[:, p_, :].rearrange("p (b t h c) -> p b t h c", b=2, t=2, h=HEADS) for p_ in range(2)]

        for n_ in ("p_centered p_squared p_vared p_logged p_rstd p_normed p_qk_mm p_v_mm p_qk_out p_v_out "
                   "p_hi p_res p_mid p_lo t_projected t_added t_centered t_squared t_vared t_logged t_rstd "
                   "t_normed t_fc1 t_gelu t_fc2 t_done").split():
            sem(n_)
        for n_ in "a_scores a_max a_hi a_res a_mid a_lo a_mT a_mrows a_keys a_exp a_pv a_sums a_logsum a_rsum a_out".split():
            sem(n_)
        STEPS = 4
        PER = {"a_scores": 8, "a_max": 8, "a_keys": 8, "a_exp": 8}
        W = {n_: PER.get(n_, STEPS) if n_[:2] == "a_" else 1 for n_ in sems if n_[:2] in ("p_", "t_", "a_")}

        def credit(eng, names):
            for n_ in names.split():
                eng.sem_inc(sems[n_], CREDIT * W[n_])

        def done(eng, name, u, j=0):
            eng.wait_ge(sems[name], V(u, W[name], j))

        s_parted = [sem("s_parted0"), sem("s_parted1")]
        s_stacked = [sem("s_stacked0"), sem("s_stacked1")]
        s_wld = sem("s_wld")
        s_fold = sem("s_fold")
        s_bmm = sem("s_bmm")
        s_bias = sem("s_bias")
        s_zero = sem("s_zero")
        s_ones = sem("s_ones")
        s_sel = sem("s_sel")
        FOLDS, BMMS, BIASES = 8, 2, 4

        def ticks(prep, tail):
            chain = (["p_center", "p_var", "p_qk", "p_v"] if prep else []) + (
                ["t_proj", "t_center", "t_var", "t_fc1", "t_fc2"] if tail else [])
            yield "scores", 0, 0
            yield "scores", 0, 1
            yield "max", 0, 0
            yield "mrow", 0, 0
            for i in range(STEPS):
                if i + 1 < STEPS:
                    yield "scores", i + 1, 0
                yield "keys", i, 0
                if chain:
                    yield chain.pop(0), 0, 0
                if i + 1 < STEPS:
                    yield "scores", i + 1, 1
                    yield "max", i + 1, 0
                yield "keys", i, 1
                if chain:
                    yield chain.pop(0), 0, 0
                if i + 1 < STEPS:
                    yield "mrow", i + 1, 0
                if i > 0:
                    yield "values", i - 1, 0
                if chain:
                    yield chain.pop(0), 0, 0
            yield "values", STEPS - 1, 0
            for c in chain:
                yield c, 0, 0

        def layers(eng, fold, rnd, chain_only, at_block=lambda: None):
            with eng.Fori(0, DEPTH) as L:
                base = L * PAIRS
                fold(L)
                first, last = (base, 0, 0), (base + (PAIRS - 1), 1, PAIRS - 1)
                chain_only(first, "prep")
                rnd(first, prep=True, tail=False)
                with eng.Fori(0, PAIRS - 1) as it:
                    at_block()
                    rnd((base + it, 1, it), prep=True, tail=True)
                    rnd((base + it + 1, 0, it + 1), prep=True, tail=True)
                at_block()
                rnd(last, prep=False, tail=True)
                chain_only(last, "tail")

        PREP = ("p_center", "p_var", "p_qk", "p_v")
        TAIL = ("t_proj", "t_center", "t_var", "t_fc1", "t_fc2")

        with nc.Block() as block:
            @block.sync
            def _(sp):
                def fold(L):
                    sp.wait_ge(s_zero, 5)
                    done(sp, "t_done", (L * PAIRS - 1, 1, 0))
                    pw = proj_w[bass.ds(L, 1)].rearrange("a (g i d) n -> (a i) d g n", g=2, i=HG)
                    for i in range(HG):
                        sp.dma_start(wproj_pad[32 * i:32 * i + HD], pw[i]).then_inc(s_wld, 16)
                    sp.dma_start(wqkv_raw, qkv_w[bass.ds(L, 1)].rearrange("a k n -> (a k) n")).then_inc(s_wld, 16)
                    sp.dma_start(bqkv_row[0:1], qkv_b[bass.ds(L, 1)]).then_inc(s_wld, 16)
                    sp.dma_start(wproj_raw, proj_w[bass.ds(L, 1)].rearrange("a k n -> (a k) n")).then_inc(s_wld, 16)
                    sp.dma_start(wfc1_raw, fc1_w[bass.ds(L, 1)].rearrange("a k n -> (a k) n")).then_inc(s_wld, 16)
                    f2 = fc2_w[bass.ds(L, 1)].rearrange("a (c k) n -> (a c) k n", c=2)
                    for c in range(2):
                        sp.dma_start(wfc2[:, c, :], f2[c]).then_inc(s_wld, 16)
                    for col, v in ((L1W, ln1_w), (L1B, ln1_b), (L2W, ln2_w), (L2B, ln2_b), (PB, proj_b), (F2B, fc2_b)):
                        sp.dma_start(vecs[:, col:col + 1], v[bass.ds(L, 1)].rearrange("a d -> d a")).then_inc(s_wld, 16)
                    f1b = fc1_b[bass.ds(L, 1)].rearrange("a (c d) -> c d a", c=2)
                    for c in range(2):
                        sp.dma_start(vecs[:, F1B + c:F1B + c + 1], f1b[c]).then_inc(s_wld, 16)

                def move(u):
                    par = u[1]
                    done(sp, "p_lo", u)
                    sp.dma_start(scratch[par].rearrange("a s p n -> p (a s) n"),
                                 parts_flat).then_inc(s_parted[par], 16)
                    sp.wait_ge(s_parted[par], VD(u, 1))
                    passed(sp)
                    done(sp, "a_keys", shift(u, -2), 7)
                    passed(sp)
                    for side, terms in ((0, Q_TERMS), (1, K_TERMS)):
                        for t, part in enumerate(terms):
                            src = scratch[par, part, side].rearrange("(d h) n -> d (h n)", h=HEADS)
                            sp.dma_start(stack[t * HD:(t + 1) * HD, par, side, :], src).then_inc(s_stacked[par], 16)

                parts_flat = parts.rearrange("p a s n -> p (a s) n")

                def chain_only(u, what):
                    if what == "prep":
                        move(u)

                def rnd(u, prep, tail):
                    if prep:
                        move(shift(u, 1))

                layers(sp, fold, rnd, chain_only)
                sp.wait_ge(s_stacked[0], VD((DEPTH * PAIRS - 1, 0, 0), NLD))
                sp.wait_ge(s_stacked[1], VD((DEPTH * PAIRS - 1, 1, 0), NLD))

            @block.gpsimd
            def _(pool):
                credit(pool, "p_hi p_res p_mid p_lo")
                pool.memset(vaug, 1.0).then_inc(s_ones, 1)
                pool.memset(msel, 0.0).then_inc(s_sel, 1)
                pool.wait_ge(s_sel, 1)
                for part in range(3):
                    pool.affine_select(out=msel, in_=msel, compare_op=ALU.not_equal, fill=1.0,
                                       base=-HG * part, pattern=[[-1, HG], [0, P]],
                                       channel_multiplier=1).then_inc(s_sel, 1)
                    pool.wait_ge(s_sel, part + 2)

                def split(u):
                    par = u[1]
                    done(pool, "p_qk_out", u)
                    pu = shift(u, -1)
                    pool.wait_ge(s_parted[pu[1]], VD(pu, 1))
                    passed(pool)
                    pool.tensor_scalar(parts[:, 0], qk32, 1.0, 0.0, ALU.mult, ALU.add).then_inc(sems["p_hi"], 1)
                    done(pool, "p_hi", u)
                    pool.tensor_tensor(res32, qk32, parts[:, 0], ALU.subtract).then_inc(sems["p_res"], 1)
                    done(pool, "p_res", u)
                    passed(pool)
                    pool.tensor_scalar(parts[:, 1], res32, 1.0, 0.0, ALU.mult, ALU.add).then_inc(sems["p_mid"], 1)
                    done(pool, "p_mid", u)
                    pool.tensor_tensor(parts[:, 2], res32, parts[:, 1], ALU.subtract).then_inc(sems["p_lo"], 1)

                def chain_only(u, what):
                    if what == "prep":
                        split(u)

                def rnd(u, prep, tail):
                    if prep:
                        split(shift(u, 1))

                layers(pool, lambda L: None, rnd, chain_only)

            @block.tensor
            def _(pe):
                credit(pe, "p_centered p_vared p_qk_mm p_v_mm t_projected t_centered t_vared t_fc1 t_fc2 "
                           "a_scores a_mT a_keys a_pv")
                pe.wait_ge(s_sel, 4)
                pe.wait_ge(s_ones, 1)
                pe.wait_ge(s_zero, 5)

                def fold(L):
                    pe.wait_ge(s_fold, L * FOLDS + FOLDS)
                    for col, w, b, ln in ((QB, wqk_perm[:, 0], bqk_perm[:, 0], L1B), (KB, wqk_perm[:, 1], bqk_perm[:, 1], L1B),
                                          (VB, wqkv_raw[:, 2 * D:3 * D], bqkv_row[:, 2 * D:3 * D], L1B),
                                          (HB, wfc1_raw[:, 0:D], None, L2B), (HB + 1, wfc1_raw[:, D:2 * D], None, L2B)):
                        last = pe.matmul(ps[:, 5, col:col + 1], w, vecs[:, ln:ln + 1], start=True, stop=b is None)
                        if b is not None:
                            last = pe.matmul(ps[:, 5, col:col + 1], b, e0[:, :], start=False, stop=True)
                    last.then_inc(s_bmm, 1)
                    pe.wait_ge(s_bias, L * BIASES + 3)
                    pe.matmul(ps[:, 6, 0:1], wproj_raw, bias[:, VB:VB + 1], start=True, stop=True).then_inc(s_bmm, 1)

                def chain(name, u, after):
                    par = u[1]
                    if name == "p_center":
                        done(pe, "t_done", shift(u, -3))
                        done(pe, "p_qk_out", shift(u, -1))
                        done(pe, "p_v_out", shift(u, -1))
                        if after is not None:
                            done(pe, "t_done", after)
                        pe.matmul(ps[:, 5, 0:T2], center[:, :], hu(u), start=True, stop=True).then_inc(sems["p_centered"], 1)
                    elif name == "p_var":
                        done(pe, "p_squared", u)
                        pe.matmul(ps[:, 6, 0:T2], mean[:, :], sq, start=True, stop=True).then_inc(sems["p_vared"], 1)
                    elif name == "p_qk":
                        done(pe, "p_normed", u)
                        pe.matmul(ps[:, 5, 0:T2], wq_f, y, start=True, stop=True)
                        pe.matmul(ps[:, 6, 0:T2], wk_f, y, start=True, stop=True).then_inc(sems["p_qk_mm"], 1)
                    elif name == "p_v":
                        done(pe, "p_qk_out", u)
                        for b in range(2):
                            for t in range(2):
                                last = pe.matmul(ps[0:KT[t], 5, (2 * b + t) * D:(2 * b + t + 1) * D],
                                                 y[:, b * NT + t * P:b * NT + t * P + KT[t]], wv_f, start=True, stop=True)
                        last.then_inc(sems["p_v_mm"], 1)
                    elif name == "t_proj":
                        done(pe, "p_v_out", after)
                        done(pe, "p_qk_out", after)
                        done(pe, "t_done", shift(u, -1))
                        done(pe, "a_out", u, STEPS - 1)
                        for g in range(2):
                            last = pe.matmul(ps[:, 5, 0:T2], wproj_pad[:, g, :], onorm[:, par, g, :], start=(g == 0), stop=(g == 1))
                        last.then_inc(sems["t_projected"], 1)
                    elif name == "t_center":
                        done(pe, "t_added", u)
                        pe.matmul(ps[:, 5, 0:T2], center[:, :], hu(u), start=True, stop=True).then_inc(sems["t_centered"], 1)
                    elif name == "t_var":
                        done(pe, "t_squared", u)
                        pe.matmul(ps[:, 6, 0:T2], mean[:, :], sq, start=True, stop=True).then_inc(sems["t_vared"], 1)
                    elif name == "t_fc1":
                        done(pe, "t_normed", u)
                        for c in range(2):
                            last = pe.matmul(ps[:, 5 + c, 0:T2], wfc1_f[:, c * D:(c + 1) * D], y, start=True, stop=True)
                        last.then_inc(sems["t_fc1"], 1)
                    elif name == "t_fc2":
                        done(pe, "t_gelu", u)
                        for c in range(2):
                            last = pe.matmul(ps[:, 5, 0:T2], wfc2[:, c, :], act[:, c, :], start=(c == 0), stop=(c == 1))
                        last.then_inc(sems["t_fc2"], 1)

                def attend(name, u, i, t):
                    par = u[1]
                    b, g = divmod(i, 2)
                    ap = i % 2
                    qs = stack[0:KROWS, par, 0, :].rearrange("p (h n) -> p h n", h=HEADS)
                    ks = stack[0:KROWS, par, 1, :].rearrange("p (h n) -> p h n", h=HEADS)
                    if name == "scores":
                        if i == 0 and t == 0:
                            pe.wait_ge(s_stacked[par], VD(u, NLD))
                        done(pe, "a_max", u, 2 * i + t - 1)
                        for hh in range(HG):
                            last = pe.matmul(ps[0:KT[t], hh // 2, (hh % 2) * NT:(hh % 2 + 1) * NT],
                                             qs[:, HG * g + hh, b * NT + t * P:b * NT + t * P + KT[t]],
                                             ks[:, HG * g + hh, b * NT:(b + 1) * NT], start=True, stop=True)
                        last.then_inc(sems["a_scores"], 1)
                    elif name == "mrow":
                        done(pe, "a_lo", u, i)
                        done(pe, "a_mrows", u, i - 1)
                        for tt in range(2):
                            last = pe.matmul(ps[0:32, 7, tt * P:tt * P + KT[tt]], mparts[0:KT[tt], ap, tt, :],
                                             identb[0:KT[tt], 0:KT[tt]], start=True, stop=True)
                        last.then_inc(sems["a_mT"], 1)
                    elif name == "keys":
                        if t == 0:
                            done(pe, "a_mrows", u, i)
                        done(pe, "a_exp", u, 2 * i + t - 1)
                        for hh in range(HG):
                            o = ps[0:KT[t], 2 + hh // 2, (hh % 2) * NT:(hh % 2 + 1) * NT]
                            pe.matmul(o, ks[:, HG * g + hh, b * NT + t * P:b * NT + t * P + KT[t]],
                                      qs[:, HG * g + hh, b * NT:(b + 1) * NT], start=True, stop=False)
                            last = pe.matmul(o, msel[:, hh, 0:KT[t]], mrows[:, ap, 0:NT], start=False, stop=True)
                        last.then_inc(sems["a_keys"], 1)
                    elif name == "values":
                        done(pe, "a_exp", u, 2 * i + 1)
                        done(pe, "a_out", u, i - 1)
                        for t_ in range(2):
                            for hh in range(HG):
                                last = pe.matmul(ps[32 * hh:32 * hh + 32, 4, 0:NT], vau[par][0:KT[t_], b, t_, HG * g + hh, :],
                                                 probs[0:KT[t_], ap, t_, hh, :], start=(t_ == 0), stop=(t_ == 1))
                        last.then_inc(sems["a_pv"], 1)

                def chain_only(u, what):
                    for name in (PREP if what == "prep" else TAIL):
                        chain(name, u, shift(u, -1) if what == "prep" else u)

                def rnd(u, prep, tail):
                    for name, i, t in ticks(prep, tail):
                        if name in PREP:
                            chain(name, shift(u, 1), None)
                        elif name in TAIL:
                            chain(name, shift(u, -1), shift(u, 1) if prep else u)
                        else:
                            attend(name, u, i, t)

                layers(pe, fold, rnd, chain_only)

            @block.scalar
            def _(sc):
                credit(sc, "p_squared p_logged p_rstd p_qk_out t_squared t_logged t_rstd t_gelu "
                           "a_exp a_logsum a_rsum")

                def fold(L):
                    exp_ln_tables()
                    sc.wait_ge(s_bias, L * BIASES + BIASES)

                def exp_ln_tables():
                    sc.preload_act_table_set("natural_log_exp_and_others")

                def rstd(pre, u):
                    done(sc, pre + "_vared", u)
                    sc.activation(rs, ps[:, 6, 0:T2], ACT.Ln, bias=eps_col[:, :]).then_inc(sems[pre + "_logged"], 1)
                    done(sc, pre + "_logged", u)
                    sc.activation(rs, rs, ACT.Exp, scale=-0.5).then_inc(sems[pre + "_rstd"], 1)

                def chain(name, u):
                    if name == "p_center" or name == "t_center":
                        pre = name[0]
                        done(sc, pre + "_centered", u)
                        sc.activation(sq, ps[:, 5, 0:T2], ACT.Square).then_inc(sems[pre + "_squared"], 1)
                    elif name == "p_var" or name == "t_var":
                        rstd(name[0], u)
                    elif name == "p_qk":
                        done(sc, "p_qk_mm", u)
                        done(sc, "p_lo", shift(u, -1))
                        sc.activation(qk32[:, 0, :], ps[:, 5, 0:T2], ACT.Identity, bias=bias[:, QB:QB + 1], scale=SCALE)
                        sc.activation(qk32[:, 1, :], ps[:, 6, 0:T2], ACT.Identity, bias=bias[:, KB:KB + 1]).then_inc(sems["p_qk_out"], 1)
                    elif name == "t_fc1":
                        done(sc, "t_fc1", u)
                        sc.activation(act[:, 0, :], ps[:, 5, 0:T2], ACT.Gelu, bias=bias[:, HB:HB + 1])
                        sc.activation(act[:, 1, :], ps[:, 6, 0:T2], ACT.Gelu, bias=bias[:, HB + 1:HB + 2]).then_inc(sems["t_gelu"], 1)
                        exp_ln_tables()

                def attend(name, u, i, t):
                    ap = i % 2
                    if name == "keys":
                        done(sc, "a_keys", u, 2 * i + t)
                        done(sc, "a_pv", u, i - 2)
                        sc.activation(probs[0:KT[t], ap, t].rearrange("p (a b) n -> p a (b n)", a=2),
                                      ps[0:KT[t], 2:4, 0:2 * NT], ACT.Exp).then_inc(sems["a_exp"], 1)
                    elif name == "values":
                        done(sc, "a_sums", u, i)
                        done(sc, "a_out", u, i - 2)
                        sc.activation(rsum[:, ap], sums[:, ap], ACT.Ln).then_inc(sems["a_logsum"], 1)
                        done(sc, "a_logsum", u, i)
                        sc.activation(rsum[:, ap], rsum[:, ap], ACT.Exp, scale=-1.0).then_inc(sems["a_rsum"], 1)

                def chain_only(u, what):
                    for name in (PREP if what == "prep" else TAIL):
                        chain(name, u)

                def rnd(u, prep, tail):
                    for name, i, t in ticks(prep, tail):
                        if name in PREP:
                            chain(name, shift(u, 1))
                        elif name in TAIL:
                            chain(name, shift(u, -1))
                        else:
                            attend(name, u, i, t)

                layers(sc, fold, rnd, chain_only, exp_ln_tables)

            @block.vector
            def _(dve):
                credit(dve, "p_normed p_v_out t_added t_normed t_done a_max a_hi a_res a_mid a_lo a_mrows a_sums a_out")
                for z in (negmax, mparts, mrows):
                    dve.memset(z, 0.0).then_inc(s_zero, 1)
                dve.memset(wproj_pad, 0.0).then_inc(s_zero, 1)
                dve.memset(bqkv_row, 0.0).then_inc(s_zero, 1)

                def fold(L):
                    dve.wait_ge(s_wld, L * (16 * NWL) + 16 * NWL)
                    for s_ in range(2):
                        dve.tensor_copy(wqk_perm[:, s_].rearrange("p (d h) -> p d h", h=HEADS),
                                        wqkv_raw[:, s_ * D:(s_ + 1) * D].rearrange("p (h d) -> p d h", h=HEADS)).then_inc(s_fold, 1)
                        dve.tensor_copy(bqk_perm[:, s_].rearrange("p (d h) -> p d h", h=HEADS),
                                        bqkv_row[:, s_ * D:(s_ + 1) * D].rearrange("p (h d) -> p d h", h=HEADS)).then_inc(s_fold, 1)
                    dve.wait_ge(s_fold, L * FOLDS + 4)
                    for dst, src, ln in ((wq_f, wqk_perm[:, 0], L1W), (wk_f, wqk_perm[:, 1], L1W),
                                         (wv_f, wqkv_raw[:, 2 * D:3 * D], L1W), (wfc1_f, wfc1_raw, L2W)):
                        dve.tensor_scalar(dst, src, vecs[:, ln:ln + 1], None, ALU.mult).then_inc(s_fold, 1)
                    dve.wait_ge(s_bmm, L * BMMS + 1)
                    dve.tensor_scalar(bias[:, QB:QB + 1], ps[:, 5, QB:QB + 1], SCALE, None, ALU.mult).then_inc(s_bias, 1)
                    dve.tensor_copy(bias[:, KB:VB + 1], ps[:, 5, KB:VB + 1]).then_inc(s_bias, 1)
                    dve.tensor_tensor(bias[:, HB:HB + 2], ps[:, 5, HB:HB + 2], vecs[:, F1B:F1B + 2], ALU.add).then_inc(s_bias, 1)
                    dve.wait_ge(s_bmm, L * BMMS + 2)
                    dve.tensor_tensor(bias[:, OB:OB + 1], ps[:, 6, 0:1], vecs[:, PB:PB + 1], ALU.add).then_inc(s_bias, 1)
                    dve.wait_ge(s_bias, L * BIASES + BIASES)

                def chain(name, u):
                    par = u[1]
                    if name == "p_var" or name == "t_var":
                        pre = name[0]
                        done(dve, pre + "_rstd", u)
                        dve.tensor_tensor(y, ps[:, 5, 0:T2], rs, ALU.mult).then_inc(sems[pre + "_normed"], 1)
                    elif name == "p_v":
                        done(dve, "p_v_mm", u)
                        done(dve, "a_pv", shift(u, -2), STEPS - 1)
                        for t in range(2):
                            src = ps[0:KT[t], 5, :].rearrange("p (b t h c) -> p b t h c", b=2, t=2, h=HEADS)[:, :, t]
                            for b in range(2):
                                last = dve.tensor_copy(vau[par][0:KT[t], b, t, :, 0:HD], src[:, b])
                        last.then_inc(sems["p_v_out"], 1)
                    elif name == "t_proj":
                        done(dve, "t_projected", u)
                        dve.scalar_tensor_tensor(hu(u), ps[:, 5, 0:T2], bias[:, OB:OB + 1], hu(u), ALU.add, ALU.add).then_inc(sems["t_added"], 1)
                    elif name == "t_fc2":
                        done(dve, "t_fc2", u)
                        dve.scalar_tensor_tensor(hu(u), ps[:, 5, 0:T2], vecs[:, F2B:F2B + 1], hu(u), ALU.add, ALU.add).then_inc(sems["t_done"], 1)

                def attend(name, u, i, t):
                    par = u[1]
                    b, g = divmod(i, 2)
                    ap = i % 2
                    mp = mparts[:, ap]
                    if name == "scores":
                        done(dve, "a_scores", u, 2 * i + t)
                        dve.tensor_reduce(negmax[0:KT[t], ap, t], ps[0:KT[t], 0:2, 0:2 * NT].rearrange(
                            "p a (b n) -> p a b n", b=2), AX.X, ALU.max, negate=True).then_inc(sems["a_max"], 1)
                    elif name == "max":
                        done(dve, "a_max", u, 2 * i + 1)
                        done(dve, "a_mT", u, i - 2)
                        dve.tensor_copy(mp[:, :, 0:HG], negmax[:, ap]).then_inc(sems["a_hi"], 1)
                        done(dve, "a_hi", u, i)
                        dve.tensor_tensor(negres[:, ap], negmax[:, ap], mp[:, :, 0:HG], ALU.subtract).then_inc(sems["a_res"], 1)
                        done(dve, "a_res", u, i)
                        dve.tensor_copy(mp[:, :, HG:2 * HG], negres[:, ap]).then_inc(sems["a_mid"], 1)
                        done(dve, "a_mid", u, i)
                        dve.tensor_tensor(mp[:, :, 2 * HG:3 * HG], negres[:, ap], mp[:, :, HG:2 * HG], ALU.subtract).then_inc(sems["a_lo"], 1)
                    elif name == "mrow":
                        done(dve, "a_mT", u, i)
                        done(dve, "a_keys", u, 2 * (i - 2) + 1)
                        dve.tensor_copy(mrows[0:32, ap, 0:NT], ps[0:32, 7, 0:NT]).then_inc(sems["a_mrows"], 1)
                    elif name == "values":
                        done(dve, "a_pv", u, i)
                        done(dve, "a_logsum", u, i - 2)
                        passed(dve)
                        dve.stream_shuffle(sums[:, ap], ps[:, 4, 0:NT], [HD + k % HD for k in range(32)]).then_inc(sems["a_sums"], 1)
                        done(dve, "a_rsum", u, i)
                        done(dve, "t_projected", shift(u, -2))
                        dve.tensor_tensor(onorm[:, par, g, b * NT:(b + 1) * NT], ps[:, 4, 0:NT], rsum[:, ap], ALU.mult).then_inc(sems["a_out"], 1)

                def chain_only(u, what):
                    for name in (PREP if what == "prep" else TAIL):
                        chain(name, u)

                def rnd(u, prep, tail):
                    for name, i, t in ticks(prep, tail):
                        if name in PREP:
                            chain(name, shift(u, 1))
                        elif name in TAIL:
                            chain(name, shift(u, -1))
                        else:
                            attend(name, u, i, t)

                layers(dve, fold, rnd, chain_only)
        if debug == "layers":
            s_dbg = sem("s_dbg")
            with nc.Block() as block:
                @block.sync
                def _(sp):
                    sp.dma_start(out, h[:, :]).then_inc(s_dbg, 16)
                    sp.wait_ge(s_dbg, 16)
            return

        at[0] = 0
        txt_rows = carve(2, D)
        hc, skip, yn, zz = carve(S2), carve(S2), carve(S2), carve(S2)
        sq3, rs3 = carve(S2), carve(S2)
        PADW = TAPS - 1
        xpad = carve(2, S + 2 * PADW)
        cv = carve(2, S2)
        ex, op, lg = carve(2 * S2), carve(2 * S2), carve(2 * S2)
        lz = carve(S2)
        dbc = carve(2, S2)
        bres = carve(2, S2)
        uu = carve(2, 2, S2)
        delta = carve(2, 2, S2)
        du = carve(2, 2, S2)
        bcs = carve(2, 2, S2, dt=BF16)
        zg = carve(2, S2)
        res = carve(2, S2)
        decay = carve(2, 2, S2)
        brep = carve(2, 2, S2)
        inp = carve(2, 2, S2)
        state = carve(2, 2, S2)
        prod = carve(2, 2, S2)
        h1, gl, fo = carve(S2), carve(S2), carve(S2)
        rows = carve(2 * 2, D)
        wp_raw, wp_f = carve(2 * D), carve(2 * D)
        wx_pad = carve(D)
        wdt_pad = carve(D)
        w1_raw, w2_raw, w1T, w2T = carve(D), carve(D), carve(D), carve(D)
        diagD = carve(D)
        amat = carve(NS)
        alog = carve(NS)
        mvec = carve(16)
        taps = carve(TAPS)
        bxz = carve(2)
        bsel = carve(2 * NS, P, dt=BF16)
        NW, NB, LG, LB, CB, DTB, DV, B1, B2 = range(9)

        for n_ in ("n_centered n_squared n_vared n_logged n_rstd n_scaled n_normed n_txt n_txt_out "
                   "k_centered k_squared k_vared k_logged k_rstd k_normed k_res "
                   "g_centered g_squared g_vared g_logged g_rstd g_normed xz_mm xz_out conv_step "
                   "su_abs su_exp su_one su_ln su_err su_cor su_out dbc_mm dbc_out b_hi b_res b_mid b_lo dt_mm dt_out "
                   "sd_abs sd_exp sd_one sd_ln sd_err sd_cor sd_out du_out "
                   "z_abs z_exp z_ln z_arg z_sig z_out "
                   "f_gated f_added f_centered f_squared f_vared f_logged f_rstd f_normed f_mm1 f_gelu f_mm2 f_out f_T f_rows").split():
            sem(n_)
            W[n_] = 2 * TAPS if n_ == "conv_step" else 1
        for n_ in "m_b m_brep m_inp m_c m_decay m_scan m_prod m_sum".split():
            sem(n_)
            W[n_] = NS
        s_txt = [sem("s_txt0"), sem("s_txt1")]
        s_stored = [sem("s_stored0"), sem("s_stored1")]
        s_w3, s_set, s_set2, s_mm3, s_ev3, s_neg = (sem(n_) for n_ in "s_w3 s_set s_set2 s_mm3 s_ev3 s_neg".split())
        PRE = ("n_center", "n_var", "txt", "k_center", "k_var", "g_center", "g_var", "xz", "conv", "z1", "su1", "z2",
               "su2", "z3", "su3", "dbc", "split", "dt", "sd1", "sd2", "sd3", "du")
        POST = ("gate", "f_center", "f_var", "f_1", "f_2", "f_T")

        def ticks3(pre, post):
            chain = (list(POST) if post else []) + (list(PRE) if pre else [])
            yield "start", 0
            for n in range(NS):
                yield "ahead", n + 1
                yield "step", n
                for c in chain[:2]:
                    yield c, 0
                chain = chain[2:]
            assert not chain

        def fusion(eng, rnd, chain_only, at_block=lambda: None):
            first, last = (0, 0, 0), (PAIRS - 1, 1, PAIRS - 1)
            chain_only(first, "pre")
            rnd(first, pre=True, post=False)
            with eng.Fori(0, PAIRS - 1) as it:
                at_block()
                rnd((it, 1, it), pre=True, post=True)
                rnd((it + 1, 0, it + 1), pre=True, post=True)
            at_block()
            rnd(last, pre=False, post=True)
            chain_only(last, "post")

        def images(ap, n=S):
            return ap.rearrange("p (b n) -> p b n", n=n)

        def flat(ap):
            return ap.rearrange("p a n -> p (a n)")

        with nc.Block() as block:
            @block.sync
            def _(sp):
                sp.wait_ge(s_set, 7)
                def put(dst, src):
                    sp.dma_start(dst, src).then_inc(s_w3, 16)
                put(wp_raw, m_W_proj)
                put(wx_pad[:, 0:RANK + 2 * NS], m_W_x)
                put(wx_pad[:, 2 * RANK:3 * RANK], m_W_x[:, RANK:RANK + 2 * NS])
                put(wx_pad[:, 3 * RANK:4 * RANK], m_W_x[:, RANK:RANK + 2 * NS])
                put(wdt_pad[0:RANK], m_W_dt)
                put(w1_raw, f_W1)
                put(w2_raw, f_W2)
                put(alog, m_A_log)
                put(taps, m_conv_w.rearrange("d a k -> d (a k)"))
                for col, v in ((NW, norm_w), (NB, norm_b), (LG, m_ln_g), (LB, m_ln_b), (CB, m_conv_b), (DTB, m_b_dt),
                               (DV, m_D), (B1, f_b1), (B2, f_b2)):
                    put(mvec[:, col:col + 1], v.rearrange("(d a) -> d a", a=1))

                def load_txt(u):
                    q, par = u[:2]
                    done(sp, "n_txt", shift(u, -2))
                    src = txt[bass.ds(q * 4 + 2 * par, 2)].rearrange("b n d -> (b n) d")
                    sp.dma_start(txt_rows[0:2 * TXT, par, :], src).then_inc(s_txt[par], 16)

                def store(u):
                    q, par = u[:2]
                    done(sp, "f_rows", u)
                    o = out[bass.ds(q * 4 + 2 * par, 2)].rearrange("b n d -> n b d")
                    r = rows.rearrange("p (b t) d -> p b t d", b=2)
                    sp.dma_start(o[0:P], r[:, :, 0]).then_inc(s_stored[par], 16)
                    sp.dma_start(o[P:S], r[0:S - P, :, 1]).then_inc(s_stored[par], 16)

                def chain_only(u, what):
                    if what == "pre":
                        load_txt(u)
                    else:
                        store(u)

                def rnd(u, pre, post):
                    if pre:
                        load_txt(shift(u, 1))
                    if post:
                        store(shift(u, -1))

                fusion(sp, rnd, chain_only)
                for par in range(2):
                    sp.wait_ge(s_stored[par], VD((PAIRS - 1, par, 0), 2))

            @block.gpsimd
            def _(pool):
                credit(pool, "su_one su_cor sd_one sd_cor b_hi b_res b_mid b_lo du_out m_inp")
                for z in (txt_rows, flat(xpad), wdt_pad, diagD, bsel, flat(decay[:, 0]), flat(decay[:, 1])):
                    pool.memset(z, 0.0).then_inc(s_set, 1)
                pool.memset(bcs.rearrange("p a b n -> p (a b n)"), 0.0).then_inc(s_set2, 1)
                pool.wait_ge(s_set, 7)
                for k in range(3):
                    pool.affine_select(out=bsel, in_=bsel, compare_op=ALU.not_equal, fill=1.0, base=-32 * (k + 1),
                                       pattern=[[-1, 2 * NS], [0, P]], channel_multiplier=1).then_inc(s_set2, 1)
                    pool.wait_ge(s_set2, k + 2)
                pool.wait_ge(s_w3, 16 * 18)
                for w in (w1_raw, w2_raw):
                    pool.affine_select(out=w, in_=w, compare_op=ALU.is_ge, fill=0.0, base=0,
                                       pattern=[[-1, D]], channel_multiplier=1).then_inc(s_set2, 1)

                def chain(name, u):
                    par = u[1]
                    if name in ("su1", "sd1"):
                        pre = name[:2]
                        done(pool, pre + "_exp", u)
                        passed(pool)
                        pool.tensor_scalar(op, ex, 1.0, 1.0, ALU.mult, ALU.add).then_inc(sems[pre + "_one"], 1)
                    elif name in ("su2", "sd2"):
                        pre = name[:2]
                        done(pool, pre + "_ln", u)
                        done(pool, pre + "_err", u)
                        pool.tensor_tensor(lg, lg, op, ALU.subtract).then_inc(sems[pre + "_cor"], 1)
                    elif name == "split":
                        bc = bcs[:, par]
                        done(pool, "dbc_out", u)
                        done(pool, "m_c", shift(u, -2), NS - 1)
                        passed(pool)
                        pool.tensor_scalar(bc, dbc, 1.0, 0.0, ALU.mult, ALU.add).then_inc(sems["b_hi"], 1)
                        done(pool, "b_hi", u)
                        pool.tensor_tensor(bres[64:P], dbc[64:P], bc[64:P], ALU.subtract).then_inc(sems["b_res"], 1)
                        done(pool, "b_res", u)
                        passed(pool)
                        pool.tensor_scalar(bc[64:P], bres[64:P], 1.0, 0.0, ALU.mult, ALU.add).then_inc(sems["b_mid"], 1)
                        done(pool, "b_mid", u)
                        pool.tensor_tensor(bc[96:P], bres[96:P], bc[96:P], ALU.subtract).then_inc(sems["b_lo"], 1)
                        done(pool, "b_lo", u)
                        passed(pool)
                    elif name == "du":
                        done(pool, "sd_out", u)
                        pool.tensor_tensor(flat(du[:, par]), flat(delta[:, par]), flat(uu[:, par]), ALU.mult).then_inc(sems["du_out"], 1)

                def inputs(u, n):
                    par = u[1]
                    if n == 0:
                        done(pool, "du_out", u)
                    done(pool, "m_brep", u, n)
                    done(pool, "m_scan", u, n - 2)
                    pool.tensor_tensor(flat(inp[:, n % 2]), flat(du[:, par]), flat(brep[:, n % 2]), ALU.mult).then_inc(sems["m_inp"], 1)

                def chain_only(u, what):
                    for name in (PRE if what == "pre" else POST):
                        chain(name, u)

                def rnd(u, pre, post):
                    for name, n in ticks3(pre, post):
                        if name == "start":
                            inputs(u, 0)
                        elif name == "ahead" and n < NS:
                            inputs(u, n)
                        elif name in PRE:
                            chain(name, shift(u, 1))

                fusion(pool, rnd, chain_only)

            @block.tensor
            def _(pe):
                credit(pe, "n_centered n_vared n_txt k_centered k_vared g_centered g_vared xz_mm dbc_mm dt_mm "
                           "f_centered f_vared f_mm1 f_mm2 f_T m_b m_c m_sum")
                pe.wait_ge(s_set, 7)
                pe.wait_ge(s_w3, 16 * 18)
                pe.wait_ge(s_set2, 6)
                pe.matmul(ps[:, 6, 0:1], wp_raw[:, 0:D], mvec[:, LB:LB + 1], start=True, stop=True)
                pe.matmul(ps[:, 6, 1:2], wp_raw[:, D:2 * D], mvec[:, LB:LB + 1], start=True, stop=True)
                pe.transpose(ps[:, 7, 0:D], w1_raw, ident[:, :])
                pe.transpose(ps[:, 7, D:2 * D], w2_raw, ident[:, :]).then_inc(s_mm3, 1)
                pe.wait_ge(s_ev3, 6)

                def center_of(src, pre):
                    pe.matmul(ps[:, 6, 0:src.shape[-1]], center[:, :], src, start=True, stop=True).then_inc(sems[pre + "_centered"], 1)

                def var_of(n, pre, u):
                    done(pe, pre + "_squared", u)
                    pe.matmul(ps[:, 7, 0:n], mean[:, :], sq3[:, 0:n], start=True, stop=True).then_inc(sems[pre + "_vared"], 1)

                def chain(name, u, after=None):
                    par = u[1]
                    if name == "n_center":
                        done(pe, "f_rows", shift(u, -2))
                        done(pe, "dt_out", shift(u, -1))
                        center_of(hu(u), "n")
                    elif name == "n_var":
                        var_of(T2, "n", u)
                    elif name == "txt":
                        pe.wait_ge(s_txt[par], VD(u, 1))
                        done(pe, "n_logged", u)
                        pe.transpose(ps[:, 7, 0:P], txt_rows[:, par, :], ident[:, :]).then_inc(sems["n_txt"], 1)
                    elif name == "k_center":
                        done(pe, "n_normed", u)
                        done(pe, "n_txt_out", u)
                        center_of(hc, "k")
                    elif name == "k_var":
                        var_of(S2, "k", u)
                    elif name == "g_center":
                        done(pe, "k_normed", u)
                        center_of(skip, "g")
                    elif name == "g_var":
                        var_of(S2, "g", u)
                    elif name == "xz":
                        done(pe, "g_normed", u)
                        for k in range(2):
                            last = pe.matmul(ps[:, 6 + k, 0:S2], wp_f[:, k * D:(k + 1) * D], yn, start=True, stop=True)
                        last.then_inc(sems["xz_mm"], 1)
                    elif name == "dbc":
                        done(pe, "xz_out", u)
                        done(pe, "su_out", u)
                        for k in range(2):
                            last = pe.matmul(ps[:, 6 + k, 0:S2], wx_pad, uu[:, par, k, :], start=True, stop=True)
                        last.then_inc(sems["dbc_mm"], 1)
                    elif name == "dt":
                        done(pe, "dbc_out", u)
                        for k in range(2):
                            last = pe.matmul(ps[:, 6 + k, 0:S2], wdt_pad, dbc[:, k, :], start=True, stop=True)
                        last.then_inc(sems["dt_mm"], 1)
                    elif name == "f_center":
                        done(pe, "f_added", u)
                        done(pe, "f_rows", shift(u, -1))
                        done(pe, "dt_out", after)
                        center_of(h1, "f")
                    elif name == "f_var":
                        var_of(S2, "f", u)
                    elif name == "f_1":
                        done(pe, "f_normed", u)
                        pe.matmul(ps[:, 6, 0:S2], w1T, yn, start=True, stop=True).then_inc(sems["f_mm1"], 1)
                    elif name == "f_2":
                        done(pe, "f_gelu", u)
                        pe.matmul(ps[:, 7, 0:S2], w2T, gl, start=True, stop=True).then_inc(sems["f_mm2"], 1)
                    elif name == "f_T":
                        done(pe, "f_out", u)
                        for b in range(2):
                            for t in range(2):
                                m = P if t == 0 else S - P
                                last = pe.transpose(ps[0:m, 6, (2 * b + t) * D:(2 * b + t + 1) * D],
                                                    fo[:, b * S + t * P:b * S + t * P + m], ident[:, :])
                        last.then_inc(sems["f_T"], 1)

                def rep_b(u, n):
                    if n == 0:
                        done(pe, "b_lo", u)
                    done(pe, "m_brep", u, n - 1)
                    for k in range(2):
                        last = pe.matmul(ps[:, k, 0:S2], bsel[:, n, :], bcs[:, u[1], k, :], start=True, stop=True)
                    last.then_inc(sems["m_b"], 1)

                def rep_c(u, n):
                    done(pe, "m_prod", u, n - 1)
                    for k in range(2):
                        last = pe.matmul(ps[:, 2 + k, 0:S2], bsel[:, NS + n, :], bcs[:, u[1], k, :], start=True, stop=True)
                    last.then_inc(sems["m_c"], 1)

                def add_up(u, n):
                    par = u[1]
                    if n == 0:
                        done(pe, "f_gated", shift(u, -2))
                        pe.matmul(ps[:, 4 + par, 0:S2], diagD, uu[:, par, 0, :], start=True, stop=False)
                        pe.matmul(ps[:, 4 + par, 0:S2], diagD, uu[:, par, 1, ::-1], start=False, stop=False)
                    done(pe, "m_prod", u, n)
                    pe.matmul(ps[:, 4 + par, 0:S2], ident[:, :], prod[:, n % 2, 0, :], start=False, stop=False)
                    pe.matmul(ps[:, 4 + par, 0:S2], ident[:, :], prod[:, n % 2, 1, ::-1], start=False,
                              stop=(n == NS - 1)).then_inc(sems["m_sum"], 1)

                def chain_only(u, what):
                    for name in (PRE if what == "pre" else POST):
                        chain(name, u, u)

                def rnd(u, pre, post):
                    for name, n in ticks3(pre, post):
                        if name == "start":
                            rep_b(u, 0)
                            rep_c(u, 0)
                        elif name == "ahead":
                            if n < NS:
                                rep_b(u, n)
                        elif name == "step":
                            if n + 1 < NS:
                                rep_c(u, n + 1)
                            add_up(u, n)
                        elif name in PRE:
                            chain(name, shift(u, 1))
                        else:
                            chain(name, shift(u, -1), u)

                fusion(pe, rnd, chain_only)

            @block.scalar
            def _(sc):
                credit(sc, "n_squared n_logged n_rstd k_squared k_logged k_rstd g_squared g_logged g_rstd xz_out "
                           "su_abs su_exp su_ln dbc_out dt_out sd_abs sd_exp sd_ln z_abs z_exp z_ln z_sig "
                           "f_squared f_logged f_rstd f_gelu f_rows m_brep m_decay")

                def exp_ln_tables():
                    sc.preload_act_table_set("natural_log_exp_and_others")

                exp_ln_tables()
                sc.wait_ge(s_w3, 16 * 18)
                sc.wait_ge(s_mm3, 1)
                sc.activation(w1T, ps[:, 7, 0:D], ACT.Copy).then_inc(s_ev3, 1)
                sc.activation(w2T, ps[:, 7, D:2 * D], ACT.Copy).then_inc(s_ev3, 1)
                sc.activation(alog, alog, ACT.Exp).then_inc(s_neg, 1)
                sc.wait_ge(s_neg, 1)
                sc.activation(amat, alog, ACT.Copy, scale=-1.0).then_inc(s_neg, 1)
                sc.wait_ge(s_neg, 2)
                sc.wait_ge(s_ev3, 6)

                def squared(n, pre, u):
                    done(sc, pre + "_centered", u)
                    sc.activation(sq3[:, 0:n], ps[:, 6, 0:n], ACT.Square).then_inc(sems[pre + "_squared"], 1)

                def rstd(n, pre, u):
                    done(sc, pre + "_vared", u)
                    sc.activation(rs3[:, 0:n], ps[:, 7, 0:n], ACT.Ln, bias=eps_col[:, :]).then_inc(sems[pre + "_logged"], 1)
                    done(sc, pre + "_logged", u)
                    sc.activation(rs3[:, 0:n], rs3[:, 0:n], ACT.Exp, scale=-0.5).then_inc(sems[pre + "_rstd"], 1)

                def exp_neg_abs(dst, src, pre, u):
                    sc.activation(dst, src, ACT.Abs).then_inc(sems[pre + "_abs"], 1)
                    done(sc, pre + "_abs", u)
                    sc.activation(dst, dst, ACT.Exp, scale=-1.0).then_inc(sems[pre + "_exp"], 1)

                def chain(name, u):
                    par = u[1]
                    if name in ("n_center", "k_center", "g_center", "f_center"):
                        squared(T2 if name[0] == "n" else S2, name[0], u)
                    elif name in ("n_var", "k_var", "g_var", "f_var"):
                        rstd(T2 if name[0] == "n" else S2, name[0], u)
                    elif name == "xz":
                        done(sc, "xz_mm", u)
                        done(sc, "conv_step", shift(u, -1), 2 * TAPS - 1)
                        done(sc, "z_out", shift(u, -1))
                        sc.activation(xpad[:, :, PADW:PADW + S], images(ps[:, 6, 0:S2]), ACT.Identity, bias=bxz[:, 0:1])
                        sc.activation(zz, ps[:, 7, 0:S2], ACT.Identity, bias=bxz[:, 1:2]).then_inc(sems["xz_out"], 1)
                    elif name == "z1":
                        done(sc, "xz_out", u)
                        exp_neg_abs(lz, zz, "z", u)
                    elif name == "z2":
                        done(sc, "z_exp", u)
                        sc.activation(lz, lz, ACT.Ln, bias=one_col[:, :]).then_inc(sems["z_ln"], 1)
                    elif name == "z3":
                        done(sc, "z_arg", u)
                        sc.activation(lz, lz, ACT.Exp).then_inc(sems["z_sig"], 1)
                    elif name == "su1":
                        done(sc, "conv_step", u, 2 * TAPS - 1)
                        exp_neg_abs(ex, flat(cv), "su", u)
                    elif name == "sd1":
                        done(sc, "dt_mm", u)
                        done(sc, "su_out", u)
                        sc.activation(cv, ps[:, 6:8, 0:S2], ACT.Identity, bias=mvec[:, DTB:DTB + 1]).then_inc(sems["dt_out"], 1)
                        done(sc, "dt_out", u)
                        exp_neg_abs(ex, flat(cv), "sd", u)
                    elif name in ("su2", "sd2"):
                        pre = name[:2]
                        done(sc, pre + "_one", u)
                        sc.activation(lg, op, ACT.Ln).then_inc(sems[pre + "_ln"], 1)
                    elif name == "dbc":
                        done(sc, "dbc_mm", u)
                        done(sc, "b_res", shift(u, -1))
                        sc.activation(dbc, ps[:, 6:8, 0:S2], ACT.Copy).then_inc(sems["dbc_out"], 1)
                    elif name == "f_1":
                        done(sc, "f_mm1", u)
                        sc.activation(gl, ps[:, 6, 0:S2], ACT.Gelu, bias=mvec[:, B1:B1 + 1]).then_inc(sems["f_gelu"], 1)
                        exp_ln_tables()
                    elif name == "f_T":
                        done(sc, "f_T", u)
                        pu = shift(u, -1)
                        sc.wait_ge(s_stored[pu[1]], VD(pu, 2))
                        pv = ps[:, 6, :].rearrange("p (b t d) -> p b t d", b=2, t=2)
                        rv = rows.rearrange("p (b t) d -> p b t d", b=2)
                        sc.activation(rv[:, :, 0], pv[:, :, 0], ACT.Copy)
                        sc.activation(rv[0:S - P, :, 1], pv[0:S - P, :, 1], ACT.Copy).then_inc(sems["f_rows"], 1)

                def rep_b(u, n):
                    done(sc, "m_b", u, n)
                    done(sc, "m_inp", u, n - 2)
                    sc.activation(brep[:, n % 2], ps[:, 0:2, 0:S2], ACT.Copy).then_inc(sems["m_brep"], 1)

                def decays(u, n):
                    par = u[1]
                    if n == 0:
                        done(sc, "sd_out", u)
                    done(sc, "m_scan", u, n - 2)
                    o = decay[:, n % 2].rearrange("p k (b s) -> p (k b) s", b=2)[:, :, 1:S]
                    i = delta[:, par].rearrange("p k (b s) -> p (k b) s", b=2)[:, :, 1:S]
                    sc.activation(o, i, ACT.Exp, scale=amat[:, n:n + 1]).then_inc(sems["m_decay"], 1)

                def chain_only(u, what):
                    for name in (PRE if what == "pre" else POST):
                        chain(name, u)

                def rnd(u, pre, post):
                    for name, n in ticks3(pre, post):
                        if name == "start" or (name == "ahead" and n < NS):
                            rep_b(u, n)
                            decays(u, n)
                        elif name in PRE:
                            chain(name, shift(u, 1))
                        elif name in POST:
                            chain(name, shift(u, -1))

                fusion(sc, rnd, chain_only, exp_ln_tables)

            @block.vector
            def _(dve):
                credit(dve, "n_scaled n_normed n_txt_out k_normed k_res g_normed conv_step su_err su_out sd_err sd_out "
                            "z_arg z_out f_gated f_added f_normed f_out m_scan m_prod")
                dve.wait_ge(s_w3, 16 * 18)
                dve.tensor_scalar(wp_f, wp_raw, mvec[:, LG:LG + 1], None, ALU.mult).then_inc(s_ev3, 1)
                dve.wait_ge(s_set, 7)
                dve.tensor_scalar(diagD, ident[:, :], mvec[:, DV:DV + 1], None, ALU.mult).then_inc(s_ev3, 1)
                dve.wait_ge(s_mm3, 1)
                dve.tensor_copy(bxz, ps[:, 6, 0:2]).then_inc(s_ev3, 1)
                dve.memset(lz, 0.0).then_inc(s_ev3, 1)

                def conv(u):
                    j = 0
                    vf = images(cv[:, 0, :])
                    vb = images(cv[:, 1, :])[:, ::-1, ::-1]
                    for k in range(TAPS):
                        for v, off in ((vf, k), (vb, 2 * PADW - k)):
                            src = xpad[:, :, off:off + S]
                            if k == 0:
                                dve.tensor_scalar(v, src, taps[:, 0:1], mvec[:, CB:CB + 1], ALU.mult, ALU.add).then_inc(sems["conv_step"], 1)
                            else:
                                done(dve, "conv_step", u, j - 2)
                                dve.scalar_tensor_tensor(v, src, taps[:, k:k + 1], v, ALU.mult, ALU.add).then_inc(sems["conv_step"], 1)
                            j += 1

                def chain(name, u):
                    par = u[1]
                    if name == "n_var":
                        done(dve, "n_rstd", u)
                        done(dve, "k_res", shift(u, -1))
                        o = images(hc)[:, :, 0:NT]
                        dve.scalar_tensor_tensor(o, images(ps[:, 6, 0:T2], NT), mvec[:, NW:NW + 1], images(rs3[:, 0:T2], NT),
                                                 ALU.mult, ALU.mult).then_inc(sems["n_scaled"], 1)
                        done(dve, "n_scaled", u)
                        dve.tensor_scalar(o, o, mvec[:, NB:NB + 1], None, ALU.add).then_inc(sems["n_normed"], 1)
                    elif name == "txt":
                        done(dve, "n_txt", u)
                        dve.tensor_copy(images(hc)[:, :, NT:S], images(ps[:, 7, 0:2 * TXT], TXT)).then_inc(sems["n_txt_out"], 1)
                    elif name == "k_var":
                        done(dve, "k_rstd", u)
                        dve.tensor_tensor(skip, ps[:, 6, 0:S2], rs3, ALU.mult).then_inc(sems["k_normed"], 1)
                        done(dve, "k_normed", u)
                        dve.tensor_tensor(res[:, par], hc, skip, ALU.add).then_inc(sems["k_res"], 1)
                    elif name in ("g_var", "f_var"):
                        done(dve, name[0] + "_rstd", u)
                        dve.tensor_tensor(yn, ps[:, 6, 0:S2], rs3, ALU.mult).then_inc(sems[name[0] + "_normed"], 1)
                    elif name == "conv":
                        done(dve, "xz_out", u)
                        conv(u)
                    elif name == "z2":
                        done(dve, "z_ln", u)
                        dve.scalar_tensor_tensor(lz, zz, 0.0, lz, ALU.min, ALU.subtract).then_inc(sems["z_arg"], 1)
                    elif name == "z3":
                        done(dve, "z_sig", u)
                        dve.tensor_tensor(zg[:, par], zz, lz, ALU.mult).then_inc(sems["z_out"], 1)
                    elif name in ("su2", "sd2"):
                        pre = name[:2]
                        done(dve, pre + "_one", u)
                        done(dve, pre + "_ln", u)
                        dve.scalar_tensor_tensor(op, op, -1.0, ex, ALU.add, ALU.subtract).then_inc(sems[pre + "_err"], 1)
                    elif name in ("su3", "sd3"):
                        pre = name[:2]
                        done(dve, pre + "_cor", u)
                        if pre == "su":
                            done(dve, "m_sum", shift(u, -2), 0)
                            dst = uu[:, par]
                        else:
                            done(dve, "m_decay", shift(u, -2), NS - 1)
                            dst = delta[:, par]
                        dve.scalar_tensor_tensor(flat(dst), flat(cv), 0.0, lg, ALU.max, ALU.add).then_inc(sems[pre + "_out"], 1)
                    elif name == "gate":
                        done(dve, "m_sum", u, NS - 1)
                        dve.tensor_tensor(h1, ps[:, 4 + par, 0:S2], zg[:, par], ALU.mult).then_inc(sems["f_gated"], 1)
                        done(dve, "f_gated", u)
                        dve.tensor_tensor(h1, h1, res[:, par], ALU.add).then_inc(sems["f_added"], 1)
                    elif name == "f_2":
                        done(dve, "f_mm2", u)
                        dve.scalar_tensor_tensor(fo, ps[:, 7, 0:S2], mvec[:, B2:B2 + 1], h1, ALU.add, ALU.add).then_inc(sems["f_out"], 1)

                def step(u, n):
                    done(dve, "m_inp", u, n)
                    done(dve, "m_decay", u, n)
                    dve.tensor_tensor_scan(flat(state[:, n % 2]), flat(decay[:, n % 2]), flat(inp[:, n % 2]), 0.0,
                                           ALU.mult, ALU.add).then_inc(sems["m_scan"], 1)
                    done(dve, "m_scan", u, n)
                    done(dve, "m_c", u, n)
                    done(dve, "m_sum", u, n - 2)
                    dve.tensor_tensor(prod[:, n % 2], state[:, n % 2], ps[:, 2:4, 0:S2], ALU.mult).then_inc(sems["m_prod"], 1)

                def chain_only(u, what):
                    for name in (PRE if what == "pre" else POST):
                        chain(name, u)

                def rnd(u, pre, post):
                    for name, n in ticks3(pre, post):
                        if name == "step":
                            step(u, n)
                        elif name in PRE:
                            chain(name, shift(u, 1))
                        elif name in POST:
                            chain(name, shift(u, -1))

                fusion(dve, rnd, chain_only)


_INS = ["x", "txt", "L0_tok_conv_w", "L0_tok_conv_b", "L0_tok_cls_token", "L0_tok_pos_embed", "L0_tok_ln1_w",
        "L0_tok_ln1_b", "L0_tok_qkv_w", "L0_tok_qkv_b", "L0_tok_proj_w", "L0_tok_proj_b", "L0_tok_ln2_w",
        "L0_tok_ln2_b", "L0_tok_fc1_w", "L0_tok_fc1_b", "L0_tok_fc2_w", "L0_tok_fc2_b", "L0_tok_norm_w",
        "L0_tok_norm_b", "L0_attn_ln_g", "L0_attn_ln_b", "L0_attn_W_proj", "L0_attn_conv_w", "L0_attn_conv_b",
        "L0_attn_W_x", "L0_attn_W_dt", "L0_attn_b_dt", "L0_attn_A_log", "L0_attn_D", "L0_ffn_W1", "L0_ffn_b1",
        "L0_ffn_W2", "L0_ffn_b2"]


def kernel(**inputs):
    import numpy as _np
    import concourse.bacc as _bacc
    from concourse.bass_utils import run_bass_kernel_spmd as _run

    nc = _bacc.Bacc("TRN2", target_bir_lowering=False, num_devices=1)
    arrays, args = {}, []
    for name in _INS:
        a = _np.ascontiguousarray(inputs[name])
        arrays[f"in_{name}"] = a
        args.append(nc.dram_tensor(f"in_{name}", a.shape, mybir.dt.from_np(a.dtype), kind="ExternalInput").ap())
    b, tokens, dim = inputs["x"].shape[0], inputs["L0_tok_pos_embed"].shape[1], inputs["L0_tok_conv_w"].shape[1]
    out = nc.dram_tensor("out_0", (b, tokens + inputs["txt"].shape[1], dim), F32, kind="ExternalOutput").ap()
    scratch = nc.dram_tensor("scratch", (2, 3, 2, dim, 2 * tokens), BF16, kind="Internal").ap()
    early_fusion(nc, *args, out, scratch)
    r = _run(nc, [arrays], core_ids=[0])
    return r.results[0]["out_0"]
```

```python
from contextlib import ExitStack
from functools import partial

import concourse.bass as bass
from concourse import mybir

F32 = mybir.dt.float32
BF16 = mybir.dt.bfloat16
ACT = mybir.ActivationFunctionType
ALU = mybir.AluOpType
AX = mybir.AxisListType

P = 128
ARENA = 35960
CREDIT = 3


def shift(u, d):
    q, par, lq = u
    n = par + d
    return (q + n // 2, n % 2, lq + n // 2)


def V(u, k=1, j=0):
    q, par = u[:2]
    return q * (2 * k) + ((par + CREDIT) * k + j + 1)


def VD(u, n):
    return u[0] * (16 * n) + 16 * n


def early_fusion(nc, x, txt, conv_w, conv_b, cls_token, pos_embed, ln1_w, ln1_b, qkv_w, qkv_b,
                 proj_w, proj_b, ln2_w, ln2_b, fc1_w, fc1_b, fc2_w, fc2_b, norm_w, norm_b,
                 m_ln_g, m_ln_b, m_W_proj, m_conv_w, m_conv_b, m_W_x, m_W_dt, m_b_dt, m_A_log, m_D,
                 f_W1, f_b1, f_W2, f_b2, out, scratch, debug=None):
    B, CH, IMG, _ = x.shape
    D = conv_w.shape[1]
    DEPTH = ln1_w.shape[0]
    NT = pos_embed.shape[1]
    PS = 16
    G = IMG // PS
    NP = G * G
    HEADS, HD = 8, D // 8
    HG = 4
    T2 = 2 * NT
    UNITS = B // 2
    PAIRS = UNITS // 2
    TXT = txt.shape[1]
    S = NT + TXT
    S2 = 2 * S
    NS = m_A_log.shape[1]
    RANK = m_W_dt.shape[0]
    TAPS = m_conv_w.shape[2]
    EPS = 1e-5
    KT = (P, NT - P)
    SCALE = HD ** -0.5

    with ExitStack() as ctx:
        def sb(name, shape, dt=F32):
            return ctx.enter_context(nc.sbuf_tensor(name, shape, dt))

        sems = {}

        def sem(name):
            if name not in sems:
                sems[name] = ctx.enter_context(nc.semaphore(name))
            return sems[name]

        def passed(eng):
            eng.sem_inc(sem("s_passed"), 1)

        ps = ctx.enter_context(nc.psum_tensor("ps", [P, 8, 512], F32))

        ident = sb("ident", [P, P])
        identb = sb("identb", [P, P], BF16)
        center = sb("center", [P, P])
        mean = sb("mean", [P, P])
        e0 = sb("e0", [P, 1])
        eps_col = sb("eps_col", [P, 1])
        one_col = sb("one_col", [P, 1])
        h = sb("h", [P, B * NT])
        arena = sb("arena", [P, ARENA])
        h3 = h[:, :].rearrange("p (b n) -> p b n", n=NT)

        at = [0]

        def carve(*dims, dt=F32):
            n = 1
            for d_ in dims:
                n *= d_
            words = n if dt == F32 else (n + 1) // 2
            a = arena[:, at[0]:at[0] + words]
            at[0] += words
            assert at[0] <= ARENA, at[0]
            if dt != F32:
                a = a.bitcast(dt)
            if len(dims) == 2:
                a = a.rearrange("p (a b) -> p a b", b=dims[1])
            elif len(dims) == 3:
                a = a.rearrange("p (a b c) -> p a b c", b=dims[1], c=dims[2])
            elif len(dims) == 4:
                a = a.rearrange("p (a b c d) -> p a b c d", b=dims[1], c=dims[2], d=dims[3])
            return a

        def hu(u):
            _, par, lq = u
            return h[:, bass.ds(lq * (2 * T2) + par * T2, T2)]

        XW = G * IMG
        patches = carve(2, 2, XW)
        wconv = carve(8, D)
        pos_rows = carve(2, D)
        posb = carve(NT)
        cls_col = carve(1)
        convb_col = carve(1)
        s_const = sem("s_const")
        s_init = sem("s_init")
        s_wl = sem("s_wl")
        s_xl = [sem("s_xl0"), sem("s_xl1")]
        s_posT = sem("s_posT")
        s_pose = sem("s_pose")
        s_emb = sem("s_emb")
        s_hemb = sem("s_hemb")
        NXL = 2 * 2 * CH

        with nc.Block() as block:
            @block.gpsimd
            def _(pool):
                pool.memset(ident[:, :], 0.0).then_inc(s_const, 1)
                pool.memset(identb[:, :], 0.0).then_inc(s_const, 1)
                pool.memset(center[:, :], -1.0 / D).then_inc(s_const, 1)
                pool.memset(mean[:, :], 1.0 / D).then_inc(s_const, 1)
                pool.memset(e0[:, :], 0.0).then_inc(s_const, 1)
                pool.memset(eps_col[:, :], EPS).then_inc(s_const, 1)
                pool.memset(one_col[:, :], 1.0).then_inc(s_const, 1)
                pool.wait_ge(s_const, 7)
                for m, v in ((ident, 1.0), (identb, 1.0), (center, 1.0 - 1.0 / D)):
                    pool.affine_select(out=m[:, :], in_=m[:, :], compare_op=ALU.not_equal, fill=v, base=0,
                                       pattern=[[-1, P]], channel_multiplier=1).then_inc(s_init, 1)
                pool.affine_select(out=e0[:, :], in_=e0[:, :], compare_op=ALU.not_equal, fill=1.0, base=0,
                                   pattern=[[0, 1]], channel_multiplier=1).then_inc(s_init, 1)

            @block.sync
            def _(sp):
                for half in range(2):
                    for c in range(CH):
                        r = (half * CH + c) * PS
                        src = conv_w.rearrange("(c i f j) n -> f c i j n", c=CH, i=PS, f=2)[half, c]
                        sp.dma_start(wconv[r:r + PS], src).then_inc(s_wl, 16)
                sp.dma_start(pos_rows[:, 0, :], pos_embed[0, 0:P, :]).then_inc(s_wl, 16)
                sp.dma_start(pos_rows[0:NT - P, 1, :], pos_embed[0, P:NT, :]).then_inc(s_wl, 16)
                sp.dma_start(cls_col, cls_token[0].rearrange("a d -> d a")).then_inc(s_wl, 16)
                sp.dma_start(convb_col, conv_b.rearrange("(d a) -> d a", a=1)).then_inc(s_wl, 16)

                def load(u):
                    q, par = u
                    for half in range(2):
                        for c in range(CH):
                            for b in range(2):
                                r = (half * CH + c) * PS
                                src = x[bass.ds(q * 4 + (par * 2 + b), 1), c].rearrange(
                                    "b (g i) w -> i (b g) w", i=PS)[:, :, 8 * half:]
                                dst = patches[r:r + PS, par, b].rearrange(
                                    "p (g w) -> p g w", w=IMG)[:, :, 0:IMG - 8 * half]
                                sp.dma_start(dst, src).then_inc(s_xl[par], 16)
                load((0, 0))
                load((0, 1))
                with sp.Fori(1, PAIRS) as q:
                    for par in range(2):
                        sp.wait_ge(s_emb, q * 2 + (par - 1))
                        passed(sp)
                        load((q, par))

            @block.tensor
            def _(pe):
                pe.wait_ge(s_init, 4)
                pe.wait_ge(s_wl, 16 * 10)
                pe.transpose(ps[:, 0, 0:P], pos_rows[:, 0, :], ident[:, :])
                pe.transpose(ps[:, 0, P:NT], pos_rows[0:NT - P, 1, :], ident[0:NT - P, 0:NT - P]).then_inc(s_posT, 1)
                with pe.Fori(0, PAIRS) as q:
                    for par in range(2):
                        pe.wait_ge(s_xl[par], VD((q, par), NXL))
                        pe.wait_ge(s_hemb, q * 2 + par)
                        for j in range(8):
                            last = pe.matmul(ps[:, 2 + par, 0:2 * NP], wconv[0:96, j, :],
                                             patches[0:96, par, :, bass.ds(j, NP, step=PS)],
                                             start=(j == 0), stop=(j == 7))
                        last.then_inc(s_emb, 1)

            @block.vector
            def _(dve):
                dve.wait_ge(s_posT, 1)
                dve.tensor_scalar(posb[:, 1:NT], ps[:, 0, 1:NT], convb_col, None, ALU.add).then_inc(s_pose, 1)
                dve.tensor_scalar(h3[:, :, 0:1], cls_col.rearrange("p (a b) -> p a b", b=1).broadcast_to((P, B, 1)),
                                  ps[:, 0, 0:1], None, ALU.add).then_inc(s_hemb, 1)
                dve.wait_ge(s_pose, 1)
                with dve.Fori(0, PAIRS) as q:
                    for par in range(2):
                        dve.wait_ge(s_emb, q * 2 + (par + 1))
                        dst = h[:, bass.ds(q * (2 * T2) + par * T2, T2)].rearrange("p (b n) -> p b n", n=NT)
                        dve.tensor_tensor(dst[:, :, 1:NT],
                                          ps[:, 2 + par, 0:2 * NP].rearrange("p (b n) -> p b n", n=NP),
                                          posb[:, 1:NT].rearrange("p (a n) -> p a n", a=1).broadcast_to((P, 2, NP)),
                                          ALU.add).then_inc(s_hemb, 1)
        if debug == "embed":
            s_dbg = sem("s_dbg")
            with nc.Block() as block:
                @block.sync
                def _(sp):
                    sp.dma_start(out, h[:, :]).then_inc(s_dbg, 16)
                    sp.wait_ge(s_dbg, 16)
            return

        at[0] = 0
        stack = carve(2, 2, HEADS * T2, dt=BF16)
        vaug = carve(2, 2 * 2 * HEADS * 2 * HD)
        probs = carve(2, 2, HG, NT)
        onorm = carve(2, 2, T2)
        sums = carve(2, NT)
        rsum = carve(2, NT)
        negmax = carve(2, 2, HG)
        negres = carve(2, 2, HG)
        mparts = carve(2, 2, 32, dt=BF16)
        mrows = carve(2, NT + 1, dt=BF16)
        sq, rs, y = carve(T2), carve(T2), carve(T2)
        qk32 = carve(2, T2)
        res32 = carve(2, T2)
        parts = carve(3, 2, T2, dt=BF16)
        act = carve(2, T2)
        wqkv_raw = carve(3 * D)
        wqk_perm = carve(2, D)
        bqkv_row = carve(3 * D)
        bqk_perm = carve(2, D)
        wq_f, wk_f, wv_f = carve(D), carve(D), carve(D)
        wproj_pad = carve(2, D)
        wproj_raw = carve(D)
        wfc1_raw = carve(2 * D)
        wfc1_f = carve(2 * D)
        wfc2 = carve(2, D)
        vecs = carve(8)
        bias = carve(8)
        msel = carve(HG, P, dt=BF16)
        L1W, L1B, L2W, L2B, PB, F2B, F1B = 0, 1, 2, 3, 4, 5, 6
        QB, KB, VB, HB, OB = 0, 1, 2, 3, 5
        Q_TERMS = (0, 0, 0, 1, 1, 2)
        K_TERMS = (0, 1, 2, 0, 1, 0)
        NLD = 2 * len(Q_TERMS)
        KROWS = HD * len(Q_TERMS)
        NWL = 4 + 1 + 1 + 1 + 1 + 1 + 1 + 6 + 2

        vau = [vaug[:, p_, :].rearrange("p (b t h c) -> p b t h c", b=2, t=2, h=HEADS) for p_ in range(2)]

        for n_ in ("p_centered p_squared p_vared p_logged p_rstd p_normed p_qk_mm p_v_mm p_qk_out p_v_out "
                   "p_hi p_res p_mid p_lo t_projected t_added t_centered t_squared t_vared t_logged t_rstd "
                   "t_normed t_fc1 t_gelu t_fc2 t_done").split():
            sem(n_)
        for n_ in "a_scores a_max a_hi a_res a_mid a_lo a_mT a_mrows a_keys a_exp a_pv a_sums a_logsum a_rsum a_out".split():
            sem(n_)
        STEPS = 4
        PER = {"a_scores": 8, "a_max": 8, "a_keys": 8, "a_exp": 8}
        W = {n_: PER.get(n_, STEPS) if n_[:2] == "a_" else 1 for n_ in sems if n_[:2] in ("p_", "t_", "a_")}

        def credit(eng, names):
            for n_ in names.split():
                eng.sem_inc(sems[n_], CREDIT * W[n_])

        def done(eng, name, u, j=0):
            eng.wait_ge(sems[name], V(u, W[name], j))

        s_stacked = [sem("s_stacked0"), sem("s_stacked1")]
        s_wld = sem("s_wld")
        s_fold = sem("s_fold")
        s_bmm = sem("s_bmm")
        s_bias = sem("s_bias")
        s_zero = sem("s_zero")
        s_ones = sem("s_ones")
        s_sel = sem("s_sel")
        FOLDS, BMMS, BIASES = 8, 2, 4

        def ticks(prep, tail):
            chain = (["p_center", "p_var", "p_qk", "p_v"] if prep else []) + (
                ["t_proj", "t_center", "t_var", "t_fc1", "t_fc2"] if tail else [])

            def link(i=STEPS):
                if chain and (prep or i > 0):
                    yield chain.pop(0), 0, 0, 0

            for i in range(STEPS):
                ahead = (0, i + 1) if i + 1 < STEPS else (1, 0) if prep else None
                behind = (0, i - 1) if i > 0 else (-1, STEPS - 1) if tail else None
                normed = (0, i - 2) if i > 1 else (-1, STEPS - 2 + i) if tail else None
                if ahead:
                    yield "scores", *ahead, 0
                yield "keys", 0, i, 0
                if normed:
                    yield "norm", *normed, 0
                yield from link(i)
                if ahead:
                    yield "scores", *ahead, 1
                    yield "max", *ahead, 0
                yield "keys", 0, i, 1
                yield from link(i)
                if i % 2 == 1:
                    yield from link()
                if ahead:
                    yield "mrow", *ahead, 0
                if behind:
                    yield "values", *behind, 0
            yield from ((c, 0, 0, 0) for c in chain)

        def begin():
            yield "scores", 0, 0, 0
            yield "scores", 0, 0, 1
            yield "max", 0, 0, 0
            yield "mrow", 0, 0, 0

        def layers(eng, fold, rnd, chain_only, run=lambda u, steps: None, at_block=lambda: None):
            with eng.Fori(0, DEPTH) as L:
                base = L * PAIRS
                fold(L)
                first, last = (base, 0, 0), (base + (PAIRS - 1), 1, PAIRS - 1)
                chain_only(first, "prep")
                run(first, begin())
                rnd(first, prep=True, tail=False)
                with eng.Fori(0, PAIRS - 1) as it:
                    at_block()
                    rnd((base + it, 1, it), prep=True, tail=True)
                    rnd((base + it + 1, 0, it + 1), prep=True, tail=True)
                at_block()
                rnd(last, prep=False, tail=True)
                run(last, (("norm", 0, STEPS - 2, 0), ("values", 0, STEPS - 1, 0), ("norm", 0, STEPS - 1, 0)))
                chain_only(last, "tail")

        PREP = ("p_center", "p_var", "p_qk", "p_v")
        TAIL = ("t_proj", "t_center", "t_var", "t_fc1", "t_fc2")

        with nc.Block() as block:
            @block.sync
            def _(sp):
                def fold(L):
                    sp.wait_ge(s_zero, 5)
                    done(sp, "t_done", (L * PAIRS - 1, 1, 0))
                    pw = proj_w[bass.ds(L, 1)].rearrange("a (g i d) n -> (a i) d g n", g=2, i=HG)
                    for i in range(HG):
                        sp.dma_start(wproj_pad[32 * i:32 * i + HD], pw[i]).then_inc(s_wld, 16)
                    sp.dma_start(wqkv_raw, qkv_w[bass.ds(L, 1)].rearrange("a k n -> (a k) n")).then_inc(s_wld, 16)
                    sp.dma_start(bqkv_row[0:1], qkv_b[bass.ds(L, 1)]).then_inc(s_wld, 16)
                    sp.dma_start(wproj_raw, proj_w[bass.ds(L, 1)].rearrange("a k n -> (a k) n")).then_inc(s_wld, 16)
                    sp.dma_start(wfc1_raw, fc1_w[bass.ds(L, 1)].rearrange("a k n -> (a k) n")).then_inc(s_wld, 16)
                    f2 = fc2_w[bass.ds(L, 1)].rearrange("a (c k) n -> (a c) k n", c=2)
                    for c in range(2):
                        sp.dma_start(wfc2[:, c, :], f2[c]).then_inc(s_wld, 16)
                    for col, v in ((L1W, ln1_w), (L1B, ln1_b), (L2W, ln2_w), (L2B, ln2_b), (PB, proj_b), (F2B, fc2_b)):
                        sp.dma_start(vecs[:, col:col + 1], v[bass.ds(L, 1)].rearrange("a d -> d a")).then_inc(s_wld, 16)
                    f1b = fc1_b[bass.ds(L, 1)].rearrange("a (c d) -> c d a", c=2)
                    for c in range(2):
                        sp.dma_start(vecs[:, F1B + c:F1B + c + 1], f1b[c]).then_inc(s_wld, 16)

                def move(u):
                    par = u[1]
                    for part, name in enumerate(("p_hi", "p_mid", "p_lo")):
                        done(sp, name, u)
                        passed(sp)
                        if part == 0:
                            done(sp, "a_keys", shift(u, -2), 7)
                            passed(sp)
                        for side, terms in ((0, Q_TERMS), (1, K_TERMS)):
                            for t in range(len(terms)):
                                if terms[t] == part:
                                    dst = stack[t * HD:(t + 1) * HD, par, side, :].rearrange("d (h n) -> d h n", h=HEADS)
                                    sp.dma_start(dst, parts[:, part, side, :]).then_inc(s_stacked[par], 16)

                def chain_only(u, what):
                    if what == "prep":
                        move(u)

                def rnd(u, prep, tail):
                    if prep:
                        move(shift(u, 1))

                layers(sp, fold, rnd, chain_only)
                sp.wait_ge(s_stacked[0], VD((DEPTH * PAIRS - 1, 0, 0), NLD))
                sp.wait_ge(s_stacked[1], VD((DEPTH * PAIRS - 1, 1, 0), NLD))

            @block.gpsimd
            def _(pool):
                credit(pool, "p_hi p_res p_mid p_lo")
                pool.memset(vaug, 1.0).then_inc(s_ones, 1)
                pool.memset(msel, 0.0).then_inc(s_sel, 1)
                pool.wait_ge(s_sel, 1)
                for part in range(3):
                    pool.affine_select(out=msel, in_=msel, compare_op=ALU.not_equal, fill=1.0,
                                       base=-HG * part, pattern=[[-1, HG], [0, P]],
                                       channel_multiplier=1).then_inc(s_sel, 1)
                    pool.wait_ge(s_sel, part + 2)

                def split(u):
                    par = u[1]
                    done(pool, "p_qk_out", u)
                    pu = shift(u, -1)
                    pool.wait_ge(s_stacked[pu[1]], VD(pu, NLD))
                    passed(pool)
                    pool.tensor_scalar(parts[:, 0], qk32, 1.0, 0.0, ALU.mult, ALU.add).then_inc(sems["p_hi"], 1)
                    done(pool, "p_hi", u)
                    pool.tensor_tensor(res32, qk32, parts[:, 0], ALU.subtract).then_inc(sems["p_res"], 1)
                    done(pool, "p_res", u)
                    passed(pool)
                    pool.tensor_scalar(parts[:, 1], res32, 1.0, 0.0, ALU.mult, ALU.add).then_inc(sems["p_mid"], 1)
                    done(pool, "p_mid", u)
                    pool.tensor_tensor(parts[:, 2], res32, parts[:, 1], ALU.subtract).then_inc(sems["p_lo"], 1)

                def chain_only(u, what):
                    if what == "prep":
                        split(u)

                def rnd(u, prep, tail):
                    if prep:
                        split(shift(u, 1))

                layers(pool, lambda L: None, rnd, chain_only)

            @block.tensor
            def _(pe):
                credit(pe, "p_centered p_vared p_qk_mm p_v_mm t_projected t_centered t_vared t_fc1 t_fc2 "
                           "a_scores a_mT a_keys a_pv")
                pe.wait_ge(s_sel, 4)
                pe.wait_ge(s_ones, 1)
                pe.wait_ge(s_zero, 5)

                def fold(L):
                    pe.wait_ge(s_fold, L * FOLDS + FOLDS)
                    for col, w, b, ln in ((QB, wqk_perm[:, 0], bqk_perm[:, 0], L1B), (KB, wqk_perm[:, 1], bqk_perm[:, 1], L1B),
                                          (VB, wqkv_raw[:, 2 * D:3 * D], bqkv_row[:, 2 * D:3 * D], L1B),
                                          (HB, wfc1_raw[:, 0:D], None, L2B), (HB + 1, wfc1_raw[:, D:2 * D], None, L2B)):
                        last = pe.matmul(ps[:, 5, col:col + 1], w, vecs[:, ln:ln + 1], start=True, stop=b is None)
                        if b is not None:
                            last = pe.matmul(ps[:, 5, col:col + 1], b, e0[:, :], start=False, stop=True)
                    last.then_inc(s_bmm, 1)
                    pe.wait_ge(s_bias, L * BIASES + 3)
                    pe.matmul(ps[:, 6, 0:1], wproj_raw, bias[:, VB:VB + 1], start=True, stop=True).then_inc(s_bmm, 1)

                def chain(name, u, after):
                    par = u[1]
                    if name == "p_center":
                        done(pe, "t_done", shift(u, -3))
                        done(pe, "p_qk_out", shift(u, -1))
                        done(pe, "p_v_out", shift(u, -1))
                        if after is not None:
                            done(pe, "t_done", after)
                        pe.matmul(ps[:, 5, 0:T2], center[:, :], hu(u), start=True, stop=True).then_inc(sems["p_centered"], 1)
                    elif name == "p_var":
                        done(pe, "p_squared", u)
                        pe.matmul(ps[:, 6, 0:T2], mean[:, :], sq, start=True, stop=True).then_inc(sems["p_vared"], 1)
                    elif name == "p_qk":
                        done(pe, "p_normed", u)
                        pe.matmul(ps[:, 5, 0:T2], wq_f, y, start=True, stop=True)
                        pe.matmul(ps[:, 6, 0:T2], wk_f, y, start=True, stop=True).then_inc(sems["p_qk_mm"], 1)
                    elif name == "p_v":
                        done(pe, "p_qk_out", u)
                        for b in range(2):
                            for t in range(2):
                                last = pe.matmul(ps[0:KT[t], 5, (2 * b + t) * D:(2 * b + t + 1) * D],
                                                 y[:, b * NT + t * P:b * NT + t * P + KT[t]], wv_f, start=True, stop=True)
                        last.then_inc(sems["p_v_mm"], 1)
                    elif name == "t_proj":
                        done(pe, "p_v_out", after)
                        done(pe, "p_qk_out", after)
                        done(pe, "t_done", shift(u, -1))
                        done(pe, "a_out", u, STEPS - 1)
                        for g in range(2):
                            last = pe.matmul(ps[:, 5, 0:T2], wproj_pad[:, g, :], onorm[:, par, g, :], start=(g == 0), stop=(g == 1))
                        last.then_inc(sems["t_projected"], 1)
                    elif name == "t_center":
                        done(pe, "t_added", u)
                        pe.matmul(ps[:, 5, 0:T2], center[:, :], hu(u), start=True, stop=True).then_inc(sems["t_centered"], 1)
                    elif name == "t_var":
                        done(pe, "t_squared", u)
                        pe.matmul(ps[:, 6, 0:T2], mean[:, :], sq, start=True, stop=True).then_inc(sems["t_vared"], 1)
                    elif name == "t_fc1":
                        done(pe, "t_normed", u)
                        for c in range(2):
                            last = pe.matmul(ps[:, 5 + c, 0:T2], wfc1_f[:, c * D:(c + 1) * D], y, start=True, stop=True)
                        last.then_inc(sems["t_fc1"], 1)
                    elif name == "t_fc2":
                        done(pe, "t_gelu", u)
                        for c in range(2):
                            last = pe.matmul(ps[:, 5, 0:T2], wfc2[:, c, :], act[:, c, :], start=(c == 0), stop=(c == 1))
                        last.then_inc(sems["t_fc2"], 1)

                def attend(name, u, i, t):
                    par = u[1]
                    b, g = divmod(i, 2)
                    ap = i % 2
                    qs = stack[0:KROWS, par, 0, :].rearrange("p (h n) -> p h n", h=HEADS)
                    ks = stack[0:KROWS, par, 1, :].rearrange("p (h n) -> p h n", h=HEADS)
                    if name == "scores":
                        if i == 0 and t == 0:
                            pe.wait_ge(s_stacked[par], VD(u, NLD))
                        done(pe, "a_max", u, 2 * i + t - 1)
                        for hh in range(HG):
                            last = pe.matmul(ps[0:KT[t], hh // 2, (hh % 2) * NT:(hh % 2 + 1) * NT],
                                             qs[:, HG * g + hh, b * NT + t * P:b * NT + t * P + KT[t]],
                                             ks[:, HG * g + hh, b * NT:(b + 1) * NT], start=True, stop=True)
                        last.then_inc(sems["a_scores"], 1)
                    elif name == "mrow":
                        done(pe, "a_lo", u, i)
                        done(pe, "a_mrows", u, i - 1)
                        for tt in range(2):
                            last = pe.matmul(ps[0:32, 7, tt * P:tt * P + KT[tt]], mparts[0:KT[tt], ap, tt, :],
                                             identb[0:KT[tt], 0:KT[tt]], start=True, stop=True)
                        last.then_inc(sems["a_mT"], 1)
                    elif name == "keys":
                        if t == 0:
                            done(pe, "a_mrows", u, i)
                        done(pe, "a_exp", u, 2 * i + t - 1)
                        for hh in range(HG):
                            o = ps[0:KT[t], 2 + hh // 2, (hh % 2) * NT:(hh % 2 + 1) * NT]
                            pe.matmul(o, ks[:, HG * g + hh, b * NT + t * P:b * NT + t * P + KT[t]],
                                      qs[:, HG * g + hh, b * NT:(b + 1) * NT], start=True, stop=False)
                            last = pe.matmul(o, msel[:, hh, 0:KT[t]], mrows[:, ap, 0:NT], start=False, stop=True)
                        last.then_inc(sems["a_keys"], 1)
                    elif name == "values":
                        done(pe, "a_exp", u, 2 * i + 1)
                        done(pe, "a_out", u, i - 1)
                        for t_ in range(2):
                            for hh in range(HG):
                                last = pe.matmul(ps[32 * hh:32 * hh + 32, 4, 0:NT], vau[par][0:KT[t_], b, t_, HG * g + hh, :],
                                                 probs[0:KT[t_], ap, t_, hh, :], start=(t_ == 0), stop=(t_ == 1))
                        last.then_inc(sems["a_pv"], 1)

                def chain_only(u, what):
                    for name in (PREP if what == "prep" else TAIL):
                        chain(name, u, shift(u, -1) if what == "prep" else u)

                def run(u, steps):
                    for name, d, i, t in steps:
                        attend(name, shift(u, d), i, t)

                def rnd(u, prep, tail):
                    for name, d, i, t in ticks(prep, tail):
                        if name in PREP:
                            chain(name, shift(u, 1), None)
                        elif name in TAIL:
                            chain(name, shift(u, -1), shift(u, 1) if prep else u)
                        else:
                            attend(name, shift(u, d), i, t)

                layers(pe, fold, rnd, chain_only, run)

            @block.scalar
            def _(sc):
                credit(sc, "p_squared p_logged p_rstd p_qk_out t_squared t_logged t_rstd t_gelu "
                           "a_exp a_logsum a_rsum")

                def fold(L):
                    exp_ln_tables()
                    sc.wait_ge(s_bias, L * BIASES + BIASES)

                def exp_ln_tables():
                    sc.preload_act_table_set("natural_log_exp_and_others")

                def rstd(pre, u):
                    done(sc, pre + "_vared", u)
                    sc.activation(rs, ps[:, 6, 0:T2], ACT.Ln, bias=eps_col[:, :]).then_inc(sems[pre + "_logged"], 1)
                    done(sc, pre + "_logged", u)
                    sc.activation(rs, rs, ACT.Exp, scale=-0.5).then_inc(sems[pre + "_rstd"], 1)

                def chain(name, u):
                    if name == "p_center" or name == "t_center":
                        pre = name[0]
                        done(sc, pre + "_centered", u)
                        sc.activation(sq, ps[:, 5, 0:T2], ACT.Square).then_inc(sems[pre + "_squared"], 1)
                    elif name == "p_var" or name == "t_var":
                        rstd(name[0], u)
                    elif name == "p_qk":
                        done(sc, "p_qk_mm", u)
                        done(sc, "p_lo", shift(u, -1))
                        sc.activation(qk32[:, 0, :], ps[:, 5, 0:T2], ACT.Identity, bias=bias[:, QB:QB + 1], scale=SCALE)
                        sc.activation(qk32[:, 1, :], ps[:, 6, 0:T2], ACT.Identity, bias=bias[:, KB:KB + 1]).then_inc(sems["p_qk_out"], 1)
                    elif name == "t_fc1":
                        done(sc, "t_fc1", u)
                        sc.activation(act[:, 0, :], ps[:, 5, 0:T2], ACT.Gelu, bias=bias[:, HB:HB + 1])
                        sc.activation(act[:, 1, :], ps[:, 6, 0:T2], ACT.Gelu, bias=bias[:, HB + 1:HB + 2]).then_inc(sems["t_gelu"], 1)
                        exp_ln_tables()

                def attend(name, u, i, t):
                    ap = i % 2
                    if name == "keys":
                        done(sc, "a_keys", u, 2 * i + t)
                        done(sc, "a_pv", u, i - 2)
                        sc.activation(probs[0:KT[t], ap, t].rearrange("p (a b) n -> p a (b n)", a=2),
                                      ps[0:KT[t], 2:4, 0:2 * NT], ACT.Exp).then_inc(sems["a_exp"], 1)
                    elif name == "values":
                        done(sc, "a_sums", u, i)
                        done(sc, "a_out", u, i - 2)
                        sc.activation(rsum[:, ap], sums[:, ap], ACT.Ln).then_inc(sems["a_logsum"], 1)
                        done(sc, "a_logsum", u, i)
                        sc.activation(rsum[:, ap], rsum[:, ap], ACT.Exp, scale=-1.0).then_inc(sems["a_rsum"], 1)

                def chain_only(u, what):
                    for name in (PREP if what == "prep" else TAIL):
                        chain(name, u)

                def run(u, steps):
                    for name, d, i, t in steps:
                        attend(name, shift(u, d), i, t)

                def rnd(u, prep, tail):
                    for name, d, i, t in ticks(prep, tail):
                        if name in PREP:
                            chain(name, shift(u, 1))
                        elif name in TAIL:
                            chain(name, shift(u, -1))
                        else:
                            attend(name, shift(u, d), i, t)

                layers(sc, fold, rnd, chain_only, run, exp_ln_tables)

            @block.vector
            def _(dve):
                credit(dve, "p_normed p_v_out t_added t_normed t_done a_max a_hi a_res a_mid a_lo a_mrows a_sums a_out")
                for z in (negmax, mparts, mrows):
                    dve.memset(z, 0.0).then_inc(s_zero, 1)
                dve.memset(wproj_pad, 0.0).then_inc(s_zero, 1)
                dve.memset(bqkv_row, 0.0).then_inc(s_zero, 1)

                def fold(L):
                    dve.wait_ge(s_wld, L * (16 * NWL) + 16 * NWL)
                    for s_ in range(2):
                        dve.tensor_copy(wqk_perm[:, s_].rearrange("p (d h) -> p d h", h=HEADS),
                                        wqkv_raw[:, s_ * D:(s_ + 1) * D].rearrange("p (h d) -> p d h", h=HEADS)).then_inc(s_fold, 1)
                        dve.tensor_copy(bqk_perm[:, s_].rearrange("p (d h) -> p d h", h=HEADS),
                                        bqkv_row[:, s_ * D:(s_ + 1) * D].rearrange("p (h d) -> p d h", h=HEADS)).then_inc(s_fold, 1)
                    dve.wait_ge(s_fold, L * FOLDS + 4)
                    for dst, src, ln in ((wq_f, wqk_perm[:, 0], L1W), (wk_f, wqk_perm[:, 1], L1W),
                                         (wv_f, wqkv_raw[:, 2 * D:3 * D], L1W), (wfc1_f, wfc1_raw, L2W)):
                        dve.tensor_scalar(dst, src, vecs[:, ln:ln + 1], None, ALU.mult).then_inc(s_fold, 1)
                    dve.wait_ge(s_bmm, L * BMMS + 1)
                    dve.tensor_scalar(bias[:, QB:QB + 1], ps[:, 5, QB:QB + 1], SCALE, None, ALU.mult).then_inc(s_bias, 1)
                    dve.tensor_copy(bias[:, KB:VB + 1], ps[:, 5, KB:VB + 1]).then_inc(s_bias, 1)
                    dve.tensor_tensor(bias[:, HB:HB + 2], ps[:, 5, HB:HB + 2], vecs[:, F1B:F1B + 2], ALU.add).then_inc(s_bias, 1)
                    dve.wait_ge(s_bmm, L * BMMS + 2)
                    dve.tensor_tensor(bias[:, OB:OB + 1], ps[:, 6, 0:1], vecs[:, PB:PB + 1], ALU.add).then_inc(s_bias, 1)
                    dve.wait_ge(s_bias, L * BIASES + BIASES)

                def chain(name, u):
                    par = u[1]
                    if name == "p_var" or name == "t_var":
                        pre = name[0]
                        done(dve, pre + "_rstd", u)
                        dve.tensor_tensor(y, ps[:, 5, 0:T2], rs, ALU.mult).then_inc(sems[pre + "_normed"], 1)
                    elif name == "p_v":
                        done(dve, "p_v_mm", u)
                        done(dve, "a_pv", shift(u, -2), STEPS - 1)
                        for t in range(2):
                            src = ps[0:KT[t], 5, :].rearrange("p (b t h c) -> p b t h c", b=2, t=2, h=HEADS)[:, :, t]
                            for b in range(2):
                                last = dve.tensor_copy(vau[par][0:KT[t], b, t, :, 0:HD], src[:, b])
                        last.then_inc(sems["p_v_out"], 1)
                    elif name == "t_proj":
                        done(dve, "t_projected", u)
                        dve.scalar_tensor_tensor(hu(u), ps[:, 5, 0:T2], bias[:, OB:OB + 1], hu(u), ALU.add, ALU.add).then_inc(sems["t_added"], 1)
                    elif name == "t_fc2":
                        done(dve, "t_fc2", u)
                        dve.scalar_tensor_tensor(hu(u), ps[:, 5, 0:T2], vecs[:, F2B:F2B + 1], hu(u), ALU.add, ALU.add).then_inc(sems["t_done"], 1)

                def attend(name, u, i, t):
                    par = u[1]
                    b, g = divmod(i, 2)
                    ap = i % 2
                    mp = mparts[:, ap]
                    if name == "scores":
                        done(dve, "a_scores", u, 2 * i + t)
                        dve.tensor_reduce(negmax[0:KT[t], ap, t], ps[0:KT[t], 0:2, 0:2 * NT].rearrange(
                            "p a (b n) -> p a b n", b=2), AX.X, ALU.max, negate=True).then_inc(sems["a_max"], 1)
                    elif name == "max":
                        done(dve, "a_max", u, 2 * i + 1)
                        done(dve, "a_mT", u, i - 2)
                        dve.tensor_copy(mp[:, :, 0:HG], negmax[:, ap]).then_inc(sems["a_hi"], 1)
                        done(dve, "a_hi", u, i)
                        dve.tensor_tensor(negres[:, ap], negmax[:, ap], mp[:, :, 0:HG], ALU.subtract).then_inc(sems["a_res"], 1)
                        done(dve, "a_res", u, i)
                        dve.tensor_copy(mp[:, :, HG:2 * HG], negres[:, ap]).then_inc(sems["a_mid"], 1)
                        done(dve, "a_mid", u, i)
                        dve.tensor_tensor(mp[:, :, 2 * HG:3 * HG], negres[:, ap], mp[:, :, HG:2 * HG], ALU.subtract).then_inc(sems["a_lo"], 1)
                    elif name == "mrow":
                        done(dve, "a_mT", u, i)
                        done(dve, "a_keys", u, 2 * (i - 2) + 1)
                        dve.tensor_copy(mrows[0:32, ap, 0:NT], ps[0:32, 7, 0:NT]).then_inc(sems["a_mrows"], 1)
                    elif name == "values":
                        done(dve, "a_pv", u, i)
                        done(dve, "a_logsum", u, i - 2)
                        passed(dve)
                        dve.stream_shuffle(sums[:, ap], ps[:, 4, 0:NT], [HD + k % HD for k in range(32)]).then_inc(sems["a_sums"], 1)
                    elif name == "norm":
                        done(dve, "a_rsum", u, i)
                        done(dve, "t_projected", shift(u, -2))
                        dve.tensor_tensor(onorm[:, par, g, b * NT:(b + 1) * NT], ps[:, 4, 0:NT], rsum[:, ap], ALU.mult).then_inc(sems["a_out"], 1)

                def chain_only(u, what):
                    for name in (PREP if what == "prep" else TAIL):
                        chain(name, u)

                def run(u, steps):
                    for name, d, i, t in steps:
                        attend(name, shift(u, d), i, t)

                def rnd(u, prep, tail):
                    for name, d, i, t in ticks(prep, tail):
                        if name in PREP:
                            chain(name, shift(u, 1))
                        elif name in TAIL:
                            chain(name, shift(u, -1))
                        else:
                            attend(name, shift(u, d), i, t)

                layers(dve, fold, rnd, chain_only, run)
        if debug == "layers":
            s_dbg = sem("s_dbg")
            with nc.Block() as block:
                @block.sync
                def _(sp):
                    sp.dma_start(out, h[:, :]).then_inc(s_dbg, 16)
                    sp.wait_ge(s_dbg, 16)
            return

        at[0] = 0
        txt_rows = carve(2, D)
        hc, skip, yn = carve(S2), carve(S2), carve(S2)
        zz = carve(2, S2)
        sq3, rs3 = carve(S2), carve(S2)
        PADW = TAPS - 1
        xpad = carve(2, 2, S + 2 * PADW)
        cv = carve(2, S2)
        ex, op, lg = carve(2 * S2), carve(2 * S2), carve(2 * S2)
        lz = carve(S2)
        dbc = carve(2, S2)
        bres = carve(2, S2)
        uu = carve(2, 2, S2)
        delta = carve(2, 2, S2)
        du = carve(2, 2, S2)
        bcs = carve(2, 2, S2, dt=BF16)
        zg = carve(2, S2)
        tres = carve(UNITS, 2 * TXT)
        decay = carve(2, 2, S2)
        brep = carve(2, 2, S2)
        inp = carve(2, 2, S2)
        state = carve(2, 2, S2)
        prod = carve(2, 2, S2)
        pair = carve(2, 2, S2)
        h1 = carve(S2)
        gl = carve(S2)
        rows = carve(2 * 2, D)
        wp_raw, wp_f = carve(2 * D), carve(2 * D)
        wx_pad = carve(D)
        wdt_pad = carve(D)
        w1_raw, w2_raw, w1T, w2T = carve(D), carve(D), carve(D), carve(D)
        diagD = carve(D)
        amat = carve(NS)
        alog = carve(NS)
        mvec = carve(16)
        taps = carve(TAPS)
        bxz = carve(2)
        bsel = carve(2 * NS, P, dt=BF16)
        NW, NB, LG, LB, CB, DTB, DV, B1, B2 = range(9)

        for n_ in ("n_centered n_squared n_vared n_logged n_rstd n_scaled n_normed n_txt n_txt_out "
                   "k_centered k_squared k_vared k_logged k_rstd k_normed k_res "
                   "g_centered g_squared g_vared g_logged g_rstd g_normed xz_mm xz_out conv_step "
                   "su_abs su_exp su_one su_ln su_err su_cor su_out dbc_mm dbc_out b_hi b_res b_mid b_lo dt_mm dt_out "
                   "sd_abs sd_exp sd_one sd_ln sd_err sd_cor sd_out du_out "
                   "z_abs z_exp z_ln z_arg z_sig z_out "
                   "f_gated f_added f_centered f_squared f_vared f_logged f_rstd f_normed f_mm1 f_gelu f_mm2 f_out f_T f_rows").split():
            sem(n_)
            W[n_] = 2 * TAPS if n_ == "conv_step" else 1
        for n_ in ("dbc_mm", "dbc_out", "dt_mm", "dt_out"):
            W[n_] = 2
        for n_ in "m_b m_brep m_inp m_c m_decay m_scan m_prod m_pair m_sum".split():
            sem(n_)
            W[n_] = NS // 2 if n_ in ("m_pair", "m_sum") else NS
        s_txt = [sem("s_txt0"), sem("s_txt1")]
        s_stored = [sem("s_stored0"), sem("s_stored1")]
        s_w3, s_set, s_set2, s_mm3, s_ev3, s_neg = (sem(n_) for n_ in "s_w3 s_set s_set2 s_mm3 s_ev3 s_neg".split())
        NORMS = ("n_center", "n_var", "n_norm", "txt", "k_center", "k_var", "k_norm", "g_center", "g_var", "g_norm")
        INNER = ("xz", "conv0", "conv1", "conv2", "conv3", "su1", "su2", "su_err", "su3", "dbc", "dt", "split0", "split1",
                 "split2", "split3", "sd1", "sd2", "sd_err", "sd3", "du", "z1", "z2", "z_arg", "z3", "z_gate")
        POST = ("gate", "f_center", "f_var", "f_norm", "f_1", "f_2", "f_T")
        BETWEEN = (("xz",), ("conv0", "conv1"), ("gate", "conv2", "conv3"), ("f_center", "su1"), ("f_var", "su2"),
                   ("f_norm", "su_err"), ("f_1", "su3", "z1"), ("dbc", "z2"), ("n_center", "dt", "split0"),
                   ("n_var", "f_2", "sd1", "split1"), ("n_norm", "txt", "sd2", "split2", "z_arg"),
                   ("f_T", "k_center", "sd_err", "split3"), ("k_var", "sd3"), ("k_norm", "du"), ("g_center", "z3"),
                   ("g_var", "g_norm", "z_gate"))
        assert TAPS == 4 and NS == len(BETWEEN)
        assert sorted(NORMS + INNER + POST) == sorted(c for cs in BETWEEN for c in cs)
        AHEAD = 2

        def ticks3(norms, inner, post, chain_first=False):
            for n in range(NS):
                yield "step", 0, n
                if n > 0 or post:
                    yield ("product", 0, n - 1) if n > 0 else ("product", -1, NS - 1)
                ahead = (0, n + AHEAD) if n + AHEAD < NS else (1, n + AHEAD - NS) if inner else None
                if ahead and not chain_first:
                    yield "ahead", *ahead
                for c in BETWEEN[n]:
                    if c in NORMS and norms:
                        yield c, 2, 0
                    if c in INNER and inner:
                        yield c, 1, 0
                    if c in POST and post:
                        yield c, -1, 0
                if ahead and chain_first:
                    yield "ahead", *ahead
                if n % 2 == 1 and (n > 1 or post):
                    yield ("sum", 0, n // 2 - 1) if n > 1 else ("sum", -1, NS // 2 - 1)

        def fusion(eng, run, at_block=lambda: None, chain_first=False):
            ticks = partial(ticks3, chain_first=chain_first)
            first, last = (0, 0, 0), (PAIRS - 1, 1, PAIRS - 1)
            run(first, ((c, 0, 0) for c in NORMS + INNER))
            run(first, ((c, 1, 0) for c in NORMS))
            run(first, (("ahead", 0, n) for n in range(AHEAD)))
            run(first, ticks(norms=True, inner=True, post=False))
            with eng.Fori(0, PAIRS - 2) as it:
                at_block()
                run((it, 1, it), ticks(norms=True, inner=True, post=True))
                run((it + 1, 0, it + 1), ticks(norms=True, inner=True, post=True))
            at_block()
            run(shift(last, -2), ticks(norms=True, inner=True, post=True))
            run(shift(last, -1), ticks(norms=False, inner=True, post=True))
            run(last, ticks(norms=False, inner=False, post=True))
            run(last, (("product", 0, NS - 1), ("sum", 0, NS // 2 - 1)))
            run(last, ((c, 0, 0) for c in POST))

        def images(ap, n=S):
            return ap.rearrange("p (b n) -> p b n", n=n)

        def flat(ap):
            return ap.rearrange("p a n -> p (a n)")

        def tu(u):
            q, par = u[:2]
            return tres.rearrange("p u n -> p (u n)")[:, bass.ds(q * (4 * TXT) + par * (2 * TXT), 2 * TXT)].rearrange(
                "p (b n) -> p b n", b=2)

        with nc.Block() as block:
            @block.sync
            def _(sp):
                sp.wait_ge(s_set, 7)
                def put(dst, src):
                    sp.dma_start(dst, src).then_inc(s_w3, 16)
                put(wp_raw, m_W_proj)
                put(wx_pad[:, 0:RANK + 2 * NS], m_W_x)
                put(wx_pad[:, 2 * RANK:3 * RANK], m_W_x[:, RANK:RANK + 2 * NS])
                put(wx_pad[:, 3 * RANK:4 * RANK], m_W_x[:, RANK:RANK + 2 * NS])
                put(wdt_pad[0:RANK], m_W_dt)
                put(w1_raw, f_W1)
                put(w2_raw, f_W2)
                put(alog, m_A_log)
                put(taps, m_conv_w.rearrange("d a k -> d (a k)"))
                for col, v in ((NW, norm_w), (NB, norm_b), (LG, m_ln_g), (LB, m_ln_b), (CB, m_conv_b), (DTB, m_b_dt),
                               (DV, m_D), (B1, f_b1), (B2, f_b2)):
                    put(mvec[:, col:col + 1], v.rearrange("(d a) -> d a", a=1))

                def load_txt(u):
                    q, par = u[:2]
                    done(sp, "n_txt", shift(u, -2))
                    src = txt[bass.ds(q * 4 + 2 * par, 2)].rearrange("b n d -> (b n) d")
                    sp.dma_start(txt_rows[0:2 * TXT, par, :], src).then_inc(s_txt[par], 16)

                def store(u):
                    q, par = u[:2]
                    done(sp, "f_rows", u)
                    o = out[bass.ds(q * 4 + 2 * par, 2)].rearrange("b n d -> n b d")
                    r = rows.rearrange("p (b t) d -> p b t d", b=2)
                    sp.dma_start(o[0:P], r[:, :, 0]).then_inc(s_stored[par], 16)
                    sp.dma_start(o[P:S], r[0:S - P, :, 1]).then_inc(s_stored[par], 16)

                def run(u, steps):
                    for name, d, n in steps:
                        if name == "n_center":
                            load_txt(shift(u, d))
                        elif name == "f_T":
                            store(shift(u, d))

                fusion(sp, run)
                for par in range(2):
                    sp.wait_ge(s_stored[par], VD((PAIRS - 1, par, 0), 2))

            @block.gpsimd
            def _(pool):
                credit(pool, "su_one su_cor sd_one sd_cor b_hi b_res b_mid b_lo du_out m_inp")
                for z in (txt_rows, xpad.rearrange("p k b n -> p (k b n)"), wdt_pad, diagD, bsel, flat(decay[:, 0]), flat(decay[:, 1])):
                    pool.memset(z, 0.0).then_inc(s_set, 1)
                pool.memset(bcs.rearrange("p a b n -> p (a b n)"), 0.0).then_inc(s_set2, 1)
                pool.wait_ge(s_set, 7)
                for k in range(3):
                    pool.affine_select(out=bsel, in_=bsel, compare_op=ALU.not_equal, fill=1.0, base=-32 * (k + 1),
                                       pattern=[[-1, 2 * NS], [0, P]], channel_multiplier=1).then_inc(s_set2, 1)
                    pool.wait_ge(s_set2, k + 2)
                pool.wait_ge(s_w3, 16 * 18)
                for w in (w1_raw, w2_raw):
                    pool.affine_select(out=w, in_=w, compare_op=ALU.is_ge, fill=0.0, base=0,
                                       pattern=[[-1, D]], channel_multiplier=1).then_inc(s_set2, 1)

                def alone(u, before):
                    done(pool, *before)
                    passed(pool)

                def chain(name, u, before):
                    par = u[1]
                    bc = bcs[:, par]
                    if name in ("su1", "sd1"):
                        pre = name[:2]
                        done(pool, pre + "_exp", u)
                        passed(pool)
                        pool.tensor_scalar(op, ex, 1.0, 1.0, ALU.mult, ALU.add).then_inc(sems[pre + "_one"], 1)
                    elif name in ("su_err", "sd_err"):
                        pre = name[:2]
                        done(pool, pre + "_ln", u)
                        done(pool, pre + "_err", u)
                        pool.tensor_tensor(lg, lg, op, ALU.subtract).then_inc(sems[pre + "_cor"], 1)
                    elif name == "split0":
                        done(pool, "dbc_out", u, 1)
                        done(pool, "m_c", shift(u, -2), NS - 1)
                        passed(pool)
                        pool.tensor_scalar(bc, dbc, 1.0, 0.0, ALU.mult, ALU.add).then_inc(sems["b_hi"], 1)
                    elif name == "split1":
                        done(pool, "b_hi", u)
                        alone(u, before)
                        pool.tensor_tensor(bres[64:P], dbc[64:P], bc[64:P], ALU.subtract).then_inc(sems["b_res"], 1)
                        alone(u, ("b_res", u))
                    elif name == "split2":
                        alone(u, before)
                        pool.tensor_scalar(bc[64:P], bres[64:P], 1.0, 0.0, ALU.mult, ALU.add).then_inc(sems["b_mid"], 1)
                        alone(u, ("b_mid", u))
                    elif name == "split3":
                        alone(u, before)
                        pool.tensor_tensor(bc[96:P], bres[96:P], bc[96:P], ALU.subtract).then_inc(sems["b_lo"], 1)
                        alone(u, ("b_lo", u))
                    elif name == "du":
                        done(pool, "sd_out", u)
                        pool.tensor_tensor(flat(du[:, par]), flat(delta[:, par]), flat(uu[:, par]), ALU.mult).then_inc(sems["du_out"], 1)

                def inputs(u, n):
                    par = u[1]
                    if n == 0:
                        done(pool, "du_out", u)
                    done(pool, "m_brep", u, n)
                    done(pool, "m_scan", u, n - 2)
                    pool.tensor_tensor(flat(inp[:, n % 2]), flat(du[:, par]), flat(brep[:, n % 2]), ALU.mult).then_inc(sems["m_inp"], 1)

                signal = {"su1": "su_one", "sd1": "sd_one", "su_err": "su_cor", "sd_err": "sd_cor", "split0": "b_hi",
                          "split1": "b_res", "split2": "b_mid", "split3": "b_lo", "du": "du_out"}

                def run(u, steps):
                    before = ("m_inp", u, 0)
                    for name, d, n in steps:
                        v = shift(u, d)
                        if name == "ahead":
                            inputs(v, n)
                            before = ("m_inp", v, n)
                        elif name in signal:
                            chain(name, v, before)
                            before = (signal[name], v)

                fusion(pool, run)

            @block.tensor
            def _(pe):
                credit(pe, "n_centered n_vared n_txt k_centered k_vared g_centered g_vared xz_mm dbc_mm dt_mm "
                           "f_centered f_vared f_mm1 f_mm2 f_T m_b m_c m_sum")
                pe.wait_ge(s_set, 7)
                pe.wait_ge(s_w3, 16 * 18)
                pe.wait_ge(s_set2, 6)
                pe.matmul(ps[:, 6, 0:1], wp_raw[:, 0:D], mvec[:, LB:LB + 1], start=True, stop=True)
                pe.matmul(ps[:, 6, 1:2], wp_raw[:, D:2 * D], mvec[:, LB:LB + 1], start=True, stop=True)
                pe.transpose(ps[:, 7, 0:D], w1_raw, ident[:, :])
                pe.transpose(ps[:, 7, D:2 * D], w2_raw, ident[:, :]).then_inc(s_mm3, 1)
                pe.wait_ge(s_ev3, 6)

                def center_of(src, pre):
                    pe.matmul(ps[:, 6, 0:src.shape[-1]], center[:, :], src, start=True, stop=True).then_inc(sems[pre + "_centered"], 1)

                def var_of(n, pre, u):
                    done(pe, pre + "_squared", u)
                    pe.matmul(ps[:, 7, 0:n], mean[:, :], sq3[:, 0:n], start=True, stop=True).then_inc(sems[pre + "_vared"], 1)

                def chain(name, u):
                    par = u[1]
                    if name == "n_center":
                        done(pe, "f_gelu", shift(u, -3))
                        done(pe, "xz_out", shift(u, -1))
                        center_of(hu(u), "n")
                    elif name == "n_var":
                        done(pe, "dt_out", shift(u, -1), 1)
                        var_of(T2, "n", u)
                    elif name == "txt":
                        pe.wait_ge(s_txt[par], VD(u, 1))
                        done(pe, "n_logged", u)
                        pe.transpose(ps[:, 7, 0:P], txt_rows[:, par, :], ident[:, :]).then_inc(sems["n_txt"], 1)
                    elif name == "k_center":
                        done(pe, "n_normed", u)
                        done(pe, "n_txt_out", u)
                        center_of(hc, "k")
                    elif name == "k_var":
                        var_of(S2, "k", u)
                    elif name == "g_center":
                        done(pe, "k_normed", u)
                        center_of(skip, "g")
                    elif name == "g_var":
                        var_of(S2, "g", u)
                    elif name == "xz":
                        done(pe, "g_normed", u)
                        for k in range(2):
                            last = pe.matmul(ps[:, 6 + k, 0:S2], wp_f[:, k * D:(k + 1) * D], yn, start=True, stop=True)
                        last.then_inc(sems["xz_mm"], 1)
                    elif name in ("dbc", "dt"):
                        for k in range(2):
                            if name == "dbc" and k == 0:
                                done(pe, "dt_out", shift(u, -1), 1)
                                done(pe, "f_rows", shift(u, -3))
                                done(pe, "f_normed", shift(u, -2))
                                done(pe, "su_out", u)
                            elif name == "dt" and k == 0:
                                done(pe, "dbc_out", u, 1)
                            w, src = (wx_pad, uu[:, par, k, :]) if name == "dbc" else (wdt_pad, dbc[:, k, :])
                            pe.matmul(ps[:, 5 + 2 * k, 0:S2], w, src, start=True, stop=True).then_inc(sems[name + "_mm"], 1)
                    elif name == "f_center":
                        done(pe, "f_added", u)
                        if not isinstance(u[0], int) or u[0] < PAIRS - 1:
                            done(pe, "xz_out", shift(u, 2))
                        done(pe, "f_rows", shift(u, -1))
                        center_of(h1, "f")
                    elif name == "f_var":
                        var_of(S2, "f", u)
                    elif name == "f_1":
                        done(pe, "f_normed", u)
                        pe.matmul(ps[:, 6, 0:S2], w1T, yn, start=True, stop=True).then_inc(sems["f_mm1"], 1)
                    elif name == "f_2":
                        done(pe, "f_gelu", u)
                        if not isinstance(u[0], int) or u[0] < PAIRS - 1:
                            done(pe, "dt_out", shift(u, 2), 1)
                        pe.matmul(ps[:, 5, 0:S2], w2T, gl, start=True, stop=True).then_inc(sems["f_mm2"], 1)
                    elif name == "f_T":
                        done(pe, "f_out", u)
                        for b in range(2):
                            for t in range(2):
                                m = P if t == 0 else S - P
                                last = pe.transpose(ps[0:m, 5, (2 * b + t) * D:(2 * b + t + 1) * D],
                                                    h1[:, b * S + t * P:b * S + t * P + m], ident[:, :])
                        last.then_inc(sems["f_T"], 1)

                def rep_b(u, n):
                    if n == 0:
                        done(pe, "b_lo", u)
                    done(pe, "m_brep", u, n - 1)
                    for k in range(2):
                        last = pe.matmul(ps[:, k, 0:S2], bsel[:, n, :], bcs[:, u[1], k, :], start=True, stop=True)
                    last.then_inc(sems["m_b"], 1)

                def rep_c(u, n):
                    done(pe, "m_prod", u, n - 1)
                    for k in range(2):
                        last = pe.matmul(ps[:, 2 + k, 0:S2], bsel[:, NS + n, :], bcs[:, u[1], k, :], start=True, stop=True)
                    last.then_inc(sems["m_c"], 1)

                def add_up(u, m):
                    par = u[1]
                    if m == 0:
                        done(pe, "f_gated", shift(u, -1))
                        pe.matmul(ps[:, 4, 0:S2], diagD, uu[:, par, 0, :], start=True, stop=False)
                        pe.matmul(ps[:, 4, 0:S2], diagD, uu[:, par, 1, ::-1], start=False, stop=False)
                    done(pe, "m_pair", u, m)
                    pe.matmul(ps[:, 4, 0:S2], ident[:, :], pair[:, m % 2, 0, :], start=False, stop=False)
                    pe.matmul(ps[:, 4, 0:S2], ident[:, :], pair[:, m % 2, 1, ::-1], start=False,
                              stop=(m == NS // 2 - 1)).then_inc(sems["m_sum"], 1)

                def run(u, steps):
                    for name, d, n in steps:
                        v = shift(u, d)
                        if name == "ahead":
                            rep_b(v, n)
                        elif name == "product":
                            rep_c(v, n)
                        elif name == "sum":
                            add_up(v, n)
                        else:
                            chain(name, v)

                fusion(pe, run)

            @block.scalar
            def _(sc):
                credit(sc, "n_squared n_logged n_rstd k_squared k_logged k_rstd g_squared g_logged g_rstd xz_out "
                           "su_abs su_exp su_ln dbc_out dt_out sd_abs sd_exp sd_ln z_abs z_exp z_ln z_sig "
                           "f_squared f_logged f_rstd f_gelu f_rows m_brep m_decay")

                def exp_ln_tables():
                    sc.preload_act_table_set("natural_log_exp_and_others")

                exp_ln_tables()
                sc.wait_ge(s_w3, 16 * 18)
                sc.wait_ge(s_mm3, 1)
                sc.activation(w1T, ps[:, 7, 0:D], ACT.Copy).then_inc(s_ev3, 1)
                sc.activation(w2T, ps[:, 7, D:2 * D], ACT.Copy).then_inc(s_ev3, 1)
                sc.activation(alog, alog, ACT.Exp).then_inc(s_neg, 1)
                sc.wait_ge(s_neg, 1)
                sc.activation(amat, alog, ACT.Copy, scale=-1.0).then_inc(s_neg, 1)
                sc.wait_ge(s_neg, 2)
                sc.wait_ge(s_ev3, 6)

                def squared(n, pre, u):
                    done(sc, pre + "_centered", u)
                    sc.activation(sq3[:, 0:n], ps[:, 6, 0:n], ACT.Square).then_inc(sems[pre + "_squared"], 1)

                def rstd(n, pre, u):
                    done(sc, pre + "_vared", u)
                    sc.activation(rs3[:, 0:n], ps[:, 7, 0:n], ACT.Ln, bias=eps_col[:, :]).then_inc(sems[pre + "_logged"], 1)
                    done(sc, pre + "_logged", u)
                    sc.activation(rs3[:, 0:n], rs3[:, 0:n], ACT.Exp, scale=-0.5).then_inc(sems[pre + "_rstd"], 1)

                def exp_neg_abs(dst, src, pre, u):
                    sc.activation(dst, src, ACT.Abs).then_inc(sems[pre + "_abs"], 1)
                    done(sc, pre + "_abs", u)
                    sc.activation(dst, dst, ACT.Exp, scale=-1.0).then_inc(sems[pre + "_exp"], 1)

                def chain(name, u):
                    par = u[1]
                    if name in ("n_center", "k_center", "g_center", "f_center"):
                        squared(T2 if name[0] == "n" else S2, name[0], u)
                    elif name in ("n_var", "k_var", "g_var", "f_var"):
                        rstd(T2 if name[0] == "n" else S2, name[0], u)
                    elif name == "xz":
                        done(sc, "xz_mm", u)
                        done(sc, "conv_step", shift(u, -2), 2 * TAPS - 1)
                        done(sc, "z_out", shift(u, -2))
                        sc.activation(xpad[:, par, :, PADW:PADW + S], images(ps[:, 6, 0:S2]), ACT.Identity, bias=bxz[:, 0:1])
                        sc.activation(zz[:, par], ps[:, 7, 0:S2], ACT.Identity, bias=bxz[:, 1:2]).then_inc(sems["xz_out"], 1)
                    elif name == "z1":
                        done(sc, "xz_out", u)
                        exp_neg_abs(lz, zz[:, par], "z", u)
                    elif name == "z2":
                        done(sc, "z_exp", u)
                        sc.activation(lz, lz, ACT.Ln, bias=one_col[:, :]).then_inc(sems["z_ln"], 1)
                    elif name == "z3":
                        done(sc, "z_arg", u)
                        sc.activation(lz, lz, ACT.Exp).then_inc(sems["z_sig"], 1)
                    elif name == "su1":
                        done(sc, "conv_step", u, 2 * TAPS - 1)
                        exp_neg_abs(ex, flat(cv), "su", u)
                    elif name == "dt":
                        done(sc, "su_out", u)
                        for k in range(2):
                            done(sc, "dt_mm", u, k)
                            sc.activation(cv[:, k], ps[:, 5 + 2 * k, 0:S2], ACT.Identity, bias=mvec[:, DTB:DTB + 1]).then_inc(sems["dt_out"], 1)
                    elif name == "sd1":
                        done(sc, "dt_out", u, 1)
                        exp_neg_abs(ex, flat(cv), "sd", u)
                    elif name in ("su2", "sd2"):
                        pre = name[:2]
                        done(sc, pre + "_one", u)
                        sc.activation(lg, op, ACT.Ln).then_inc(sems[pre + "_ln"], 1)
                    elif name == "dbc":
                        done(sc, "b_res", shift(u, -1))
                        for k in range(2):
                            done(sc, "dbc_mm", u, k)
                            sc.activation(dbc[:, k], ps[:, 5 + 2 * k, 0:S2], ACT.Copy).then_inc(sems["dbc_out"], 1)
                    elif name == "f_1":
                        done(sc, "f_mm1", u)
                        sc.activation(gl, ps[:, 6, 0:S2], ACT.Gelu, bias=mvec[:, B1:B1 + 1]).then_inc(sems["f_gelu"], 1)
                        exp_ln_tables()
                    elif name == "f_T":
                        done(sc, "f_T", u)
                        pu = shift(u, -1)
                        sc.wait_ge(s_stored[pu[1]], VD(pu, 2))
                        pv = ps[:, 5, :].rearrange("p (b t d) -> p b t d", b=2, t=2)
                        rv = rows.rearrange("p (b t) d -> p b t d", b=2)
                        sc.activation(rv[:, :, 0], pv[:, :, 0], ACT.Copy)
                        sc.activation(rv[0:S - P, :, 1], pv[0:S - P, :, 1], ACT.Copy).then_inc(sems["f_rows"], 1)

                def rep_b(u, n):
                    done(sc, "m_b", u, n)
                    done(sc, "m_inp", u, n - 2)
                    sc.activation(brep[:, n % 2], ps[:, 0:2, 0:S2], ACT.Copy).then_inc(sems["m_brep"], 1)

                def decays(u, n):
                    par = u[1]
                    if n == 0:
                        done(sc, "sd_out", u)
                    done(sc, "m_scan", u, n - 2)
                    o = decay[:, n % 2].rearrange("p k (b s) -> p (k b) s", b=2)[:, :, 1:S]
                    i = delta[:, par].rearrange("p k (b s) -> p (k b) s", b=2)[:, :, 1:S]
                    sc.activation(o, i, ACT.Exp, scale=amat[:, n:n + 1]).then_inc(sems["m_decay"], 1)

                def run(u, steps):
                    for name, d, n in steps:
                        v = shift(u, d)
                        if name == "ahead":
                            rep_b(v, n)
                            decays(v, n)
                        else:
                            chain(name, v)

                fusion(sc, run, exp_ln_tables)

            @block.vector
            def _(dve):
                credit(dve, "n_scaled n_normed n_txt_out k_normed k_res g_normed conv_step su_err su_out sd_err sd_out "
                            "z_arg z_out f_gated f_added f_normed f_out m_scan m_prod m_pair")
                dve.wait_ge(s_w3, 16 * 18)
                dve.tensor_scalar(wp_f, wp_raw, mvec[:, LG:LG + 1], None, ALU.mult).then_inc(s_ev3, 1)
                dve.wait_ge(s_set, 7)
                dve.tensor_scalar(diagD, ident[:, :], mvec[:, DV:DV + 1], None, ALU.mult).then_inc(s_ev3, 1)
                dve.wait_ge(s_mm3, 1)
                dve.tensor_copy(bxz, ps[:, 6, 0:2]).then_inc(s_ev3, 1)
                dve.memset(lz, 0.0).then_inc(s_ev3, 1)

                def conv(u, k):
                    x_ = xpad[:, u[1]]
                    for j, (v, off) in enumerate(((images(cv[:, 0, :]), k),
                                                  (images(cv[:, 1, :])[:, ::-1, ::-1], 2 * PADW - k))):
                        src = x_[:, :, off:off + S]
                        if k == 0:
                            dve.tensor_scalar(v, src, taps[:, 0:1], mvec[:, CB:CB + 1], ALU.mult, ALU.add).then_inc(sems["conv_step"], 1)
                        else:
                            done(dve, "conv_step", u, 2 * k + j - 2)
                            dve.scalar_tensor_tensor(v, src, taps[:, k:k + 1], v, ALU.mult, ALU.add).then_inc(sems["conv_step"], 1)

                def chain(name, u):
                    par = u[1]
                    if name == "n_norm":
                        done(dve, "n_rstd", u)
                        done(dve, "k_res", shift(u, -1))
                        o = images(hc)[:, :, 0:NT]
                        dve.scalar_tensor_tensor(o, images(ps[:, 6, 0:T2], NT), mvec[:, NW:NW + 1], images(rs3[:, 0:T2], NT),
                                                 ALU.mult, ALU.mult).then_inc(sems["n_scaled"], 1)
                        done(dve, "n_scaled", u)
                        dve.tensor_scalar(o, o, mvec[:, NB:NB + 1], None, ALU.add).then_inc(sems["n_normed"], 1)
                    elif name == "txt":
                        done(dve, "n_txt", u)
                        dve.tensor_copy(images(hc)[:, :, NT:S], images(ps[:, 7, 0:2 * TXT], TXT)).then_inc(sems["n_txt_out"], 1)
                    elif name == "k_norm":
                        done(dve, "k_rstd", u)
                        dve.tensor_tensor(skip, ps[:, 6, 0:S2], rs3, ALU.mult).then_inc(sems["k_normed"], 1)
                        done(dve, "k_normed", u)
                        dve.tensor_tensor(images(hu(u), NT), images(hc)[:, :, 0:NT], images(skip)[:, :, 0:NT], ALU.add)
                        dve.tensor_tensor(tu(u), images(hc)[:, :, NT:S], images(skip)[:, :, NT:S], ALU.add).then_inc(sems["k_res"], 1)
                    elif name in ("g_norm", "f_norm"):
                        done(dve, name[0] + "_rstd", u)
                        dve.tensor_tensor(yn, ps[:, 6, 0:S2], rs3, ALU.mult).then_inc(sems[name[0] + "_normed"], 1)
                    elif name[:4] == "conv":
                        done(dve, "xz_out", u)
                        conv(u, int(name[4]))
                    elif name == "z_arg":
                        done(dve, "z_ln", u)
                        dve.scalar_tensor_tensor(lz, zz[:, par], 0.0, lz, ALU.min, ALU.subtract).then_inc(sems["z_arg"], 1)
                    elif name == "z_gate":
                        done(dve, "z_sig", u)
                        dve.tensor_tensor(zg[:, par], zz[:, par], lz, ALU.mult).then_inc(sems["z_out"], 1)
                    elif name in ("su_err", "sd_err"):
                        pre = name[:2]
                        done(dve, pre + "_one", u)
                        done(dve, pre + "_ln", u)
                        dve.scalar_tensor_tensor(op, op, -1.0, ex, ALU.add, ALU.subtract).then_inc(sems[pre + "_err"], 1)
                    elif name in ("su3", "sd3"):
                        pre = name[:2]
                        done(dve, pre + "_cor", u)
                        if pre == "su":
                            done(dve, "m_sum", shift(u, -2), 0)
                            dst = uu[:, par]
                        else:
                            done(dve, "m_decay", shift(u, -2), NS - 1)
                            dst = delta[:, par]
                        dve.scalar_tensor_tensor(flat(dst), flat(cv), 0.0, lg, ALU.max, ALU.add).then_inc(sems[pre + "_out"], 1)
                    elif name == "gate":
                        done(dve, "m_sum", u, NS // 2 - 1)
                        dve.tensor_tensor(h1, ps[:, 4, 0:S2], zg[:, par], ALU.mult).then_inc(sems["f_gated"], 1)
                        done(dve, "f_gated", u)
                        h3_ = images(h1)
                        dve.tensor_tensor(h3_[:, :, 0:NT], h3_[:, :, 0:NT], images(hu(u), NT), ALU.add)
                        dve.tensor_tensor(h3_[:, :, NT:S], h3_[:, :, NT:S], tu(u), ALU.add).then_inc(sems["f_added"], 1)
                    elif name == "f_2":
                        done(dve, "f_mm2", u)
                        dve.scalar_tensor_tensor(h1, ps[:, 5, 0:S2], mvec[:, B2:B2 + 1], h1, ALU.add, ALU.add).then_inc(sems["f_out"], 1)

                def scan(u, n):
                    done(dve, "m_prod", u, n - 2)
                    done(dve, "m_inp", u, n)
                    done(dve, "m_decay", u, n)
                    dve.tensor_tensor_scan(flat(state[:, n % 2]), flat(decay[:, n % 2]), flat(inp[:, n % 2]), 0.0,
                                           ALU.mult, ALU.add).then_inc(sems["m_scan"], 1)

                def product(u, n):
                    done(dve, "m_scan", u, n)
                    if n % 2 == 0:
                        done(dve, "m_pair", u, n // 2 - 1)
                    done(dve, "m_c", u, n)
                    dve.tensor_tensor(prod[:, n % 2], state[:, n % 2], ps[:, 2:4, 0:S2], ALU.mult).then_inc(sems["m_prod"], 1)
                    if n % 2 == 1:
                        m = n // 2
                        done(dve, "m_prod", u, n)
                        done(dve, "m_sum", u, m - 2)
                        dve.tensor_tensor(pair[:, m % 2], prod[:, 0], prod[:, 1], ALU.add).then_inc(sems["m_pair"], 1)

                def run(u, steps):
                    for name, d, n in steps:
                        v = shift(u, d)
                        if name == "step":
                            scan(v, n)
                        elif name == "product":
                            product(v, n)
                        else:
                            chain(name, v)

                fusion(dve, run)


_INS = ["x", "txt", "L0_tok_conv_w", "L0_tok_conv_b", "L0_tok_cls_token", "L0_tok_pos_embed", "L0_tok_ln1_w",
        "L0_tok_ln1_b", "L0_tok_qkv_w", "L0_tok_qkv_b", "L0_tok_proj_w", "L0_tok_proj_b", "L0_tok_ln2_w",
        "L0_tok_ln2_b", "L0_tok_fc1_w", "L0_tok_fc1_b", "L0_tok_fc2_w", "L0_tok_fc2_b", "L0_tok_norm_w",
        "L0_tok_norm_b", "L0_attn_ln_g", "L0_attn_ln_b", "L0_attn_W_proj", "L0_attn_conv_w", "L0_attn_conv_b",
        "L0_attn_W_x", "L0_attn_W_dt", "L0_attn_b_dt", "L0_attn_A_log", "L0_attn_D", "L0_ffn_W1", "L0_ffn_b1",
        "L0_ffn_W2", "L0_ffn_b2"]


def kernel(**inputs):
    import numpy as _np
    import concourse.bacc as _bacc
    from concourse.bass_utils import run_bass_kernel_spmd as _run

    nc = _bacc.Bacc("TRN2", target_bir_lowering=False, num_devices=1)
    arrays, args = {}, []
    for name in _INS:
        a = _np.ascontiguousarray(inputs[name])
        arrays[f"in_{name}"] = a
        args.append(nc.dram_tensor(f"in_{name}", a.shape, mybir.dt.from_np(a.dtype), kind="ExternalInput").ap())
    b, tokens, dim = inputs["x"].shape[0], inputs["L0_tok_pos_embed"].shape[1], inputs["L0_tok_conv_w"].shape[1]
    out = nc.dram_tensor("out_0", (b, tokens + inputs["txt"].shape[1], dim), F32, kind="ExternalOutput").ap()
    scratch = nc.dram_tensor("scratch", (2, 3, 2, dim, 2 * tokens), BF16, kind="Internal").ap()
    early_fusion(nc, *args, out, scratch)
    r = _run(nc, [arrays], core_ids=[0])
    return r.results[0]["out_0"]
```

```python
from contextlib import ExitStack

import concourse.bass as bass
from concourse import mybir

F32 = mybir.dt.float32
BF16 = mybir.dt.bfloat16
ACT = mybir.ActivationFunctionType
ALU = mybir.AluOpType
AX = mybir.AxisListType

P = 128
ARENA = 35960
CREDIT = 3


def shift(u, d):
    q, par, lq = u
    n = par + d
    return (q + n // 2, n % 2, lq + n // 2)


def V(u, k=1, j=0):
    q, par = u[:2]
    return q * (2 * k) + ((par + CREDIT) * k + j + 1)


def VD(u, n):
    return u[0] * (16 * n) + 16 * n


def VC(u, n):
    return u[0] * (16 * n) + 32 * n


def early_fusion(nc, x, txt, conv_w, conv_b, cls_token, pos_embed, ln1_w, ln1_b, qkv_w, qkv_b,
                 proj_w, proj_b, ln2_w, ln2_b, fc1_w, fc1_b, fc2_w, fc2_b, norm_w, norm_b,
                 m_ln_g, m_ln_b, m_W_proj, m_conv_w, m_conv_b, m_W_x, m_W_dt, m_b_dt, m_A_log, m_D,
                 f_W1, f_b1, f_W2, f_b2, out):
    B, CH, IMG, _ = x.shape
    D = conv_w.shape[1]
    DEPTH = ln1_w.shape[0]
    NT = pos_embed.shape[1]
    PS = 16
    G = IMG // PS
    NP = G * G
    HEADS, HD = 8, D // 8
    HG = 4
    T2 = 2 * NT
    UNITS = B // 2
    PAIRS = UNITS // 2
    TXT = txt.shape[1]
    S = NT + TXT
    S2 = 2 * S
    NS = m_A_log.shape[1]
    RANK = m_W_dt.shape[0]
    TAPS = m_conv_w.shape[2]
    EPS = 1e-5
    KT = (P, NT - P)
    SCALE = HD ** -0.5

    with ExitStack() as ctx:
        def sb(name, shape, dt=F32):
            return ctx.enter_context(nc.sbuf_tensor(name, shape, dt))

        sems = {}

        def sem(name):
            if name not in sems:
                sems[name] = ctx.enter_context(nc.semaphore(name))
            return sems[name]

        def passed(eng):
            eng.sem_inc(sem("s_passed"), 1)

        ps = ctx.enter_context(nc.psum_tensor("ps", [P, 8, 512], F32))

        ident = sb("ident", [P, P])
        identb = sb("identb", [P, P], BF16)
        center = sb("center", [P, P])
        mean = sb("mean", [P, P])
        e0 = sb("e0", [P, 1])
        eps_col = sb("eps_col", [P, 1])
        one_col = sb("one_col", [P, 1])
        h = sb("h", [P, B * NT])
        arena = sb("arena", [P, ARENA])
        h3 = h[:, :].rearrange("p (b n) -> p b n", n=NT)

        at = [0]

        def carve(*dims, dt=F32):
            n = 1
            for d_ in dims:
                n *= d_
            words = n if dt == F32 else (n + 1) // 2
            a = arena[:, at[0]:at[0] + words]
            at[0] += words
            assert at[0] <= ARENA, at[0]
            if dt != F32:
                a = a.bitcast(dt)
            if len(dims) == 2:
                a = a.rearrange("p (a b) -> p a b", b=dims[1])
            elif len(dims) == 3:
                a = a.rearrange("p (a b c) -> p a b c", b=dims[1], c=dims[2])
            elif len(dims) == 4:
                a = a.rearrange("p (a b c d) -> p a b c d", b=dims[1], c=dims[2], d=dims[3])
            return a

        def hu(u):
            _, par, lq = u
            if isinstance(lq, int):
                lq %= PAIRS
            return h[:, bass.ds(lq * (2 * T2) + par * T2, T2)]

        XW = G * IMG
        HALF = 64
        KROWS1 = HALF + CH * PS
        XB = 4
        patches = carve(XB, 2, XW)
        wconv = carve(8, D)
        pos_rows = carve(2, D)
        posb = carve(NT)
        cls_col = carve(1)
        convb_col = carve(1)
        s_const = sem("s_const")
        s_init = sem("s_init")
        s_wl = sem("s_wl")
        s_xl = [sem(f"s_xl{i}") for i in range(XB)]
        s_posT = sem("s_posT")
        s_pose = sem("s_pose")
        s_emb = sem("s_emb")
        s_hemb = sem("s_hemb")
        s_gap = sem("s_gap")
        s_half = sem("s_half")
        NXL = 2 * CH

        with nc.Block() as block:
            @block.gpsimd
            def _(pool):
                pool.memset(ident[:, :], 0.0).then_inc(s_const, 1)
                pool.memset(identb[:, :], 0.0).then_inc(s_const, 1)
                pool.memset(center[:, :], -1.0 / D).then_inc(s_const, 1)
                pool.memset(mean[:, :], 1.0 / D).then_inc(s_const, 1)
                pool.memset(e0[:, :], 0.0).then_inc(s_const, 1)
                pool.memset(eps_col[:, :], EPS).then_inc(s_const, 1)
                pool.memset(one_col[:, :], 1.0).then_inc(s_const, 1)
                pool.wait_ge(s_const, 7)
                for m, v in ((ident, 1.0), (identb, 1.0), (center, 1.0 - 1.0 / D)):
                    pool.affine_select(out=m[:, :], in_=m[:, :], compare_op=ALU.not_equal, fill=v, base=0,
                                       pattern=[[-1, P]], channel_multiplier=1).then_inc(s_init, 1)
                pool.affine_select(out=e0[:, :], in_=e0[:, :], compare_op=ALU.not_equal, fill=1.0, base=0,
                                   pattern=[[0, 1]], channel_multiplier=1).then_inc(s_init, 1)

            @block.sync
            def _(sp):
                sp.wait_ge(s_gap, 1)
                for half in range(2):
                    for c in range(CH):
                        r = half * HALF + c * PS
                        src = conv_w.rearrange("(c i f j) n -> f c i j n", c=CH, i=PS, f=2)[half, c]
                        sp.dma_start(wconv[r:r + PS], src).then_inc(s_wl, 16)
                sp.dma_start(pos_rows[:, 0, :], pos_embed[0, 0:P, :]).then_inc(s_wl, 16)
                sp.dma_start(pos_rows[0:NT - P, 1, :], pos_embed[0, P:NT, :]).then_inc(s_wl, 16)
                sp.dma_start(cls_col, cls_token[0].rearrange("a d -> d a")).then_inc(s_wl, 16)
                sp.dma_start(convb_col, conv_b.rearrange("(d a) -> d a", a=1)).then_inc(s_wl, 16)

                def load(u):
                    q, par = u
                    for c in range(CH):
                        for b in range(2):
                            src = x[bass.ds(q * (2 * XB) + (par * 2 + b), 1), c].rearrange("b (g i) w -> i (b g) w", i=PS)
                            dst = patches[c * PS:(c + 1) * PS, par, b].rearrange("p (g w) -> p g w", w=IMG)
                            sp.dma_start(dst, src).then_inc(s_xl[par], 16)
                for par in range(XB):
                    sp.wait_ge(s_gap, par + 2)
                    load((0, par))
                with sp.Fori(1, UNITS // XB) as q:
                    for par in range(XB):
                        sp.wait_ge(s_emb, q * XB + (par + 1 - XB))
                        passed(sp)
                        load((q, par))

            @block.tensor
            def _(pe):
                pe.wait_ge(s_init, 4)
                pe.wait_ge(s_wl, 16 * 10)
                pe.transpose(ps[:, 0, 0:P], pos_rows[:, 0, :], ident[:, :])
                pe.transpose(ps[:, 0, P:NT], pos_rows[0:NT - P, 1, :], ident[0:NT - P, 0:NT - P]).then_inc(s_posT, 1)
                with pe.Fori(0, UNITS // XB) as q:
                    for par in range(XB):
                        pe.wait_ge(s_half, q * XB + (par + 1))
                        pe.wait_ge(s_hemb, q * XB + (par + 1))
                        for j in range(8):
                            last = pe.matmul(ps[:, 2 + par, 0:2 * NP], wconv[0:KROWS1, j, :],
                                             patches[0:KROWS1, par, :, bass.ds(j, NP, step=PS)],
                                             start=(j == 0), stop=(j == 7))
                        last.then_inc(s_emb, 1)

            def shifted(par):
                return (patches[HALF:KROWS1, par, :, 0:XW - PS // 2], patches[0:CH * PS, par, :, PS // 2:XW])

            @block.scalar
            def _(sc):
                with sc.Fori(0, UNITS // XB) as q:
                    for par in range(XB):
                        sc.wait_ge(s_xl[par], VD((q, par), NXL))
                        sc.activation(*shifted(par), ACT.Copy).then_inc(s_half, 1)

            @block.vector
            def _(dve):
                dve.memset(wconv.rearrange("p a b -> p (a b)"), 0.0).then_inc(s_gap, 1)
                for par in range(XB):
                    dve.memset(patches[32:HALF, par].rearrange("p b n -> p (b n)"), 0.0).then_inc(s_gap, 1)
                dve.wait_ge(s_posT, 1)
                dve.tensor_scalar(posb[:, 1:NT], ps[:, 0, 1:NT], convb_col, None, ALU.add).then_inc(s_pose, 1)
                dve.tensor_scalar(h3[:, :, 0:1], cls_col.rearrange("p (a b) -> p a b", b=1).broadcast_to((P, B, 1)),
                                  ps[:, 0, 0:1], None, ALU.add).then_inc(s_hemb, 2)
                dve.wait_ge(s_pose, 1)
                with dve.Fori(0, UNITS // XB) as q:
                    for par in range(XB):
                        dve.wait_ge(s_emb, q * XB + (par + 1))
                        dst = h[:, bass.ds(q * (XB * T2) + par * T2, T2)].rearrange("p (b n) -> p b n", n=NT)
                        dve.tensor_tensor(dst[:, :, 1:NT],
                                          ps[:, 2 + par, 0:2 * NP].rearrange("p (b n) -> p b n", n=NP),
                                          posb[:, 1:NT].rearrange("p (a n) -> p a n", a=1).broadcast_to((P, 2, NP)),
                                          ALU.add).then_inc(s_hemb, 1)

        at[0] = 0
        stack = carve(2, HEADS, 2, T2, dt=BF16)
        vaug = carve(2, 2 * 2 * HEADS * 2 * HD)
        probs = carve(2, 2, HG, NT)
        onorm = carve(2, 2, T2)
        sums = carve(2, NT)
        rsum = carve(2, NT)
        negmax = carve(2, 2, HG)
        negres = carve(2, 2, HG)
        mparts = carve(2, 2, 32, dt=BF16)
        mrows = carve(2, NT + 1, dt=BF16)
        sq, rs, y = carve(T2), carve(T2), carve(T2)
        qk32 = carve(2, T2)
        res32 = carve(2, T2)
        parts = carve(2, 3, T2, dt=BF16)
        act = carve(2, T2)
        wqkv_raw = carve(3 * D)
        wqk_perm = carve(2, D)
        bqkv_row = carve(3 * D)
        bqk_perm = carve(2, D)
        wq_f, wk_f, wv_f = carve(D), carve(D), carve(D)
        wproj_pad = carve(2, D)
        wproj_raw = carve(D)
        wfc1_raw = carve(2 * D)
        wfc1_f = carve(2 * D)
        wfc2 = carve(2, D)
        wproj_next, wfc2_next = carve(2, D), carve(2, D)
        vecs = carve(8)
        bias = carve(8)
        msel = carve(HG, P, dt=BF16)
        L1W, L1B, L2W, L2B, PB, F2B, F1B = 0, 1, 2, 3, 4, 5, 6
        QB, KB, VB, HB, OB, FB = 0, 1, 2, 3, 5, 6
        Q_TERMS = (0, 0, 0, 1, 1, 2)
        K_TERMS = (0, 1, 2, 0, 1, 0)
        NLD = len(Q_TERMS)
        KROWS = HD * len(Q_TERMS)
        NW_PREP, NW_TAIL = 2 + 2, HG + 2 + 2 + 4 + 2

        vau = [vaug[:, p_, :].rearrange("p (b t h c) -> p b t h c", b=2, t=2, h=HEADS) for p_ in range(2)]

        for n_ in ("p_centered p_squared p_vared p_logged p_rstd p_normed p_qk_mm p_v_mm p_qk_out p_v_out "
                   "p_hi p_res p_mid p_lo t_projected t_added t_centered t_squared t_vared t_logged t_rstd "
                   "t_normed t_fc1 t_gelu t_fc2 t_done").split():
            sem(n_)
        for n_ in "a_scores a_max a_hi a_res a_mid a_lo a_mT a_mrows a_keys a_exp a_pv a_sums a_logsum a_rsum a_out".split():
            sem(n_)
        STEPS = 4
        PER = {"a_scores": 8, "a_max": 8, "a_keys": 8, "a_exp": 8}
        W = {n_: PER.get(n_, STEPS) if n_[:2] == "a_" else 1 for n_ in sems if n_[:2] in ("p_", "t_", "a_")}

        def credit(eng, names):
            for n_ in names.split():
                eng.sem_inc(sems[n_], CREDIT * W[n_])

        def done(eng, name, u, j=0):
            eng.wait_ge(sems[name], V(u, W[name], j))

        s_stacked = [sem("s_stacked0"), sem("s_stacked1")]
        s_wprep, s_wtail = sem("s_wprep"), sem("s_wtail")
        s_fprep, s_ftail = sem("s_fprep"), sem("s_ftail")
        s_mprep, s_mtail = sem("s_mprep"), sem("s_mtail")
        s_bprep, s_btail = sem("s_bprep"), sem("s_btail")
        s_zero = sem("s_zero")
        s_ones = sem("s_ones")
        s_sel = sem("s_sel")
        F_PREP, F_TAIL, M_TAIL, B_PREP, B_TAIL = 7, 3, 2, 2, 3

        def ticks(prep, tail):
            chain = (["p_center", "p_var", "p_qk", "p_v"] if prep else []) + (
                ["t_proj", "t_center", "t_var", "t_fc1", "t_fc2"] if tail else [])

            def link(i=STEPS):
                if chain and (prep or i > 0):
                    yield chain.pop(0), 0, 0, 0

            for i in range(STEPS):
                ahead = (0, i + 1) if i + 1 < STEPS else (1, 0) if prep else None
                behind = (0, i - 1) if i > 0 else (-1, STEPS - 1) if tail else None
                normed = (0, i - 2) if i > 1 else (-1, STEPS - 2 + i) if tail else None
                if ahead:
                    yield "scores", *ahead, 0
                yield "keys", 0, i, 0
                if normed:
                    yield "norm", *normed, 0
                yield from link(i)
                if ahead:
                    yield "scores", *ahead, 1
                    yield "max", *ahead, 0
                yield "keys", 0, i, 1
                if i != STEPS - 1:
                    yield from link(i)
                if behind:
                    yield "values", *behind, 0
                if ahead:
                    yield "mrow", *ahead, 0
                if i % 2 == 1:
                    yield from link()
            yield from ((c, 0, 0, 0) for c in chain)

        def begin():
            yield "scores", 0, 0, 0
            yield "scores", 0, 0, 1
            yield "max", 0, 0, 0
            yield "mrow", 0, 0, 0

        def layers(eng, prefetch, fold_prep, fold_tail, rnd, chain_only, run=lambda u, steps: None, at_block=lambda: None):
            def middle(base):
                with eng.Fori(0, PAIRS - 1) as it:
                    at_block()
                    rnd((base + it, 1, it), prep=True, tail=True)
                    rnd((base + it + 1, 0, it + 1), prep=True, tail=True)

            first, last = (0, 0, 0), (DEPTH * PAIRS - 1, 1, PAIRS - 1)
            fold_prep(0, None)
            fold_tail(0, None)
            chain_only(first, "prep")
            run(first, begin())
            rnd(first, prep=True, tail=False)
            with eng.Fori(0, DEPTH - 1) as L:
                base = L * PAIRS
                prefetch(L + 1)
                middle(base)
                fold_prep(L + 1, (base + PAIRS - 1, 1, PAIRS - 1))
                at_block()
                rnd((base + PAIRS - 1, 1, PAIRS - 1), prep=True, tail=True)
                rnd((base + PAIRS, 0, 0), prep=True, tail=True)
                fold_tail(L + 1, (base + PAIRS, 0, 0))
            middle((DEPTH - 1) * PAIRS)
            at_block()
            rnd(last, prep=False, tail=True)
            run(last, (("norm", 0, STEPS - 2, 0), ("values", 0, STEPS - 1, 0), ("norm", 0, STEPS - 1, 0)))
            chain_only(last, "tail")

        PREP = ("p_center", "p_var", "p_qk", "p_v")
        TAIL = ("t_proj", "t_center", "t_var", "t_fc1", "t_fc2")

        with nc.Block() as block:
            @block.sync
            def _(sp):
                def load_prep(L):
                    def put(dst, src):
                        sp.dma_start(dst, src).then_inc(s_wprep, 16)
                    put(wqkv_raw, qkv_w[bass.ds(L, 1)].rearrange("a k n -> (a k) n"))
                    put(bqkv_row[0:1], qkv_b[bass.ds(L, 1)])
                    for col, v in ((L1W, ln1_w), (L1B, ln1_b)):
                        put(vecs[:, col:col + 1], v[bass.ds(L, 1)].rearrange("a d -> d a"))

                def load_tail(L):
                    def put(dst, src):
                        sp.dma_start(dst, src).then_inc(s_wtail, 16)
                    pw = proj_w[bass.ds(L, 1)].rearrange("a (g i d) n -> (a i) d g n", g=2, i=HG)
                    for i in range(HG):
                        put(wproj_next[32 * i:32 * i + HD], pw[i])
                    put(wproj_raw, proj_w[bass.ds(L, 1)].rearrange("a k n -> (a k) n"))
                    put(wfc1_raw, fc1_w[bass.ds(L, 1)].rearrange("a k n -> (a k) n"))
                    f2 = fc2_w[bass.ds(L, 1)].rearrange("a (c k) n -> (a c) k n", c=2)
                    for c in range(2):
                        put(wfc2_next[:, c, :], f2[c])
                    for col, v in ((L2W, ln2_w), (L2B, ln2_b), (PB, proj_b), (F2B, fc2_b)):
                        put(vecs[:, col:col + 1], v[bass.ds(L, 1)].rearrange("a d -> d a"))
                    f1b = fc1_b[bass.ds(L, 1)].rearrange("a (c d) -> c d a", c=2)
                    for c in range(2):
                        put(vecs[:, F1B + c:F1B + c + 1], f1b[c])

                for par in range(2):
                    sp.sem_inc(s_stacked[par], 16 * NLD)
                sp.wait_ge(s_zero, 5)
                load_prep(0)
                load_tail(0)

                def prefetch(L):
                    sp.wait_ge(s_bprep, L * B_PREP)
                    passed(sp)
                    sp.wait_ge(s_btail, L * B_TAIL)
                    passed(sp)
                    load_prep(L)
                    load_tail(L)

                def move(u):
                    par = u[1]
                    for part, name in enumerate(("p_hi", "p_mid", "p_lo")):
                        done(sp, name, u)
                        passed(sp)
                        if part == 0:
                            done(sp, "a_keys", shift(u, -2), 7)
                            passed(sp)
                        for t, (qt, kt) in enumerate(zip(Q_TERMS, K_TERMS)):
                            if max(qt, kt) == part:
                                src = parts.rearrange("p a s n -> p (a s) n")[:, qt:4 + kt:3 + kt - qt]
                                dst = stack[t * HD:(t + 1) * HD, par].rearrange("d h s n -> d (h s) n")
                                sp.dma_start(dst, src).then_inc(s_stacked[par], 16)

                def chain_only(u, what):
                    if what == "prep":
                        move(u)

                def rnd(u, prep, tail):
                    if prep:
                        move(shift(u, 1))

                nothing = lambda L, u: None
                layers(sp, prefetch, nothing, nothing, rnd, chain_only)
                sp.wait_ge(s_stacked[0], VC((DEPTH * PAIRS - 1, 0, 0), NLD))
                sp.wait_ge(s_stacked[1], VC((DEPTH * PAIRS - 1, 1, 0), NLD))

            @block.gpsimd
            def _(pool):
                credit(pool, "p_hi p_res p_mid p_lo")
                pool.memset(vaug, 1.0).then_inc(s_ones, 1)
                pool.memset(msel, 0.0).then_inc(s_sel, 1)
                pool.wait_ge(s_sel, 1)
                for part in range(3):
                    pool.affine_select(out=msel, in_=msel, compare_op=ALU.not_equal, fill=1.0,
                                       base=-HG * part, pattern=[[-1, HG], [0, P]],
                                       channel_multiplier=1).then_inc(s_sel, 1)
                    pool.wait_ge(s_sel, part + 2)

                def split(u):
                    par = u[1]
                    done(pool, "p_qk_out", u)
                    pu = shift(u, -1)
                    pool.wait_ge(s_stacked[pu[1]], VC(pu, NLD))
                    passed(pool)
                    pool.tensor_scalar(parts[:, :, 0], qk32, 1.0, 0.0, ALU.mult, ALU.add).then_inc(sems["p_hi"], 1)
                    done(pool, "p_hi", u)
                    pool.tensor_tensor(res32, qk32, parts[:, :, 0], ALU.subtract).then_inc(sems["p_res"], 1)
                    done(pool, "p_res", u)
                    passed(pool)
                    pool.tensor_scalar(parts[:, :, 1], res32, 1.0, 0.0, ALU.mult, ALU.add).then_inc(sems["p_mid"], 1)
                    done(pool, "p_mid", u)
                    pool.tensor_tensor(parts[:, :, 2], res32, parts[:, :, 1], ALU.subtract).then_inc(sems["p_lo"], 1)

                def chain_only(u, what):
                    if what == "prep":
                        split(u)

                def rnd(u, prep, tail):
                    if prep:
                        split(shift(u, 1))

                nothing = lambda L, u: None
                layers(pool, lambda L: None, nothing, nothing, rnd, chain_only)

            @block.tensor
            def _(pe):
                credit(pe, "p_centered p_vared p_qk_mm p_v_mm t_projected t_centered t_vared t_fc1 t_fc2 "
                           "a_scores a_mT a_keys a_pv")
                pe.wait_ge(s_sel, 4)
                pe.wait_ge(s_ones, 1)
                pe.wait_ge(s_zero, 5)

                def fold_prep(L, u):
                    pe.wait_ge(s_fprep, L * F_PREP + F_PREP)
                    if u is not None:
                        done(pe, "t_done", shift(u, -2))
                    for col, w, b in ((QB, wqk_perm[:, 0], bqk_perm[:, 0]), (KB, wqk_perm[:, 1], bqk_perm[:, 1]),
                                      (VB, wqkv_raw[:, 2 * D:3 * D], bqkv_row[:, 2 * D:3 * D])):
                        pe.matmul(ps[:, 5, col:col + 1], w, vecs[:, L1B:L1B + 1], start=True, stop=False)
                        last = pe.matmul(ps[:, 5, col:col + 1], b, e0[:, :], start=False, stop=True)
                    last.then_inc(s_mprep, 1)
                    pe.wait_ge(s_bprep, L * B_PREP + B_PREP)

                def fold_tail(L, u):
                    pe.wait_ge(s_ftail, L * F_TAIL + F_TAIL)
                    if u is not None:
                        done(pe, "t_done", shift(u, -1))
                        done(pe, "p_qk_out", shift(u, 1))
                        done(pe, "p_v_out", shift(u, 1))
                    for c in range(2):
                        last = pe.matmul(ps[:, 5, HB + c:HB + c + 1], wfc1_raw[:, c * D:(c + 1) * D], vecs[:, L2B:L2B + 1],
                                         start=True, stop=True)
                    last.then_inc(s_mtail, 1)
                    pe.matmul(ps[:, 6, 0:1], wproj_raw, bias[:, VB:VB + 1], start=True, stop=True).then_inc(s_mtail, 1)
                    pe.wait_ge(s_btail, L * B_TAIL + B_TAIL)

                def chain(name, u, after):
                    par = u[1]
                    if name == "p_center":
                        done(pe, "t_done", shift(u, -3))
                        done(pe, "p_qk_out", shift(u, -1))
                        done(pe, "p_v_out", shift(u, -1))
                        if after is not None:
                            done(pe, "t_done", after)
                        pe.matmul(ps[:, 5, 0:T2], center[:, :], hu(u), start=True, stop=True).then_inc(sems["p_centered"], 1)
                    elif name == "p_var":
                        done(pe, "p_squared", u)
                        pe.matmul(ps[:, 6, 0:T2], mean[:, :], sq, start=True, stop=True).then_inc(sems["p_vared"], 1)
                    elif name == "p_qk":
                        done(pe, "p_normed", u)
                        pe.matmul(ps[:, 5, 0:T2], wq_f, y, start=True, stop=True)
                        pe.matmul(ps[:, 6, 0:T2], wk_f, y, start=True, stop=True).then_inc(sems["p_qk_mm"], 1)
                    elif name == "p_v":
                        done(pe, "p_qk_out", u)
                        for b in range(2):
                            for t in range(2):
                                last = pe.matmul(ps[0:KT[t], 5, (2 * b + t) * D:(2 * b + t + 1) * D],
                                                 y[:, b * NT + t * P:b * NT + t * P + KT[t]], wv_f, start=True, stop=True)
                        last.then_inc(sems["p_v_mm"], 1)
                    elif name == "t_proj":
                        done(pe, "p_v_out", after)
                        done(pe, "p_qk_out", after)
                        done(pe, "t_done", shift(u, -1))
                        done(pe, "a_out", u, STEPS - 1)
                        for g in range(2):
                            last = pe.matmul(ps[:, 5, 0:T2], wproj_pad[:, g, :], onorm[:, par, g, :], start=(g == 0), stop=(g == 1))
                        last.then_inc(sems["t_projected"], 1)
                    elif name == "t_center":
                        done(pe, "t_added", u)
                        pe.matmul(ps[:, 5, 0:T2], center[:, :], hu(u), start=True, stop=True).then_inc(sems["t_centered"], 1)
                    elif name == "t_var":
                        done(pe, "t_squared", u)
                        pe.matmul(ps[:, 6, 0:T2], mean[:, :], sq, start=True, stop=True).then_inc(sems["t_vared"], 1)
                    elif name == "t_fc1":
                        done(pe, "t_normed", u)
                        for c in range(2):
                            last = pe.matmul(ps[:, 5 + c, 0:T2], wfc1_f[:, c * D:(c + 1) * D], y, start=True, stop=True)
                        last.then_inc(sems["t_fc1"], 1)
                    elif name == "t_fc2":
                        done(pe, "t_gelu", u)
                        for c in range(2):
                            last = pe.matmul(ps[:, 5, 0:T2], wfc2[:, c, :], act[:, c, :], start=(c == 0), stop=(c == 1))
                        last.then_inc(sems["t_fc2"], 1)

                def attend(name, u, i, t):
                    par = u[1]
                    b, g = divmod(i, 2)
                    ap = i % 2
                    qs, ks = stack[0:KROWS, par, :, 0], stack[0:KROWS, par, :, 1]
                    if name == "scores":
                        if i == 0 and t == 0:
                            pe.wait_ge(s_stacked[par], VC(u, NLD))
                        done(pe, "a_max", u, 2 * i + t - 1)
                        for hh in range(HG):
                            last = pe.matmul(ps[0:KT[t], hh // 2, (hh % 2) * NT:(hh % 2 + 1) * NT],
                                             qs[:, HG * g + hh, b * NT + t * P:b * NT + t * P + KT[t]],
                                             ks[:, HG * g + hh, b * NT:(b + 1) * NT], start=True, stop=True)
                        last.then_inc(sems["a_scores"], 1)
                    elif name == "mrow":
                        done(pe, "a_lo", u, i)
                        done(pe, "a_mrows", u, i - 1)
                        for tt in range(2):
                            last = pe.matmul(ps[0:32, 7, tt * P:tt * P + KT[tt]], mparts[0:KT[tt], ap, tt, :],
                                             identb[0:KT[tt], 0:KT[tt]], start=True, stop=True)
                        last.then_inc(sems["a_mT"], 1)
                    elif name == "keys":
                        if t == 0:
                            done(pe, "a_mrows", u, i)
                        done(pe, "a_exp", u, 2 * i + t - 1)
                        for hh in range(HG):
                            o = ps[0:KT[t], 2 + hh // 2, (hh % 2) * NT:(hh % 2 + 1) * NT]
                            pe.matmul(o, ks[:, HG * g + hh, b * NT + t * P:b * NT + t * P + KT[t]],
                                      qs[:, HG * g + hh, b * NT:(b + 1) * NT], start=True, stop=False)
                            last = pe.matmul(o, msel[:, hh, 0:KT[t]], mrows[:, ap, 0:NT], start=False, stop=True)
                        last.then_inc(sems["a_keys"], 1)
                    elif name == "values":
                        done(pe, "a_exp", u, 2 * i + 1)
                        done(pe, "a_out", u, i - 1)
                        for t_ in range(2):
                            for hh in range(HG):
                                last = pe.matmul(ps[32 * hh:32 * hh + 32, 4, 0:NT], vau[par][0:KT[t_], b, t_, HG * g + hh, :],
                                                 probs[0:KT[t_], ap, t_, hh, :], start=(t_ == 0), stop=(t_ == 1))
                        last.then_inc(sems["a_pv"], 1)

                def chain_only(u, what):
                    for name in (PREP if what == "prep" else TAIL):
                        chain(name, u, shift(u, -1) if what == "prep" else u)

                def run(u, steps):
                    for name, d, i, t in steps:
                        attend(name, shift(u, d), i, t)

                def rnd(u, prep, tail):
                    for name, d, i, t in ticks(prep, tail):
                        if name in PREP:
                            chain(name, shift(u, 1), None)
                        elif name in TAIL:
                            chain(name, shift(u, -1), shift(u, 1) if prep else u)
                        else:
                            attend(name, shift(u, d), i, t)

                layers(pe, lambda L: None, fold_prep, fold_tail, rnd, chain_only, run)

            @block.scalar
            def _(sc):
                credit(sc, "p_squared p_logged p_rstd p_qk_out t_squared t_logged t_rstd t_gelu "
                           "a_exp a_logsum a_rsum")

                def fold_prep(L, u):
                    exp_ln_tables()
                    sc.wait_ge(s_bprep, L * B_PREP + B_PREP)
                    passed(sc)

                def fold_tail(L, u):
                    sc.wait_ge(s_btail, L * B_TAIL + B_TAIL)
                    passed(sc)

                def exp_ln_tables():
                    sc.preload_act_table_set("natural_log_exp_and_others")

                def rstd(pre, u):
                    done(sc, pre + "_vared", u)
                    sc.activation(rs, ps[:, 6, 0:T2], ACT.Ln, bias=eps_col[:, :]).then_inc(sems[pre + "_logged"], 1)
                    done(sc, pre + "_logged", u)
                    sc.activation(rs, rs, ACT.Exp, scale=-0.5).then_inc(sems[pre + "_rstd"], 1)

                def chain(name, u):
                    if name == "p_center" or name == "t_center":
                        pre = name[0]
                        done(sc, pre + "_centered", u)
                        sc.activation(sq, ps[:, 5, 0:T2], ACT.Square).then_inc(sems[pre + "_squared"], 1)
                    elif name == "p_var" or name == "t_var":
                        rstd(name[0], u)
                    elif name == "p_qk":
                        done(sc, "p_qk_mm", u)
                        done(sc, "p_lo", shift(u, -1))
                        sc.activation(qk32[:, 0, :], ps[:, 5, 0:T2], ACT.Identity, bias=bias[:, QB:QB + 1], scale=SCALE)
                        sc.activation(qk32[:, 1, :], ps[:, 6, 0:T2], ACT.Identity, bias=bias[:, KB:KB + 1]).then_inc(sems["p_qk_out"], 1)
                    elif name == "t_fc1":
                        done(sc, "t_fc1", u)
                        sc.activation(act[:, 0, :], ps[:, 5, 0:T2], ACT.Gelu, bias=bias[:, HB:HB + 1])
                        sc.activation(act[:, 1, :], ps[:, 6, 0:T2], ACT.Gelu, bias=bias[:, HB + 1:HB + 2]).then_inc(sems["t_gelu"], 1)
                        exp_ln_tables()

                def attend(name, u, i, t):
                    ap = i % 2
                    if name == "keys":
                        done(sc, "a_keys", u, 2 * i + t)
                        done(sc, "a_pv", u, i - 2)
                        sc.activation(probs[0:KT[t], ap, t].rearrange("p (a b) n -> p a (b n)", a=2),
                                      ps[0:KT[t], 2:4, 0:2 * NT], ACT.Exp).then_inc(sems["a_exp"], 1)
                    elif name == "values":
                        done(sc, "a_sums", u, i)
                        done(sc, "a_out", u, i - 2)
                        sc.activation(rsum[:, ap], sums[:, ap], ACT.Ln).then_inc(sems["a_logsum"], 1)
                        done(sc, "a_logsum", u, i)
                        sc.activation(rsum[:, ap], rsum[:, ap], ACT.Exp, scale=-1.0).then_inc(sems["a_rsum"], 1)

                def chain_only(u, what):
                    for name in (PREP if what == "prep" else TAIL):
                        chain(name, u)

                def run(u, steps):
                    for name, d, i, t in steps:
                        attend(name, shift(u, d), i, t)

                def rnd(u, prep, tail):
                    for name, d, i, t in ticks(prep, tail):
                        if name in PREP:
                            chain(name, shift(u, 1))
                        elif name in TAIL:
                            chain(name, shift(u, -1))
                        else:
                            attend(name, shift(u, d), i, t)

                layers(sc, lambda L: None, fold_prep, fold_tail, rnd, chain_only, run, exp_ln_tables)

            @block.vector
            def _(dve):
                credit(dve, "p_normed p_v_out t_added t_normed t_done a_max a_hi a_res a_mid a_lo a_mrows a_sums a_out")
                for z in (negmax, mparts, mrows):
                    dve.memset(z, 0.0).then_inc(s_zero, 1)
                dve.memset(wproj_next, 0.0).then_inc(s_zero, 1)
                dve.memset(bqkv_row, 0.0).then_inc(s_zero, 1)

                def fold_prep(L, u):
                    dve.wait_ge(s_wprep, L * (16 * NW_PREP) + 16 * NW_PREP)
                    for s_ in range(2):
                        dve.tensor_copy(wqk_perm[:, s_].rearrange("p (d h) -> p d h", h=HEADS),
                                        wqkv_raw[:, s_ * D:(s_ + 1) * D].rearrange("p (h d) -> p d h", h=HEADS)).then_inc(s_fprep, 1)
                        dve.tensor_copy(bqk_perm[:, s_].rearrange("p (d h) -> p d h", h=HEADS),
                                        bqkv_row[:, s_ * D:(s_ + 1) * D].rearrange("p (h d) -> p d h", h=HEADS)).then_inc(s_fprep, 1)
                    dve.wait_ge(s_fprep, L * F_PREP + 4)
                    for dst, src in ((wq_f, wqk_perm[:, 0]), (wk_f, wqk_perm[:, 1]), (wv_f, wqkv_raw[:, 2 * D:3 * D])):
                        dve.tensor_scalar(dst, src, vecs[:, L1W:L1W + 1], None, ALU.mult).then_inc(s_fprep, 1)
                    dve.wait_ge(s_mprep, L + 1)
                    dve.tensor_scalar(bias[:, QB:QB + 1], ps[:, 5, QB:QB + 1], SCALE, None, ALU.mult).then_inc(s_bprep, 1)
                    dve.tensor_copy(bias[:, KB:VB + 1], ps[:, 5, KB:VB + 1]).then_inc(s_bprep, 1)

                def fold_tail(L, u):
                    dve.wait_ge(s_wtail, L * (16 * NW_TAIL) + 16 * NW_TAIL)
                    dve.tensor_scalar(wfc1_f, wfc1_raw, vecs[:, L2W:L2W + 1], None, ALU.mult).then_inc(s_ftail, 1)
                    dve.tensor_copy(wproj_pad, wproj_next).then_inc(s_ftail, 1)
                    dve.tensor_copy(wfc2, wfc2_next).then_inc(s_ftail, 1)
                    dve.wait_ge(s_mtail, L * M_TAIL + 1)
                    dve.tensor_tensor(bias[:, HB:HB + 2], ps[:, 5, HB:HB + 2], vecs[:, F1B:F1B + 2], ALU.add).then_inc(s_btail, 1)
                    dve.tensor_copy(bias[:, FB:FB + 1], vecs[:, F2B:F2B + 1]).then_inc(s_btail, 1)
                    dve.wait_ge(s_mtail, L * M_TAIL + 2)
                    dve.tensor_tensor(bias[:, OB:OB + 1], ps[:, 6, 0:1], vecs[:, PB:PB + 1], ALU.add).then_inc(s_btail, 1)
                    dve.wait_ge(s_btail, L * B_TAIL + B_TAIL)

                def chain(name, u):
                    par = u[1]
                    if name == "p_var" or name == "t_var":
                        pre = name[0]
                        done(dve, pre + "_rstd", u)
                        dve.tensor_tensor(y, ps[:, 5, 0:T2], rs, ALU.mult).then_inc(sems[pre + "_normed"], 1)
                    elif name == "p_v":
                        done(dve, "p_v_mm", u)
                        done(dve, "a_pv", shift(u, -2), STEPS - 1)
                        for t in range(2):
                            src = ps[0:KT[t], 5, :].rearrange("p (b t h c) -> p b t h c", b=2, t=2, h=HEADS)[:, :, t]
                            for b in range(2):
                                last = dve.tensor_copy(vau[par][0:KT[t], b, t, :, 0:HD], src[:, b])
                        last.then_inc(sems["p_v_out"], 1)
                    elif name == "t_proj":
                        done(dve, "t_projected", u)
                        dve.scalar_tensor_tensor(hu(u), ps[:, 5, 0:T2], bias[:, OB:OB + 1], hu(u), ALU.add, ALU.add).then_inc(sems["t_added"], 1)
                    elif name == "t_fc2":
                        done(dve, "t_fc2", u)
                        dve.scalar_tensor_tensor(hu(u), ps[:, 5, 0:T2], bias[:, FB:FB + 1], hu(u), ALU.add, ALU.add).then_inc(sems["t_done"], 1)

                def attend(name, u, i, t):
                    par = u[1]
                    b, g = divmod(i, 2)
                    ap = i % 2
                    mp = mparts[:, ap]
                    if name == "scores":
                        done(dve, "a_scores", u, 2 * i + t)
                        dve.tensor_reduce(negmax[0:KT[t], ap, t], ps[0:KT[t], 0:2, 0:2 * NT].rearrange(
                            "p a (b n) -> p a b n", b=2), AX.X, ALU.max, negate=True).then_inc(sems["a_max"], 1)
                    elif name == "max":
                        done(dve, "a_max", u, 2 * i + 1)
                        done(dve, "a_mT", u, i - 2)
                        dve.tensor_copy(mp[:, :, 0:HG], negmax[:, ap]).then_inc(sems["a_hi"], 1)
                        done(dve, "a_hi", u, i)
                        dve.tensor_tensor(negres[:, ap], negmax[:, ap], mp[:, :, 0:HG], ALU.subtract).then_inc(sems["a_res"], 1)
                        done(dve, "a_res", u, i)
                        dve.tensor_copy(mp[:, :, HG:2 * HG], negres[:, ap]).then_inc(sems["a_mid"], 1)
                        done(dve, "a_mid", u, i)
                        dve.tensor_tensor(mp[:, :, 2 * HG:3 * HG], negres[:, ap], mp[:, :, HG:2 * HG], ALU.subtract).then_inc(sems["a_lo"], 1)
                    elif name == "mrow":
                        done(dve, "a_mT", u, i)
                        done(dve, "a_keys", u, 2 * (i - 2) + 1)
                        dve.tensor_copy(mrows[0:32, ap, 0:NT], ps[0:32, 7, 0:NT]).then_inc(sems["a_mrows"], 1)
                    elif name == "values":
                        done(dve, "a_pv", u, i)
                        done(dve, "a_logsum", u, i - 2)
                        passed(dve)
                        dve.stream_shuffle(sums[:, ap], ps[:, 4, 0:NT], [HD + k % HD for k in range(32)]).then_inc(sems["a_sums"], 1)
                    elif name == "norm":
                        done(dve, "a_rsum", u, i)
                        done(dve, "t_projected", shift(u, -2))
                        dve.tensor_tensor(onorm[:, par, g, b * NT:(b + 1) * NT], ps[:, 4, 0:NT], rsum[:, ap], ALU.mult).then_inc(sems["a_out"], 1)

                def chain_only(u, what):
                    for name in (PREP if what == "prep" else TAIL):
                        chain(name, u)

                def run(u, steps):
                    for name, d, i, t in steps:
                        attend(name, shift(u, d), i, t)

                def rnd(u, prep, tail):
                    for name, d, i, t in ticks(prep, tail):
                        if name in PREP:
                            chain(name, shift(u, 1))
                        elif name in TAIL:
                            chain(name, shift(u, -1))
                        else:
                            attend(name, shift(u, d), i, t)

                layers(dve, lambda L: None, fold_prep, fold_tail, rnd, chain_only, run)

        at[0] = 0
        txt_rows = carve(2, D)
        hc, skip, yn = carve(S2), carve(S2), carve(S2)
        zz = carve(2, S2)
        sq3, rs3 = carve(S2), carve(S2)
        PADW = TAPS - 1
        xpad = carve(2, 2, S + 2 * PADW)
        cv = carve(2, S2)
        ex, op, lg = carve(2 * S2), carve(2 * S2), carve(2 * S2)
        lz = carve(S2)
        dbc = carve(2, S2)
        bres = carve(2, S2)
        uu = carve(2, 2, S2)
        delta = carve(2, 2, S2)
        du = carve(2, 2, S2)
        bcs = carve(2, 2, S2, dt=BF16)
        zg = carve(2, S2)
        tres = carve(UNITS, 2 * TXT)
        decay = carve(2, 2, S2)
        brep = carve(2, 2, S2)
        inp = carve(2, 2, S2)
        state = carve(2, 2, S2)
        prod = carve(2, 2, S2)
        pair = carve(2, 2, S2)
        h1 = carve(S2)
        gl = carve(S2)
        rows = carve(2 * 2, D)
        wp_raw, wp_f = carve(2 * D), carve(2 * D)
        wx_pad = carve(D)
        wdt_pad = carve(D)
        w1_raw, w2_raw, w1T, w2T = carve(D), carve(D), carve(D), carve(D)
        diagD = carve(D)
        amat = carve(NS)
        alog = carve(NS)
        mvec = carve(16)
        taps = carve(TAPS)
        bxz = carve(2)
        bsel = carve(2 * NS, P, dt=BF16)
        NW, NB, LG, LB, CB, DTB, DV, B1, B2 = range(9)

        for n_ in ("n_centered n_squared n_vared n_logged n_rstd n_scaled n_normed n_txt n_txt_out "
                   "k_centered k_squared k_vared k_logged k_rstd k_normed k_res "
                   "g_centered g_squared g_vared g_logged g_rstd g_normed xz_mm xz_out conv_step "
                   "su_abs su_exp su_one su_ln su_err su_cor su_out dbc_mm dbc_out b_hi b_res b_mid b_lo dt_mm dt_out "
                   "sd_abs sd_exp sd_one sd_ln sd_err sd_cor sd_out du_out "
                   "z_abs z_exp z_ln z_arg z_sig z_out "
                   "f_gated f_added f_centered f_squared f_vared f_logged f_rstd f_normed f_mm1 f_gelu f_mm2 f_out f_T f_rows").split():
            sem(n_)
            W[n_] = 2 * TAPS if n_ == "conv_step" else 1
        for n_ in ("dbc_mm", "dbc_out", "dt_mm", "dt_out"):
            W[n_] = 2
        for n_ in "m_b m_brep m_inp m_c m_decay m_scan m_prod m_pair m_sum".split():
            sem(n_)
            W[n_] = NS // 2 if n_ in ("m_pair", "m_sum") else NS
        s_txt = [sem("s_txt0"), sem("s_txt1")]
        s_stored = [sem("s_stored0"), sem("s_stored1")]
        s_w3, s_set, s_set2, s_mm3, s_ev3, s_neg = (sem(n_) for n_ in "s_w3 s_set s_set2 s_mm3 s_ev3 s_neg".split())
        NORMS = ("n_center", "n_var", "n_norm", "txt", "k_center", "k_var", "k_norm", "g_center", "g_var", "g_norm")
        INNER = ("xz", "conv0", "conv1", "conv2", "conv3", "su1", "su2", "su_err", "su3", "dbc", "dt", "split0", "split1",
                 "split2", "split3", "sd1", "sd2", "sd_err", "sd3", "du", "z1", "z2", "z_arg", "z3", "z_gate")
        POST = ("gate", "f_center", "f_var", "f_norm", "f_1", "f_2", "f_add", "f_T")
        BETWEEN = (("xz",), ("conv0", "conv1"), ("gate", "conv2", "conv3"), ("f_center", "su1"), ("f_var", "su2"),
                   ("f_norm", "su_err"), ("f_1", "su3", "z1"), ("dbc", "z2"), ("dt", "n_center", "split0"),
                   ("n_var", "f_2", "sd1", "split1"), ("f_add", "n_norm", "txt", "sd2", "split2", "z_arg"),
                   ("f_T", "k_center", "sd_err", "split3"), ("k_var", "sd3"), ("k_norm", "du"), ("g_center", "z3"),
                   ("g_var", "z_gate", "g_norm"))
        assert TAPS == 4 and NS == len(BETWEEN)
        assert sorted(NORMS + INNER + POST) == sorted(c for cs in BETWEEN for c in cs)
        AHEAD = 2

        def ticks3(norms, inner, post):
            for n in range(NS):
                yield "step", 0, n
                if n > 0 or post:
                    yield ("product", 0, n - 1) if n > 0 else ("product", -1, NS - 1)
                ahead = (0, n + AHEAD) if n + AHEAD < NS else (1, n + AHEAD - NS) if inner else None
                if ahead:
                    yield "ahead", *ahead
                for c in BETWEEN[n]:
                    if c in NORMS and norms:
                        yield c, 2, 0
                    if c in INNER and inner:
                        yield c, 1, 0
                    if c in POST and post:
                        yield c, -1, 0
                if n % 2 == 1 and (n > 1 or post):
                    yield ("sum", 0, n // 2 - 1) if n > 1 else ("sum", -1, NS // 2 - 1)

        def fusion(eng, run, at_block=lambda: None):
            first, last = (0, 0, 0), (PAIRS - 1, 1, PAIRS - 1)
            run(first, ((c, 0, 0) for c in NORMS + INNER))
            run(first, ((c, 1, 0) for c in NORMS))
            run(first, (("ahead", 0, n) for n in range(AHEAD)))
            run(first, ticks3(norms=True, inner=True, post=False))
            with eng.Fori(0, PAIRS - 2) as it:
                at_block()
                run((it, 1, it), ticks3(norms=True, inner=True, post=True))
                run((it + 1, 0, it + 1), ticks3(norms=True, inner=True, post=True))
            at_block()
            run(shift(last, -2), ticks3(norms=True, inner=True, post=True))
            run(shift(last, -1), ticks3(norms=False, inner=True, post=True))
            run(last, ticks3(norms=False, inner=False, post=True))
            run(last, (("product", 0, NS - 1), ("sum", 0, NS // 2 - 1)))
            run(last, ((c, 0, 0) for c in POST))

        def images(ap, n=S):
            return ap.rearrange("p (b n) -> p b n", n=n)

        def flat(ap):
            return ap.rearrange("p a n -> p (a n)")

        def tu(u):
            q, par = u[:2]
            return tres.rearrange("p u n -> p (u n)")[:, bass.ds(q * (4 * TXT) + par * (2 * TXT), 2 * TXT)].rearrange(
                "p (b n) -> p b n", b=2)

        with nc.Block() as block:
            @block.sync
            def _(sp):
                for par in range(2):
                    sp.sem_inc(s_stored[par], 16 * 2)
                sp.wait_ge(s_set, 7)
                def put(dst, src):
                    sp.dma_start(dst, src).then_inc(s_w3, 16)
                put(wp_raw, m_W_proj)
                put(wx_pad[:, 0:RANK + 2 * NS], m_W_x)
                put(wx_pad[:, 2 * RANK:3 * RANK], m_W_x[:, RANK:RANK + 2 * NS])
                put(wx_pad[:, 3 * RANK:4 * RANK], m_W_x[:, RANK:RANK + 2 * NS])
                put(wdt_pad[0:RANK], m_W_dt)
                put(w1_raw, f_W1)
                put(w2_raw, f_W2)
                put(alog, m_A_log)
                put(taps, m_conv_w.rearrange("d a k -> d (a k)"))
                for col, v in ((NW, norm_w), (NB, norm_b), (LG, m_ln_g), (LB, m_ln_b), (CB, m_conv_b), (DTB, m_b_dt),
                               (DV, m_D), (B1, f_b1), (B2, f_b2)):
                    put(mvec[:, col:col + 1], v.rearrange("(d a) -> d a", a=1))

                def load_txt(u):
                    q, par = u[:2]
                    done(sp, "n_txt", shift(u, -2))
                    src = txt[bass.ds(q * 4 + 2 * par, 2)].rearrange("b n d -> (b n) d")
                    sp.dma_start(txt_rows[0:2 * TXT, par, :], src).then_inc(s_txt[par], 16)

                def store(u):
                    q, par = u[:2]
                    done(sp, "f_rows", u)
                    o = out[bass.ds(q * 4 + 2 * par, 2)].rearrange("b n d -> n b d")
                    r = rows.rearrange("p (b t) d -> p b t d", b=2)
                    sp.dma_start(o[0:P], r[:, :, 0]).then_inc(s_stored[par], 16)
                    sp.dma_start(o[P:S], r[0:S - P, :, 1]).then_inc(s_stored[par], 16)

                def run(u, steps):
                    for name, d, n in steps:
                        if name == "n_center":
                            load_txt(shift(u, d))
                        elif name == "f_T":
                            store(shift(u, d))

                fusion(sp, run)
                for par in range(2):
                    sp.wait_ge(s_stored[par], VC((PAIRS - 1, par, 0), 2))

            @block.gpsimd
            def _(pool):
                credit(pool, "su_one su_cor sd_one sd_cor b_hi b_res b_mid b_lo du_out m_inp")
                for z in (txt_rows, xpad.rearrange("p k b n -> p (k b n)"), wdt_pad, diagD, bsel, flat(decay[:, 0]), flat(decay[:, 1])):
                    pool.memset(z, 0.0).then_inc(s_set, 1)
                pool.memset(bcs.rearrange("p a b n -> p (a b n)"), 0.0).then_inc(s_set2, 1)
                pool.wait_ge(s_set, 7)
                for k in range(3):
                    pool.affine_select(out=bsel, in_=bsel, compare_op=ALU.not_equal, fill=1.0, base=-32 * (k + 1),
                                       pattern=[[-1, 2 * NS], [0, P]], channel_multiplier=1).then_inc(s_set2, 1)
                    pool.wait_ge(s_set2, k + 2)
                pool.wait_ge(s_w3, 16 * 18)
                for w in (w1_raw, w2_raw):
                    pool.affine_select(out=w, in_=w, compare_op=ALU.is_ge, fill=0.0, base=0,
                                       pattern=[[-1, D]], channel_multiplier=1).then_inc(s_set2, 1)

                def alone(u, before):
                    done(pool, *before)
                    passed(pool)

                def chain(name, u, before):
                    par = u[1]
                    bc = bcs[:, par]
                    if name in ("su1", "sd1"):
                        pre = name[:2]
                        done(pool, pre + "_exp", u)
                        passed(pool)
                        pool.tensor_scalar(op, ex, 1.0, 1.0, ALU.mult, ALU.add).then_inc(sems[pre + "_one"], 1)
                    elif name in ("su_err", "sd_err"):
                        pre = name[:2]
                        done(pool, pre + "_ln", u)
                        done(pool, pre + "_err", u)
                        pool.tensor_tensor(lg, lg, op, ALU.subtract).then_inc(sems[pre + "_cor"], 1)
                    elif name == "split0":
                        done(pool, "dbc_out", u, 1)
                        done(pool, "m_c", shift(u, -2), NS - 1)
                        passed(pool)
                        pool.tensor_scalar(bc, dbc, 1.0, 0.0, ALU.mult, ALU.add).then_inc(sems["b_hi"], 1)
                    elif name == "split1":
                        done(pool, "b_hi", u)
                        alone(u, before)
                        pool.tensor_tensor(bres[64:P], dbc[64:P], bc[64:P], ALU.subtract).then_inc(sems["b_res"], 1)
                        alone(u, ("b_res", u))
                    elif name == "split2":
                        alone(u, before)
                        pool.tensor_scalar(bc[64:P], bres[64:P], 1.0, 0.0, ALU.mult, ALU.add).then_inc(sems["b_mid"], 1)
                        alone(u, ("b_mid", u))
                    elif name == "split3":
                        alone(u, before)
                        pool.tensor_tensor(bc[96:P], bres[96:P], bc[96:P], ALU.subtract).then_inc(sems["b_lo"], 1)
                        alone(u, ("b_lo", u))
                    elif name == "z_gate":
                        done(pool, "z_sig", u)
                        done(pool, "f_gated", shift(u, -2))
                        pool.tensor_tensor(zg[:, par], zz[:, par], lz, ALU.mult).then_inc(sems["z_out"], 1)
                    elif name == "du":
                        done(pool, "sd_out", u)
                        pool.tensor_tensor(flat(du[:, par]), flat(delta[:, par]), flat(uu[:, par]), ALU.mult).then_inc(sems["du_out"], 1)

                def inputs(u, n):
                    par = u[1]
                    if n == 0:
                        done(pool, "du_out", u)
                    done(pool, "m_brep", u, n)
                    done(pool, "m_scan", u, n - 2)
                    pool.tensor_tensor(flat(inp[:, n % 2]), flat(du[:, par]), flat(brep[:, n % 2]), ALU.mult).then_inc(sems["m_inp"], 1)

                signal = {"su1": "su_one", "sd1": "sd_one", "su_err": "su_cor", "sd_err": "sd_cor", "split0": "b_hi",
                          "split1": "b_res", "split2": "b_mid", "split3": "b_lo", "du": "du_out",
                          "z_gate": "z_out"}

                def run(u, steps):
                    before = ("m_inp", u, 0)
                    for name, d, n in steps:
                        v = shift(u, d)
                        if name == "ahead":
                            inputs(v, n)
                            before = ("m_inp", v, n)
                        elif name in signal:
                            chain(name, v, before)
                            before = (signal[name], v)

                fusion(pool, run)

            @block.tensor
            def _(pe):
                credit(pe, "n_centered n_vared n_txt k_centered k_vared g_centered g_vared xz_mm dbc_mm dt_mm "
                           "f_centered f_vared f_mm1 f_mm2 f_T m_b m_c m_sum")
                pe.wait_ge(s_set, 7)
                pe.wait_ge(s_w3, 16 * 18)
                pe.wait_ge(s_set2, 6)
                pe.matmul(ps[:, 6, 0:1], wp_raw[:, 0:D], mvec[:, LB:LB + 1], start=True, stop=True)
                pe.matmul(ps[:, 6, 1:2], wp_raw[:, D:2 * D], mvec[:, LB:LB + 1], start=True, stop=True)
                pe.transpose(ps[:, 7, 0:D], w1_raw, ident[:, :])
                pe.transpose(ps[:, 7, D:2 * D], w2_raw, ident[:, :]).then_inc(s_mm3, 1)
                pe.wait_ge(s_ev3, 6)

                def center_of(src, pre):
                    pe.matmul(ps[:, 6, 0:src.shape[-1]], center[:, :], src, start=True, stop=True).then_inc(sems[pre + "_centered"], 1)

                def var_of(n, pre, u):
                    done(pe, pre + "_squared", u)
                    pe.matmul(ps[:, 7, 0:n], mean[:, :], sq3[:, 0:n], start=True, stop=True).then_inc(sems[pre + "_vared"], 1)

                def chain(name, u):
                    par = u[1]
                    if name == "n_center":
                        done(pe, "f_gelu", shift(u, -3))
                        done(pe, "xz_out", shift(u, -1))
                        center_of(hu(u), "n")
                    elif name == "n_var":
                        done(pe, "dt_out", shift(u, -1), 1)
                        var_of(T2, "n", u)
                    elif name == "txt":
                        pe.wait_ge(s_txt[par], VD(u, 1))
                        done(pe, "n_logged", u)
                        pe.transpose(ps[:, 7, 0:P], txt_rows[:, par, :], ident[:, :]).then_inc(sems["n_txt"], 1)
                    elif name == "k_center":
                        done(pe, "n_normed", u)
                        done(pe, "n_txt_out", u)
                        center_of(hc, "k")
                    elif name == "k_var":
                        var_of(S2, "k", u)
                    elif name == "g_center":
                        done(pe, "k_normed", u)
                        center_of(skip, "g")
                    elif name == "g_var":
                        var_of(S2, "g", u)
                    elif name == "xz":
                        done(pe, "g_normed", u)
                        for k in range(2):
                            last = pe.matmul(ps[:, 6 + k, 0:S2], wp_f[:, k * D:(k + 1) * D], yn, start=True, stop=True)
                        last.then_inc(sems["xz_mm"], 1)
                    elif name in ("dbc", "dt"):
                        for k in range(2):
                            if name == "dbc" and k == 0:
                                done(pe, "dt_out", shift(u, -1), 1)
                                done(pe, "f_rows", shift(u, -3))
                                done(pe, "f_normed", shift(u, -2))
                                done(pe, "su_out", u)
                            elif name == "dt" and k == 0:
                                done(pe, "dbc_out", u, 1)
                            w, src = (wx_pad, uu[:, par, k, :]) if name == "dbc" else (wdt_pad, dbc[:, k, :])
                            pe.matmul(ps[:, 5 + 2 * k, 0:S2], w, src, start=True, stop=True).then_inc(sems[name + "_mm"], 1)
                    elif name == "f_center":
                        done(pe, "f_added", u)
                        if not isinstance(u[0], int) or u[0] < PAIRS - 1:
                            done(pe, "xz_out", shift(u, 2))
                        done(pe, "f_rows", shift(u, -1))
                        center_of(h1, "f")
                    elif name == "f_var":
                        var_of(S2, "f", u)
                    elif name == "f_1":
                        done(pe, "f_normed", u)
                        pe.matmul(ps[:, 6, 0:S2], w1T, yn, start=True, stop=True).then_inc(sems["f_mm1"], 1)
                    elif name == "f_2":
                        done(pe, "f_gelu", u)
                        if not isinstance(u[0], int) or u[0] < PAIRS - 1:
                            done(pe, "dt_out", shift(u, 2), 1)
                        pe.matmul(ps[:, 5, 0:S2], w2T, gl, start=True, stop=True).then_inc(sems["f_mm2"], 1)
                    elif name == "f_T":
                        done(pe, "f_out", u)
                        for b in range(2):
                            for t in range(2):
                                m = P if t == 0 else S - P
                                last = pe.transpose(ps[0:m, 5, (2 * b + t) * D:(2 * b + t + 1) * D],
                                                    h1[:, b * S + t * P:b * S + t * P + m], ident[:, :])
                        last.then_inc(sems["f_T"], 1)

                def rep_b(u, n):
                    if n == 0:
                        done(pe, "b_lo", u)
                    done(pe, "m_brep", u, n - 1)
                    for k in range(2):
                        last = pe.matmul(ps[:, k, 0:S2], bsel[:, n, :], bcs[:, u[1], k, :], start=True, stop=True)
                    last.then_inc(sems["m_b"], 1)

                def rep_c(u, n):
                    done(pe, "m_prod", u, n - 1)
                    for k in range(2):
                        last = pe.matmul(ps[:, 2 + k, 0:S2], bsel[:, NS + n, :], bcs[:, u[1], k, :], start=True, stop=True)
                    last.then_inc(sems["m_c"], 1)

                def add_up(u, m):
                    par = u[1]
                    if m == 0:
                        done(pe, "f_gated", shift(u, -1))
                        pe.matmul(ps[:, 4, 0:S2], diagD, uu[:, par, 0, :], start=True, stop=False)
                        pe.matmul(ps[:, 4, 0:S2], diagD, uu[:, par, 1, ::-1], start=False, stop=False)
                    done(pe, "m_pair", u, m)
                    pe.matmul(ps[:, 4, 0:S2], ident[:, :], pair[:, m % 2, 0, :], start=False, stop=False)
                    pe.matmul(ps[:, 4, 0:S2], ident[:, :], pair[:, m % 2, 1, ::-1], start=False,
                              stop=(m == NS // 2 - 1)).then_inc(sems["m_sum"], 1)

                def run(u, steps):
                    for name, d, n in steps:
                        v = shift(u, d)
                        if name == "ahead":
                            rep_b(v, n)
                        elif name == "product":
                            rep_c(v, n)
                        elif name == "sum":
                            add_up(v, n)
                        else:
                            chain(name, v)

                fusion(pe, run)

            @block.scalar
            def _(sc):
                credit(sc, "n_squared n_logged n_rstd k_squared k_logged k_rstd g_squared g_logged g_rstd xz_out "
                           "su_abs su_exp su_ln dbc_out dt_out sd_abs sd_exp sd_ln z_abs z_exp z_ln z_sig "
                           "f_squared f_logged f_rstd f_gelu f_rows m_brep m_decay")

                def exp_ln_tables():
                    sc.preload_act_table_set("natural_log_exp_and_others")

                exp_ln_tables()
                sc.wait_ge(s_w3, 16 * 18)
                sc.wait_ge(s_mm3, 1)
                sc.activation(w1T, ps[:, 7, 0:D], ACT.Copy).then_inc(s_ev3, 1)
                sc.activation(w2T, ps[:, 7, D:2 * D], ACT.Copy).then_inc(s_ev3, 1)
                sc.activation(alog, alog, ACT.Exp).then_inc(s_neg, 1)
                sc.wait_ge(s_neg, 1)
                sc.activation(amat, alog, ACT.Copy, scale=-1.0).then_inc(s_neg, 1)
                sc.wait_ge(s_neg, 2)
                sc.wait_ge(s_ev3, 6)

                def squared(n, pre, u):
                    done(sc, pre + "_centered", u)
                    sc.activation(sq3[:, 0:n], ps[:, 6, 0:n], ACT.Square).then_inc(sems[pre + "_squared"], 1)

                def rstd(n, pre, u):
                    done(sc, pre + "_vared", u)
                    sc.activation(rs3[:, 0:n], ps[:, 7, 0:n], ACT.Ln, bias=eps_col[:, :]).then_inc(sems[pre + "_logged"], 1)
                    done(sc, pre + "_logged", u)
                    sc.activation(rs3[:, 0:n], rs3[:, 0:n], ACT.Exp, scale=-0.5).then_inc(sems[pre + "_rstd"], 1)

                def exp_neg_abs(dst, src, pre, u):
                    sc.activation(dst, src, ACT.Abs).then_inc(sems[pre + "_abs"], 1)
                    done(sc, pre + "_abs", u)
                    sc.activation(dst, dst, ACT.Exp, scale=-1.0).then_inc(sems[pre + "_exp"], 1)

                def chain(name, u):
                    par = u[1]
                    if name in ("n_center", "k_center", "g_center", "f_center"):
                        squared(T2 if name[0] == "n" else S2, name[0], u)
                    elif name in ("n_var", "k_var", "g_var", "f_var"):
                        rstd(T2 if name[0] == "n" else S2, name[0], u)
                    elif name == "xz":
                        done(sc, "xz_mm", u)
                        done(sc, "conv_step", shift(u, -2), 2 * TAPS - 1)
                        done(sc, "z_out", shift(u, -2))
                        sc.activation(xpad[:, par, :, PADW:PADW + S], images(ps[:, 6, 0:S2]), ACT.Identity, bias=bxz[:, 0:1])
                        sc.activation(zz[:, par], ps[:, 7, 0:S2], ACT.Identity, bias=bxz[:, 1:2]).then_inc(sems["xz_out"], 1)
                    elif name == "z1":
                        done(sc, "xz_out", u)
                        exp_neg_abs(lz, zz[:, par], "z", u)
                    elif name == "z2":
                        done(sc, "z_exp", u)
                        sc.activation(lz, lz, ACT.Ln, bias=one_col[:, :]).then_inc(sems["z_ln"], 1)
                    elif name == "z3":
                        done(sc, "z_arg", u)
                        sc.activation(lz, lz, ACT.Exp).then_inc(sems["z_sig"], 1)
                    elif name == "su1":
                        done(sc, "conv_step", u, 2 * TAPS - 1)
                        exp_neg_abs(ex, flat(cv), "su", u)
                    elif name == "dt":
                        done(sc, "su_out", u)
                        for k in range(2):
                            done(sc, "dt_mm", u, k)
                            sc.activation(cv[:, k], ps[:, 5 + 2 * k, 0:S2], ACT.Identity, bias=mvec[:, DTB:DTB + 1]).then_inc(sems["dt_out"], 1)
                    elif name == "sd1":
                        done(sc, "dt_out", u, 1)
                        exp_neg_abs(ex, flat(cv), "sd", u)
                    elif name in ("su2", "sd2"):
                        pre = name[:2]
                        done(sc, pre + "_one", u)
                        sc.activation(lg, op, ACT.Ln).then_inc(sems[pre + "_ln"], 1)
                    elif name == "dbc":
                        done(sc, "b_res", shift(u, -1))
                        for k in range(2):
                            done(sc, "dbc_mm", u, k)
                            sc.activation(dbc[:, k], ps[:, 5 + 2 * k, 0:S2], ACT.Copy).then_inc(sems["dbc_out"], 1)
                    elif name == "f_1":
                        done(sc, "f_mm1", u)
                        sc.activation(gl, ps[:, 6, 0:S2], ACT.Gelu, bias=mvec[:, B1:B1 + 1]).then_inc(sems["f_gelu"], 1)
                        exp_ln_tables()
                    elif name == "f_T":
                        done(sc, "f_T", u)
                        pu = shift(u, -1)
                        sc.wait_ge(s_stored[pu[1]], VC(pu, 2))
                        pv = ps[:, 5, :].rearrange("p (b t d) -> p b t d", b=2, t=2)
                        rv = rows.rearrange("p (b t) d -> p b t d", b=2)
                        sc.activation(rv[:, :, 0], pv[:, :, 0], ACT.Copy)
                        sc.activation(rv[0:S - P, :, 1], pv[0:S - P, :, 1], ACT.Copy).then_inc(sems["f_rows"], 1)

                def rep_b(u, n):
                    done(sc, "m_b", u, n)
                    done(sc, "m_inp", u, n - 2)
                    sc.activation(brep[:, n % 2], ps[:, 0:2, 0:S2], ACT.Copy).then_inc(sems["m_brep"], 1)

                def decays(u, n):
                    par = u[1]
                    if n == 0:
                        done(sc, "sd_out", u)
                    done(sc, "m_scan", u, n - 2)
                    o = decay[:, n % 2].rearrange("p k (b s) -> p (k b) s", b=2)[:, :, 1:S]
                    i = delta[:, par].rearrange("p k (b s) -> p (k b) s", b=2)[:, :, 1:S]
                    sc.activation(o, i, ACT.Exp, scale=amat[:, n:n + 1]).then_inc(sems["m_decay"], 1)

                def run(u, steps):
                    for name, d, n in steps:
                        v = shift(u, d)
                        if name == "ahead":
                            rep_b(v, n)
                            decays(v, n)
                        else:
                            chain(name, v)

                fusion(sc, run, exp_ln_tables)

            @block.vector
            def _(dve):
                credit(dve, "n_scaled n_normed n_txt_out k_normed k_res g_normed conv_step su_err su_out sd_err sd_out "
                            "z_arg z_out f_gated f_added f_normed f_out m_scan m_prod m_pair")
                dve.wait_ge(s_w3, 16 * 18)
                dve.tensor_scalar(wp_f, wp_raw, mvec[:, LG:LG + 1], None, ALU.mult).then_inc(s_ev3, 1)
                dve.wait_ge(s_set, 7)
                dve.tensor_scalar(diagD, ident[:, :], mvec[:, DV:DV + 1], None, ALU.mult).then_inc(s_ev3, 1)
                dve.wait_ge(s_mm3, 1)
                dve.tensor_copy(bxz, ps[:, 6, 0:2]).then_inc(s_ev3, 1)
                dve.memset(lz, 0.0).then_inc(s_ev3, 1)

                def conv(u, k):
                    x_ = xpad[:, u[1]]
                    for j, (v, off) in enumerate(((images(cv[:, 0, :]), k),
                                                  (images(cv[:, 1, :])[:, ::-1, ::-1], 2 * PADW - k))):
                        src = x_[:, :, off:off + S]
                        if k == 0:
                            dve.tensor_scalar(v, src, taps[:, 0:1], mvec[:, CB:CB + 1], ALU.mult, ALU.add).then_inc(sems["conv_step"], 1)
                        else:
                            done(dve, "conv_step", u, 2 * k + j - 2)
                            dve.scalar_tensor_tensor(v, src, taps[:, k:k + 1], v, ALU.mult, ALU.add).then_inc(sems["conv_step"], 1)

                def chain(name, u):
                    par = u[1]
                    if name == "n_norm":
                        done(dve, "n_rstd", u)
                        done(dve, "k_res", shift(u, -1))
                        o = images(hc)[:, :, 0:NT]
                        dve.scalar_tensor_tensor(o, images(ps[:, 6, 0:T2], NT), mvec[:, NW:NW + 1], images(rs3[:, 0:T2], NT),
                                                 ALU.mult, ALU.mult).then_inc(sems["n_scaled"], 1)
                        done(dve, "n_scaled", u)
                        dve.tensor_scalar(o, o, mvec[:, NB:NB + 1], None, ALU.add).then_inc(sems["n_normed"], 1)
                    elif name == "txt":
                        done(dve, "n_txt", u)
                        dve.tensor_copy(images(hc)[:, :, NT:S], images(ps[:, 7, 0:2 * TXT], TXT)).then_inc(sems["n_txt_out"], 1)
                    elif name == "k_norm":
                        done(dve, "k_rstd", u)
                        dve.tensor_tensor(skip, ps[:, 6, 0:S2], rs3, ALU.mult).then_inc(sems["k_normed"], 1)
                        done(dve, "k_normed", u)
                        dve.tensor_tensor(images(hu(u), NT), images(hc)[:, :, 0:NT], images(skip)[:, :, 0:NT], ALU.add)
                        dve.tensor_tensor(tu(u), images(hc)[:, :, NT:S], images(skip)[:, :, NT:S], ALU.add).then_inc(sems["k_res"], 1)
                    elif name in ("g_norm", "f_norm"):
                        done(dve, name[0] + "_rstd", u)
                        dve.tensor_tensor(yn, ps[:, 6, 0:S2], rs3, ALU.mult).then_inc(sems[name[0] + "_normed"], 1)
                    elif name[:4] == "conv":
                        done(dve, "xz_out", u)
                        conv(u, int(name[4]))
                    elif name == "z_arg":
                        done(dve, "z_ln", u)
                        dve.scalar_tensor_tensor(lz, zz[:, par], 0.0, lz, ALU.min, ALU.subtract).then_inc(sems["z_arg"], 1)
                    elif name in ("su_err", "sd_err"):
                        pre = name[:2]
                        done(dve, pre + "_one", u)
                        done(dve, pre + "_ln", u)
                        dve.scalar_tensor_tensor(op, op, -1.0, ex, ALU.add, ALU.subtract).then_inc(sems[pre + "_err"], 1)
                    elif name in ("su3", "sd3"):
                        pre = name[:2]
                        done(dve, pre + "_cor", u)
                        if pre == "su":
                            done(dve, "m_sum", shift(u, -2), 0)
                            dst = uu[:, par]
                        else:
                            done(dve, "m_decay", shift(u, -2), NS - 1)
                            dst = delta[:, par]
                        dve.scalar_tensor_tensor(flat(dst), flat(cv), 0.0, lg, ALU.max, ALU.add).then_inc(sems[pre + "_out"], 1)
                    elif name == "gate":
                        done(dve, "z_out", u)
                        done(dve, "m_sum", u, NS // 2 - 1)
                        dve.tensor_tensor(h1, ps[:, 4, 0:S2], zg[:, par], ALU.mult).then_inc(sems["f_gated"], 1)
                        done(dve, "f_gated", u)
                        h3_ = images(h1)
                        dve.tensor_tensor(h3_[:, :, 0:NT], h3_[:, :, 0:NT], images(hu(u), NT), ALU.add)
                        dve.tensor_tensor(h3_[:, :, NT:S], h3_[:, :, NT:S], tu(u), ALU.add).then_inc(sems["f_added"], 1)
                    elif name == "f_add":
                        done(dve, "f_mm2", u)
                        dve.scalar_tensor_tensor(h1, ps[:, 5, 0:S2], mvec[:, B2:B2 + 1], h1, ALU.add, ALU.add).then_inc(sems["f_out"], 1)

                def scan(u, n):
                    done(dve, "m_prod", u, n - 2)
                    done(dve, "m_inp", u, n)
                    done(dve, "m_decay", u, n)
                    dve.tensor_tensor_scan(flat(state[:, n % 2]), flat(decay[:, n % 2]), flat(inp[:, n % 2]), 0.0,
                                           ALU.mult, ALU.add).then_inc(sems["m_scan"], 1)

                def product(u, n):
                    done(dve, "m_scan", u, n)
                    if n % 2 == 0:
                        done(dve, "m_pair", u, n // 2 - 1)
                    done(dve, "m_c", u, n)
                    dve.tensor_tensor(prod[:, n % 2], state[:, n % 2], ps[:, 2:4, 0:S2], ALU.mult).then_inc(sems["m_prod"], 1)
                    if n % 2 == 1:
                        m = n // 2
                        done(dve, "m_prod", u, n)
                        done(dve, "m_sum", u, m - 2)
                        dve.tensor_tensor(pair[:, m % 2], prod[:, 0], prod[:, 1], ALU.add).then_inc(sems["m_pair"], 1)

                def run(u, steps):
                    for name, d, n in steps:
                        v = shift(u, d)
                        if name == "step":
                            scan(v, n)
                        elif name == "product":
                            product(v, n)
                        else:
                            chain(name, v)

                fusion(dve, run)


_INS = ["x", "txt", "L0_tok_conv_w", "L0_tok_conv_b", "L0_tok_cls_token", "L0_tok_pos_embed", "L0_tok_ln1_w",
        "L0_tok_ln1_b", "L0_tok_qkv_w", "L0_tok_qkv_b", "L0_tok_proj_w", "L0_tok_proj_b", "L0_tok_ln2_w",
        "L0_tok_ln2_b", "L0_tok_fc1_w", "L0_tok_fc1_b", "L0_tok_fc2_w", "L0_tok_fc2_b", "L0_tok_norm_w",
        "L0_tok_norm_b", "L0_attn_ln_g", "L0_attn_ln_b", "L0_attn_W_proj", "L0_attn_conv_w", "L0_attn_conv_b",
        "L0_attn_W_x", "L0_attn_W_dt", "L0_attn_b_dt", "L0_attn_A_log", "L0_attn_D", "L0_ffn_W1", "L0_ffn_b1",
        "L0_ffn_W2", "L0_ffn_b2"]


def kernel(**inputs):
    import numpy as _np
    import concourse.bacc as _bacc
    from concourse.bass_utils import run_bass_kernel_spmd as _run

    nc = _bacc.Bacc("TRN2", target_bir_lowering=False, num_devices=1)
    arrays, args = {}, []
    for name in _INS:
        a = _np.ascontiguousarray(inputs[name])
        arrays[f"in_{name}"] = a
        args.append(nc.dram_tensor(f"in_{name}", a.shape, mybir.dt.from_np(a.dtype), kind="ExternalInput").ap())
    b, tokens, dim = inputs["x"].shape[0], inputs["L0_tok_pos_embed"].shape[1], inputs["L0_tok_conv_w"].shape[1]
    out = nc.dram_tensor("out_0", (b, tokens + inputs["txt"].shape[1], dim), F32, kind="ExternalOutput").ap()
    early_fusion(nc, *args, out)
    r = _run(nc, [arrays], core_ids=[0])
    return r.results[0]["out_0"]
```
